# Optimizing a Trainium2 kernel written in Bass

```python
import numpy as np
import jax
import jax.numpy as jnp

def _softmax(x, axis=-1):
    return jax.nn.softmax(x, axis=axis)

def _gelu(x):
    return jax.nn.gelu(x, approximate=True)

def _silu(x):
    return jax.nn.silu(x)

def _sigmoid(x):
    return jax.nn.sigmoid(x)

def _layernorm(x, axis=-1, eps=1e-05):
    m = jnp.mean(x, axis=axis, keepdims=True)
    v = jnp.var(x, axis=axis, keepdims=True)
    return (x - m) / jnp.sqrt(v + eps)

def _scatter_add(tgt, idx, src, axis=0):
    return tgt.at[idx].add(src)

def _segment_sum(src, seg, n):
    return jax.ops.segment_sum(src, seg, n)
kernel_name = 'mk_prb_d2_jaxref_r8_db1401'

def setup_inputs(seed: int=0):
    np.random.seed(seed)
    _w = jnp.asarray

    def _L0_attn_setup():
        import jax, jax.numpy as jnp
        import numpy as np
        D_MODEL = 256
        D_STATE = 64
        D_CONV = 4
        HEADDIM = 64
        NHEADS = D_MODEL // HEADDIM
        D_IN_PROJ = 2 * D_MODEL + 2 * D_STATE + NHEADS
        CONV_DIM = D_MODEL + 2 * D_STATE
        B = 2
        L = 128

        def _mamba_fwd(u, W_in, conv_w, conv_b, W_out, A_log, D_param, dt_bias):
            Bb, Ll, _ = u.shape
            proj = u @ W_in.T
            z, x, B_toks, C_toks, dt_toks = jnp.split(proj, [D_MODEL, 2 * D_MODEL, 2 * D_MODEL + D_STATE, 2 * D_MODEL + 2 * D_STATE], axis=-1)
            xBC = jnp.concatenate([x, B_toks, C_toks], axis=-1).transpose(0, 2, 1)
            xBC = jax.lax.conv_general_dilated(xBC, conv_w, window_strides=(1,), padding=[(D_CONV - 1, 0)], feature_group_count=CONV_DIM) + conv_b[None, :, None]
            xBC = jax.nn.silu(xBC.transpose(0, 2, 1))
            x, B_toks, C_toks = jnp.split(xBC, [D_MODEL, D_MODEL + D_STATE], axis=-1)
            A = -jnp.exp(A_log)
            dt = jax.nn.softplus(dt_toks + dt_bias)
            dA = jnp.exp(dt * A)
            xh = x.reshape(Bb, Ll, NHEADS, HEADDIM)

            def step(S, inp):
                dA_t, dt_t, B_t, C_t, x_t = inp
                S = S * dA_t[:, :, None, None] + jnp.einsum('bh,bn,bhp->bhpn', dt_t, B_t, x_t)
                y_t = jnp.einsum('bhpn,bn->bhp', S, C_t)
                return (S, y_t)
            S0 = jnp.zeros((Bb, NHEADS, HEADDIM, D_STATE), u.dtype)
            xs = (dA.transpose(1, 0, 2), dt.transpose(1, 0, 2), B_toks.transpose(1, 0, 2), C_toks.transpose(1, 0, 2), xh.transpose(1, 0, 2, 3))
            _, ys = jax.lax.scan(step, S0, xs)
            y = ys.transpose(1, 0, 2, 3) + D_param[None, None, :, None] * xh
            y = y * jax.nn.silu(z.reshape(Bb, Ll, NHEADS, HEADDIM))
            return y.reshape(Bb, Ll, D_MODEL) @ W_out.T
        key = jax.random.key(seed)
        ks = jax.random.split(key, 8)
        u = jax.random.normal(ks[0], (B, L, D_MODEL), jnp.float32)
        W_in = jax.random.normal(ks[1], (D_IN_PROJ, D_MODEL), jnp.float32) * 0.02
        conv_w = jax.random.normal(ks[2], (CONV_DIM, 1, D_CONV), jnp.float32) * 0.2
        conv_b = jnp.zeros((CONV_DIM,), jnp.float32)
        W_out = jax.random.normal(ks[3], (D_MODEL, D_MODEL), jnp.float32) * 0.02
        A_log = jnp.log(jax.random.uniform(ks[4], (NHEADS,), jnp.float32, 1.0, 16.0))
        D_param = jnp.ones((NHEADS,), jnp.float32)
        dt = jnp.exp(jax.random.uniform(ks[5], (NHEADS,), jnp.float32) * (np.float32(np.log(0.1)) - np.float32(np.log(0.001))) + np.float32(np.log(0.001)))
        dt = jnp.clip(dt, 0.0001)
        dt_bias = dt + jnp.log(-jnp.expm1(-dt))
        return dict(u=u, W_in=W_in, conv_w=conv_w, conv_b=conv_b, W_out=W_out, A_log=A_log, D_param=D_param, dt_bias=dt_bias)
    _L0_attn_in = _L0_attn_setup()

    def _L0_ffn_setup():
        import jax, jax.numpy as jnp
        import numpy as np
        from jax import lax
        E = 8
        K = 2
        H = 256
        I = 512
        B, S = (2, 256)
        SCALE = 0.02

        def _silu_and_mul(gu):
            g, u = jnp.split(gu, 2, axis=-1)
            return jax.nn.silu(g) * u
        key = jax.random.key(seed)
        ks = jax.random.split(key, 6)
        return {'hidden_states': jax.random.normal(ks[0], (B, S, H), dtype=jnp.float32), 'gate_w': jax.random.normal(ks[1], (H, E), dtype=jnp.float32) * SCALE, 'w_gate_up': jax.random.normal(ks[2], (E, H, 2 * I), dtype=jnp.float32) * SCALE, 'w_down': jax.random.normal(ks[3], (E, I, H), dtype=jnp.float32) * SCALE, 'shared_gate_up': jax.random.normal(ks[4], (H, 2 * I), dtype=jnp.float32) * SCALE, 'shared_down': jax.random.normal(ks[5], (I, H), dtype=jnp.float32) * SCALE}
    _L0_ffn_in = _L0_ffn_setup()

    def _L1_attn_setup():
        import jax, jax.numpy as jnp
        import numpy as np
        B, T, D, H = (2, 256, 256, 16)
        DH = D // H
        key = jax.random.key(seed)
        k1, k2, k3 = jax.random.split(key, 3)
        x = jax.random.normal(k1, (B, T, D), dtype=jnp.float32)
        w_qkv = jax.random.normal(k2, (D, 3 * D), dtype=jnp.float32) * (1.0 / np.sqrt(D))
        w_o = jax.random.normal(k3, (D, D), dtype=jnp.float32) * (1.0 / np.sqrt(D))
        return {'x': x, 'w_qkv': w_qkv, 'w_o': w_o}
    _L1_attn_in = _L1_attn_setup()

    def _L1_ffn_setup():
        import jax, jax.numpy as jnp
        import numpy as np
        B, S, H = (1, 256, 256)
        E, K, I = (8, 2, 128)
        IS = 2 * I
        key = jax.random.key(seed)
        ks = jax.random.split(key, 8)
        w = 0.02
        return {'x': jax.random.normal(ks[0], (B, S, H), jnp.float32), 'gate_w': jax.random.normal(ks[1], (E, H), jnp.float32) * w, 'wg': jax.random.normal(ks[2], (E, H, I), jnp.float32) * w, 'wu': jax.random.normal(ks[3], (E, H, I), jnp.float32) * w, 'wd': jax.random.normal(ks[4], (E, I, H), jnp.float32) * w, 'sg': jax.random.normal(ks[5], (H, IS), jnp.float32) * w, 'su': jax.random.normal(ks[6], (H, IS), jnp.float32) * w, 'sd': jax.random.normal(ks[7], (IS, H), jnp.float32) * w}
    _L1_ffn_in = _L1_ffn_setup()
    _d = {'L0_attn_u': _L0_attn_in['u'], 'L0_attn_W_in': _L0_attn_in['W_in'], 'L0_attn_conv_w': _L0_attn_in['conv_w'], 'L0_attn_conv_b': _L0_attn_in['conv_b'], 'L0_attn_W_out': _L0_attn_in['W_out'], 'L0_attn_A_log': _L0_attn_in['A_log'], 'L0_attn_D_param': _L0_attn_in['D_param'], 'L0_attn_dt_bias': _L0_attn_in['dt_bias'], 'L0_ffn_gate_w': _L0_ffn_in['gate_w'], 'L0_ffn_w_gate_up': _L0_ffn_in['w_gate_up'], 'L0_ffn_w_down': _L0_ffn_in['w_down'], 'L0_ffn_shared_gate_up': _L0_ffn_in['shared_gate_up'], 'L0_ffn_shared_down': _L0_ffn_in['shared_down'], 'L1_attn_w_qkv': _L1_attn_in['w_qkv'], 'L1_attn_w_o': _L1_attn_in['w_o'], 'L1_ffn_gate_w': _L1_ffn_in['gate_w'], 'L1_ffn_wg': _L1_ffn_in['wg'], 'L1_ffn_wu': _L1_ffn_in['wu'], 'L1_ffn_wd': _L1_ffn_in['wd'], 'L1_ffn_sg': _L1_ffn_in['sg'], 'L1_ffn_su': _L1_ffn_in['su'], 'L1_ffn_sd': _L1_ffn_in['sd']}
    _x0 = _d['L0_attn_u']
    _d['L0_attn_u'] = jax.random.normal(jax.random.fold_in(jax.random.key(seed), 1), (16, 256, 256), dtype=_x0.dtype)
    del _x0
    return _d

def reference(L0_attn_u, L0_attn_W_in, L0_attn_conv_w, L0_attn_conv_b, L0_attn_W_out, L0_attn_A_log, L0_attn_D_param, L0_attn_dt_bias, L0_ffn_gate_w, L0_ffn_w_gate_up, L0_ffn_w_down, L0_ffn_shared_gate_up, L0_ffn_shared_down, L1_attn_w_qkv, L1_attn_w_o, L1_ffn_gate_w, L1_ffn_wg, L1_ffn_wu, L1_ffn_wd, L1_ffn_sg, L1_ffn_su, L1_ffn_sd):

    def _L0_attn_ref(u, W_in, conv_w, conv_b, W_out, A_log, D_param, dt_bias):
        import jax, jax.numpy as jnp
        import numpy as np
        D_MODEL = 256
        D_STATE = 64
        D_CONV = 4
        HEADDIM = 64
        NHEADS = D_MODEL // HEADDIM
        D_IN_PROJ = 2 * D_MODEL + 2 * D_STATE + NHEADS
        CONV_DIM = D_MODEL + 2 * D_STATE
        B = 2
        L = 128

        def _mamba_fwd(u, W_in, conv_w, conv_b, W_out, A_log, D_param, dt_bias):
            Bb, Ll, _ = u.shape
            proj = u @ W_in.T
            z, x, B_toks, C_toks, dt_toks = jnp.split(proj, [D_MODEL, 2 * D_MODEL, 2 * D_MODEL + D_STATE, 2 * D_MODEL + 2 * D_STATE], axis=-1)
            xBC = jnp.concatenate([x, B_toks, C_toks], axis=-1).transpose(0, 2, 1)
            xBC = jax.lax.conv_general_dilated(xBC, conv_w, window_strides=(1,), padding=[(D_CONV - 1, 0)], feature_group_count=CONV_DIM) + conv_b[None, :, None]
            xBC = jax.nn.silu(xBC.transpose(0, 2, 1))
            x, B_toks, C_toks = jnp.split(xBC, [D_MODEL, D_MODEL + D_STATE], axis=-1)
            A = -jnp.exp(A_log)
            dt = jax.nn.softplus(dt_toks + dt_bias)
            dA = jnp.exp(dt * A)
            xh = x.reshape(Bb, Ll, NHEADS, HEADDIM)

            def step(S, inp):
                dA_t, dt_t, B_t, C_t, x_t = inp
                S = S * dA_t[:, :, None, None] + jnp.einsum('bh,bn,bhp->bhpn', dt_t, B_t, x_t)
                y_t = jnp.einsum('bhpn,bn->bhp', S, C_t)
                return (S, y_t)
            S0 = jnp.zeros((Bb, NHEADS, HEADDIM, D_STATE), u.dtype)
            xs = (dA.transpose(1, 0, 2), dt.transpose(1, 0, 2), B_toks.transpose(1, 0, 2), C_toks.transpose(1, 0, 2), xh.transpose(1, 0, 2, 3))
            _, ys = jax.lax.scan(step, S0, xs)
            y = ys.transpose(1, 0, 2, 3) + D_param[None, None, :, None] * xh
            y = y * jax.nn.silu(z.reshape(Bb, Ll, NHEADS, HEADDIM))
            return y.reshape(Bb, Ll, D_MODEL) @ W_out.T
        return _mamba_fwd(u, W_in, conv_w, conv_b, W_out, A_log, D_param, dt_bias)

    def _L0_ffn_ref(hidden_states, gate_w, w_gate_up, w_down, shared_gate_up, shared_down):
        import jax, jax.numpy as jnp
        import numpy as np
        from jax import lax
        E = 8
        K = 2
        H = 256
        I = 512
        B, S = (2, 256)
        SCALE = 0.02

        def _silu_and_mul(gu):
            g, u = jnp.split(gu, 2, axis=-1)
            return jax.nn.silu(g) * u
        orig_shape = hidden_states.shape
        x = hidden_states.reshape(-1, orig_shape[-1])
        shared_out = _silu_and_mul(x @ shared_gate_up) @ shared_down
        router_logits = x @ gate_w
        probs = jax.nn.softmax(router_logits, axis=-1)
        topk_w, topk_i = lax.top_k(probs, K)
        topk_w = topk_w / jnp.sum(topk_w, axis=-1, keepdims=True)
        combine = jnp.sum(jax.nn.one_hot(topk_i, E, dtype=x.dtype) * topk_w[..., None], axis=1)

        def body(acc, we):
            wg, wd, cw = we
            h = _silu_and_mul(x @ wg) @ wd
            return (acc + cw[:, None] * h, None)
        moe_out, _ = lax.scan(body, jnp.zeros_like(x), (w_gate_up, w_down, combine.T))
        return (moe_out + shared_out).reshape(orig_shape)

    def _L1_attn_ref(x, w_qkv, w_o):
        import jax, jax.numpy as jnp
        import numpy as np
        B, T, D, H = (2, 256, 256, 16)
        DH = D // H
        b, t, d = x.shape
        qkv = (x @ w_qkv).reshape(b, t, 3, H, DH)
        q, k, v = (qkv[:, :, 0], qkv[:, :, 1], qkv[:, :, 2])
        scale = 1.0 / np.sqrt(DH).astype(np.float32)
        scores = jnp.einsum('bqhd,bkhd->bhqk', q, k) * scale
        causal = jnp.tril(jnp.ones((t, t), dtype=bool))
        scores = jnp.where(causal[None, None], scores, -jnp.inf)
        attn = jax.nn.softmax(scores, axis=-1)
        out = jnp.einsum('bhqk,bkhd->bqhd', attn, v).reshape(b, t, d)
        return out @ w_o

    def _L1_ffn_ref(x, gate_w, wg, wu, wd, sg, su, sd):
        import jax, jax.numpy as jnp
        import numpy as np
        B, S, H = (1, 256, 256)
        E, K, I = (8, 2, 128)
        IS = 2 * I
        b, s, h = x.shape
        xf = x.reshape(-1, h)
        T = xf.shape[0]
        scores = jax.nn.softmax(jnp.einsum('th,eh->te', xf, gate_w), axis=-1)
        topk_w, topk_i = jax.lax.top_k(scores, K)
        topk_w = topk_w / jnp.sum(topk_w, axis=-1, keepdims=True)
        cw = jnp.zeros_like(scores).at[jnp.arange(T)[:, None], topk_i].add(topk_w)
        g = jnp.einsum('th,ehi->eti', xf, wg)
        u = jnp.einsum('th,ehi->eti', xf, wu)
        hgated = jax.nn.silu(g) * u
        eo = jnp.einsum('eti,eih->eth', hgated, wd)
        y = jnp.einsum('te,eth->th', cw, eo)
        shared = jax.nn.silu(xf @ sg) * (xf @ su) @ sd
        return (y + shared).reshape(b, s, h)
    x = L0_attn_u
    xn = _layernorm(x, axis=-1)
    x = x + _L0_attn_ref(xn, L0_attn_W_in, L0_attn_conv_w, L0_attn_conv_b, L0_attn_W_out, L0_attn_A_log, L0_attn_D_param, L0_attn_dt_bias) + _L0_ffn_ref(xn, L0_ffn_gate_w, L0_ffn_w_gate_up, L0_ffn_w_down, L0_ffn_shared_gate_up, L0_ffn_shared_down)
    xn = _layernorm(x, axis=-1)
    x = x + _L1_attn_ref(xn, L1_attn_w_qkv, L1_attn_w_o) + _L1_ffn_ref(xn, L1_ffn_gate_w, L1_ffn_wg, L1_ffn_wu, L1_ffn_wd, L1_ffn_sg, L1_ffn_su, L1_ffn_sd)
    return x

_drawn_inputs = setup_inputs


def setup_inputs(seed=0):
    import zlib

    import numpy as np

    out = dict(_drawn_inputs(seed))
    spreads = {'L0_attn_conv_b': (0.0, 0.1), 'L0_attn_D_param': (1.0, 0.2)}
    factors = {}
    for name, (base, spread) in spreads.items():
        noise = np.random.default_rng([zlib.crc32(name.encode()), seed]).standard_normal(out[name].shape)
        drawn = base * np.exp(spread * noise) if base else spread * noise
        out[name] = jnp.asarray(drawn.astype(out[name].dtype))
    for name, factor in factors.items():
        out[name] = (out[name] * factor).astype(out[name].dtype)
    return out
```

```python
from contextlib import ExitStack

import concourse.bass as bass
from concourse import mybir

F32, BF16, I32 = mybir.dt.float32, mybir.dt.bfloat16, mybir.dt.int32
ALU, ACT, AX = mybir.AluOpType, mybir.ActivationFunctionType, mybir.AxisListType

P = 128
NSEQ, SEQ, D = 16, 256, 256
NTOK = NSEQ * SEQ
NT = NTOK // P
CH = SEQ // P
KD = D // P
E, TOPK = 8, 2
NJ = (NTOK * TOPK + E * (P - 1)) // P
NJ += NJ % 2
MH, MP, MS, TAPS = 4, 64, 64, 4
I0, I1S, I1 = 512, 256, 128
AH, DH = 16, 16
BIG = 1.0e30
EPS = 1e-5
HALF = NSEQ // 2


class Round:

    def __init__(self, i, u):
        self.i, self.u, self.n = i, u, i * 2 + u

    def back(self, k=1):
        u = self.u - k
        return Round(self.i + (u // 2), u % 2)


class Event:

    def __init__(self, sem, credit=0, step=1, base=0):
        self.sem, self.credit, self.step, self.base = sem, credit, step, base

    def open(self, eng):
        if self.credit:
            eng.sem_inc(self.sem, self.credit * self.step)

    def mark(self, ins):
        ins.then_inc(self.sem, self.step)

    def wait(self, eng, n, back=0):
        eng.wait_ge(self.sem, (n + (1 - back + self.credit + self.base)) * self.step)


class Chain:

    def __init__(self, sem, per, before=0):
        self.sem, self.per, self.k, self.before = sem, per, 0, before

    def start(self, eng, n):
        self.eng, self.base, self.k = eng, (n + self.before) * self.per, 0

    def __call__(self, ins):
        self.k += 1
        ins.then_inc(self.sem, 1)
        self.eng.wait_ge(self.sem, self.base + self.k)

    def end(self):
        assert self.k == self.per, (self.k, self.per)


def rounds(eng, count, body):
    with eng.Fori(0, count // 2) as i:
        for u in range(2):
            body(Round(i, u))


def build(nc, a, out):
    ctx = ExitStack()
    with ctx:
        program(nc, ctx, a, out)


def program(nc, ctx, a, out):
    def sb(name, shape, dt=F32):
        return ctx.enter_context(nc.sbuf_tensor(name, shape, dt))

    def sem(name):
        return ctx.enter_context(nc.semaphore(name))

    named, engines = {}, {}

    def ev(name, credit=0, step=1, by=None, base=0):
        first = name not in named
        if first:
            named[name] = sem(name)
        e = Event(named[name], credit, step, base)
        if first and by:
            engines.setdefault(by, []).append(e)
        return e

    bank = [ctx.enter_context(nc.psum_tensor(f"bank{i}", [P, 512], F32)) for i in range(8)]

    xn_rows = [nc.dram_tensor(f"xn_rows{l}", (NTOK, D), F32, kind="Internal").ap() for l in range(2)]
    y_rows = [nc.dram_tensor(f"y_rows{l}", (NJ * P, D), F32, kind="Internal").ap() for l in range(2)]
    lists = [nc.dram_tensor(f"slot_token{l}", (P * NJ, 1), I32, kind="Internal").ap() for l in range(2)]

    ident = sb("ident", [P, P])
    tri_le = sb("tri_le", [P, P])
    tri_gt = sb("tri_gt", [P, P])
    ones = sb("ones", [P, MS])
    quarter_le = sb("quarter_le", [P, P])
    ones_b = sb("ones_b", [P, P], BF16)
    before_b = sb("before_b", [P, P], BF16)
    ident_b = sb("ident_b", [P, P], BF16)
    future_b = sb("future_b", [P, P], BF16)
    iota_e = sb("iota_e", [P, E])
    iota_j = sb("iota_j", [P, NJ])
    token_id = sb("token_id", [P, NT], I32)
    head_mask = sb("head_mask", [P, 2])
    minus_half = sb("minus_half", [P, CH])
    zero_i = sb("zero_i", [P, NJ], I32)
    itmp_e = sb("itmp_e", [P, E], I32)

    par_i = sb("par_i", [P, 2], I32)

    X = sb("X", [P, NT, D])
    XT = sb("XT", [P, KD, NTOK])
    WGU = sb("WGU", [P, E * KD * 2 * I0])
    ARENA = sb("ARENA", [P, E * I0 // P * D])
    w_in = sb("w_in", [P, KD, 2 * D + 2 * MS])
    w_r0 = sb("w_r0", [P, KD, E + MH])
    w_out = sb("w_out", [P, KD, D])
    sh_gu = sb("sh_gu", [P, KD, 2 * I0])
    sh_dn = sb("sh_dn", [P, I0 // P, D])

    class Area:

        def __init__(self, t):
            self.t, self.at = t, 0

        def take(self, *shape):
            n = 1
            for s in shape:
                n *= s
            v = self.t[:, self.at:self.at + n]
            self.at += n
            assert self.at <= self.t.shape[1]
            names = "abcde"[:len(shape)]
            if len(shape) > 1:
                v = v.rearrange(f"p ({' '.join(names)}) -> p {' '.join(names)}",
                                **{c: s for c, s in zip(names, shape)})
            return v

    wgu0 = WGU[:, :].rearrange("p (e k n) -> p e k n", e=E, k=KD)
    wdn0 = ARENA[:, :].rearrange("p (e c n) -> p e c n", e=E, c=I0 // P)

    XN = [sb(f"XN{u}", [P, CH, D]) for u in range(2)]
    xT = [sb(f"xT{u}", [P, KD, SEQ]) for u in range(2)]
    stats = sb("stats", [P, CH, 6])
    mv = sb("mv", [P, CH, 2])
    rstd = sb("rstd", [P, CH])
    LG = sb("LG", [P, NT, E])
    DTR = sb("DTR", [P, NT, MH])
    DTA = sb("DTA", [P, NT, MH])
    DTE = sb("DTE", [P, NT, MH])
    dt_bias = sb("dt_bias", [P, MH])
    a_neg = sb("a_neg", [P, MH])
    conv_w = sb("conv_w", [P, 3, TAPS])
    conv_b = sb("conv_b", [P, 3])
    d_par = sb("d_par", [P, KD])
    hot_b = sb("hot_b", [P, NT, E], BF16)
    rs = sb("route_small", [P, 8, NT])
    ex = sb("route_experts", [P, 8, E])
    ex_i = sb("route_experts_i", [P, E], I32)
    tile_e = sb("tile_e", [P, NJ])
    tile_expert = sb("tile_expert", [P, NJ], I32)
    slot_i = [sb(f"slot{k}", [P, NT], I32) for k in range(TOPK)]
    dest_i = [sb(f"dest{k}", [P, NT], I32) for k in range(TOPK)]
    dtmp_i = sb("dtmp_i", [P, NT], I32)
    cw = [sb(f"cw{k}", [P, NT]) for k in range(TOPK)]
    ring_idx = sb("ring_idx", [P, 8], I32)
    ring_tok = sb("ring_tok", [P, 8], I32)
    slot_tok = sb("slot_tok", [P, NJ], I32)
    itmp_j = slot_tok

    rr = Area(ARENA)
    rr.at = 1024
    OH = [rr.take(NT, E) for k in range(TOPK)]
    rt = [rr.take(NT, E) for n in range(3)]
    tile_cmp = rr.take(NJ, E)

    ar = Area(ARENA)
    MHm = ar.take(CH, MH, P)
    ED = ar.take(CH, MH, P)
    CV = ar.take(3, SEQ)
    TH = ar.take(3, SEQ)
    XS = ar.take(KD, SEQ)
    ZT = ar.take(KD, SEQ)
    SZ = ar.take(KD, SEQ)
    XD = ar.take(CH, MH, MP)
    XW = ar.take(MH, MP)
    YG = ar.take(KD, SEQ)
    GM = ar.take(CH, P)
    BS = ar.take(MS)
    BT = ar.take(SEQ)
    CT = ar.take(SEQ)
    SS = ar.take(MH * MP)
    CE = ar.take(MH, P)[0:MS]

    wa = Area(WGU)
    wgu1 = wa.take(E, KD, 2 * I1)
    wdn1 = wa.take(E, D)
    sh_gu1 = wa.take(KD, 2 * I1S)
    sh_dn1 = wa.take(I1S // P, D)
    w_qkv = wa.take(KD, 3 * D)
    w_o = wa.take(KD, D)
    w_r1 = wa.take(KD, E)
    aa = Area(ARENA)
    QT = aa.take(KD, SEQ)
    KM = [aa.take(KD, SEQ) for _ in range(2)]
    V = aa.take(CH, D)
    PR = [aa.take(2, 3, P) for _ in range(2)]
    PT = [aa.take(2, 3, P) for _ in range(2)]
    SM = aa.take(CH, AH)
    SR = aa.take(CH, AH)
    MX = [aa.take(2, 3) for _ in range(2)]
    NM = [aa.take(2, 2) for _ in range(2)]
    ON = aa.take(CH, AH, DH)
    OT = aa.take(KD, SEQ)
    Y1 = aa.take(CH, D)
    Y2 = aa.take(CH, D)
    mhalf = minus_half

    SG = [sb(f"SG{u}", [P, SEQ]) for u in range(2)]
    HTt = [sb(f"HT{u}", [P, I0 // P, SEQ]) for u in range(2)]
    WM = HTt[0][:, :, :].rearrange("p i (a t) -> p (i a) t", t=P).rearrange("p (c h) t -> p c h t", h=MH)
    XG = [XN[u][:, 0, :] for u in range(2)]
    XGT = [xT[u][:, :, 0:P] for u in range(2)]
    SGE = [SG[u] for u in range(2)]
    shf = sh_gu[:, :, :].rearrange("p k n -> p (k n)")
    HE = [shf[:, u * I0:(u + 1) * I0] for u in range(2)]
    SE = shf[:, 2 * I0:3 * I0]
    HET = [HTt[u][:, :, 0:P] for u in range(2)]
    YO = [XN[u][:, 1, :] for u in range(2)]

    s_const, s_cmask = sem("const"), sem("const_masks")
    s_x = sem("load_x")
    s_w_r0, s_small, s_w_in, s_w_out = sem("load_router0"), sem("load_small"), sem("load_w_in"), sem("load_w_out")
    s_sh0, s_wgu0, s_wdn0 = sem("load_shared0"), sem("load_gate_up0"), sem("load_down0")
    s_l1a, s_l1b = sem("load_attention1"), sem("load_experts1")
    s_zero = sem("lists_zeroed")
    s_prep, s_prep2 = sem("prepare"), sem("prepare2")

    def norm_events(l):
        b = l * NSEQ
        n = {name: ev(f"norm_{name}", credit, 1, eng, b) for name, credit, eng in (
            ("var", 0, None), ("rstd", 0, None), ("xn", 0, None), ("tr", 2, "tensor"), ("xT", 1, "scalar"),
            ("keep", 2, "gpsimd"), ("lg", 2, "tensor"), ("lgc", 1, "vector"))}
        n["stored"] = [ev(f"norm_stored{u}", 1, 16, "sync", b // 2) for u in range(2)]
        n["chain"] = Chain(norm_chain, 2, b)
        return n

    norm_chain = sem("norm_chain")
    N = [norm_events(0), norm_events(1)]

    def ffn_events(l, ni, parts_before):
        return dict(ni=ni, gu=ev("ffn_gate_up", 0, 1, None, parts_before), sg=ev("ffn_silu", 2, 1, "scalar", parts_before),
                    ht=ev("ffn_inner", 4, 1, "vector", parts_before), dn=ev("ffn_down", 2, 1, "tensor", l * NSEQ),
                    add=ev("ffn_added", 2, 1, "vector", l * NSEQ))

    FF = [ffn_events(0, I0 // P, 0), ffn_events(1, I1S // P, NSEQ * I0 // P)]

    def expert_events(l):
        b = l * NJ
        x = {name: ev(f"expert_{name}", credit, 1, eng, b) for name, credit, eng in (
            ("idx", 0, "gpsimd"), ("xt", 2, "tensor"), ("xtc", 1, "scalar"), ("g", 0, "tensor"), ("u", 0, "tensor"),
            ("sg", 1, "scalar"), ("h", 2, "vector"), ("ht", 2, "tensor"), ("htc", 1, "vector"), ("dn", 2, "tensor"),
            ("yo", 2, "scalar"))}
        x["got"] = [ev(f"expert_got{u}", 0, 16, None, b // 2) for u in range(2)]
        x["out"] = [ev(f"expert_out{u}", 1, 16, "sync", b // 2) for u in range(2)]
        return x

    EX = [expert_events(0), expert_events(1)]

    s_route, s_rank, s_hot, s_exp2, s_m21, s_placed = (sem(n) for n in (
        "route_chain", "rank", "hot", "exp2", "m21", "placed"))
    route_count = [0]
    s_scat = [[ev(f"scatter{u}", 0, 16 * TOPK, None, l * NT // 2) for u in range(2)] for l in range(2)]
    s_sidx = [ev("scatter_idx", 0, TOPK, None, l * NT) for l in range(2)]
    s_slots = sem("slots")
    s_nop = sem("unfused_wait")
    s_sp = sem("softplus")
    s_spa = sem("softplus_act")
    M = {}
    for name, credit, eng in (
            ("proj", 0, "tensor"), ("mh", 1, "gpsimd"), ("dec", 1, "tensor"), ("ed", 1, "scalar"), ("ce", 1, "vector"),
            ("cv0", 1, "scalar"), ("cv", 1, "vector"), ("th", 1, "scalar"), ("zt", 1, "scalar"), ("sz", 1, "vector"),
            ("xs", 1, "vector"), ("ct", 1, "vector"), ("xtr", 1, "tensor"), ("gtr", 1, "tensor"), ("gm", 1, "vector"), ("bs", 1, "scalar"),
            ("xd", 1, "vector"), ("xw", 1, "vector"), ("wm", 1, "vector"), ("st", 1, "tensor"), ("ss", 1, "scalar"),
            ("y", 1, "tensor"), ("yg", 1, "vector"), ("o", 1, "tensor"), ("add", 1, "vector")):
        M[name] = ev(f"m_{name}", credit, 1, eng)
    M["chain"] = Chain(sem("m_chain"), TAPS - 2 + 1)
    A = {}
    for name, credit, eng in (
            ("q", 1, "tensor"), ("qc", 1, "scalar"), ("k", 1, "tensor"), ("kc", 1, "vector"), ("v", 1, "tensor"), ("vc", 1, "scalar"),
            ("s", 0, "tensor"), ("max", 2, "vector"), ("nm", 2, "vector"), ("exp", 2, "scalar"), ("pt", 2, "tensor"), ("ptc", 2, "vector"),
            ("pv", 2, "tensor"), ("sr", 1, "vector"), ("on", 1, "vector"), ("ot", 1, "tensor"), ("otc", 1, "scalar"),
            ("wo", 1, "tensor"), ("add", 1, "vector"), ("comb", 1, "vector")):
        A[name] = ev(f"a_{name}", credit, 1, eng)
    A["mchain"] = Chain(sem("a_max_chain"), 2)
    A["cchain"] = Chain(sem("a_combine_chain"), CH)
    A["y"] = [ev(f"a_y{k}", 0, 16) for k in range(CH * TOPK)]
    s_aidx = ev("a_idx")
    s_hmask = sem("head_mask")
    FY = [ev(f"fin_y{k}", 0, 16) for k in range(4)]
    FO = [ev(f"fin_out{k}", 1, 16, "sync") for k in range(2)]
    FC = ev("fin_done", 2, 1, "vector")
    FI = ev("fin_index")
    FCH = Chain(sem("fin_ch"), 1)

    block = ctx.enter_context(nc.Block())

    def unfuse(eng):
        eng.sem_inc(s_nop, 1)

    def open_events(eng, name):
        for e in engines.get(name, []):
            e.open(eng)

    x_in = a["u"].rearrange("(t p) d -> p t d", p=P)
    x_out = out.rearrange("(t p) d -> p t d", p=P)

    @block.sync
    def _(eng):
        open_events(eng, "sync")
        eng.dma_start(X[:, :, :], x_in).then_inc(s_x, 16)
        eng.dma_start(w_r0[:, :, 0:E], a["gate0"].rearrange("(k p) n -> p k n", p=P)).then_inc(s_w_r0, 16)
        eng.dma_start(w_r0[:, :, E:E + MH], a["w_dt"].rearrange("(k p) n -> p k n", p=P)).then_inc(s_w_r0, 16)
        eng.dma_start(dt_bias[:, :], a["dt_bias"].partition_broadcast(P)).then_inc(s_small, 16)
        eng.dma_start(a_neg[:, :], a["A_log"].partition_broadcast(P)).then_inc(s_small, 16)
        eng.dma_start(conv_w[:, :, :], a["conv_w"]).then_inc(s_small, 16)
        eng.dma_start(conv_b[:, :], a["conv_b"]).then_inc(s_small, 16)
        for q in range(2):
            eng.dma_start(d_par[q * MP:(q + 1) * MP, :], a["D_param"][q, :].partition_broadcast(MP)).then_inc(s_small, 16)
        eng.dma_start(w_in[:, :, :], a["w_in"].rearrange("(k p) n -> p k n", p=P)).then_inc(s_w_in, 16)
        eng.dma_start(w_out[:, :, :], a["w_out"].rearrange("(k p) n -> p k n", p=P)).then_inc(s_w_out, 16)
        eng.dma_start(sh_gu[:, :, :], a["sh_gu0"].rearrange("(k p) n -> p k n", p=P)).then_inc(s_sh0, 16)
        eng.dma_start(sh_dn[:, :, :], a["sh_dn0"].rearrange("(c p) n -> p c n", p=P)).then_inc(s_sh0, 16)
        eng.wait_ge(s_cmask, 3)
        for l in range(2):
            eng.dma_start(lists[l].rearrange("(p j) o -> p (j o)", p=P), zero_i[:, :]).then_inc(s_zero, 16)
        for e in range(E):
            eng.dma_start(wgu0[:, e, :, :], a["gu0"][e].rearrange("(k p) n -> p k n", p=P)).then_inc(s_wgu0, 16)

        def store_xn(l):
            def body(r):
                N[l]["xn"].wait(eng, r.n)
                rows = xn_rows[l].rearrange("(t p) d -> p t d", p=P)
                N[l]["stored"][r.u].mark(eng.dma_start(rows[:, bass.ds(r.n * CH, CH), :], XN[r.u][:, :, :]))
            rounds(eng, NSEQ, body)

        def lists_back(l):
            for u in range(2):
                s_scat[l][u].wait(eng, NT // 2 - 1)
            eng.dma_start(slot_tok[:, :], lists[l].rearrange("(p j) o -> p (j o)", p=P)).then_inc(s_slots, 16)

        def store_y(l):
            def body(r):
                EX[l]["yo"].wait(eng, r.n)
                rows = y_rows[l].rearrange("(j p) d -> p j d", p=P)
                EX[l]["out"][r.u].mark(eng.dma_start(rows[:, bass.ds(r.n, 1), :], YO[r.u].unsqueeze(1)))
            rounds(eng, NJ, body)

        store_xn(0)
        M["add"].wait(eng, NSEQ - 1)
        for e in range(E):
            eng.dma_start(wdn0[:, e, :, :], a["dn0"][e].rearrange("(c p) n -> p c n", p=P)).then_inc(s_wdn0, 16)
        lists_back(0)
        store_y(0)
        EX[0]["u"].wait(eng, NJ - 1)
        eng.dma_start(w_r1, a["gate1"].rearrange("(k p) n -> p k n", p=P)).then_inc(s_l1a, 16)
        eng.dma_start(w_qkv, a["qkv"].rearrange("(k p) n -> p k n", p=P)).then_inc(s_l1a, 16)
        eng.dma_start(w_o, a["w_o"].rearrange("(k p) n -> p k n", p=P)).then_inc(s_l1a, 16)
        eng.dma_start(sh_gu1[:, :, 0:I1S], a["sg1"].rearrange("(k p) n -> p k n", p=P)).then_inc(s_l1b, 16)
        eng.dma_start(sh_gu1[:, :, I1S:2 * I1S], a["su1"].rearrange("(k p) n -> p k n", p=P)).then_inc(s_l1b, 16)
        eng.dma_start(sh_dn1, a["sd1"].rearrange("(c p) n -> p c n", p=P)).then_inc(s_l1b, 16)
        for e in range(E):
            eng.dma_start(wgu1[:, e, :, 0:I1], a["wg1"][e].rearrange("(k p) n -> p k n", p=P)).then_inc(s_l1b, 16)
            eng.dma_start(wgu1[:, e, :, I1:2 * I1], a["wu1"][e].rearrange("(k p) n -> p k n", p=P)).then_inc(s_l1b, 16)
        eng.dma_start(wdn1, a["wd1"].rearrange("e p n -> p e n")).then_inc(s_l1b, 16)
        store_xn(1)
        lists_back(1)
        store_y(1)

        def store_out(r):
            FC.wait(eng, r.n)
            FO[r.u].mark(eng.dma_start(x_out[:, bass.ds(r.n, 1), :], X[:, bass.ds(r.n, 1), :]))
        rounds(eng, NT, store_out)
        for u in range(2):
            FO[u].wait(eng, NT // 2 - 1)

    @block.gpsimd
    def _(eng):
        open_events(eng, "gpsimd")
        eng.memset(zero_i[:, :], 0).then_inc(s_cmask, 1)
        n = 0
        for t, v in ((ident, 0.0), (tri_le, 1.0), (tri_gt, 1.0), (ones, 1.0), (quarter_le, 0.25), (ident_b, 0.0),
                     (ones_b, 1.0), (before_b, 1.0), (future_b, 0.0), (minus_half, -0.5)):
            eng.memset(t[:, :], v).then_inc(s_const, 1)
            n += 1
        eng.iota(itmp_e[:, :], [[1, E]], base=0, channel_multiplier=0).then_inc(s_const, 1)
        eng.iota(itmp_j[:, :], [[1, NJ]], base=0, channel_multiplier=0).then_inc(s_const, 1)
        eng.iota(token_id[:, :], [[P, NT]], base=0, channel_multiplier=1).then_inc(s_const, 1)
        eng.iota(par_i[:, 0:1], [[0, 1]], base=0, channel_multiplier=1).then_inc(s_const, 1)
        n += 4
        eng.wait_ge(s_const, n)
        sel = eng.affine_select
        for t, op, fill, sign in ((ident, ALU.not_equal, 1.0, -1), (ident_b, ALU.not_equal, 1.0, -1)):
            sel(out=t[:, :], in_=t[:, :], compare_op=op, fill=fill, base=0, pattern=[[-1, P]],
                channel_multiplier=1).then_inc(s_const, 1)
        sel(out=tri_le[:, :], in_=tri_le[:, :], compare_op=ALU.is_ge, fill=0.0, base=0, pattern=[[1, P]],
            channel_multiplier=-1).then_inc(s_const, 1)
        sel(out=quarter_le[:, :], in_=quarter_le[:, :], compare_op=ALU.is_ge, fill=0.0, base=0, pattern=[[1, P]],
            channel_multiplier=-1).then_inc(s_const, 1)
        sel(out=tri_gt[:, :], in_=tri_gt[:, :], compare_op=ALU.is_gt, fill=0.0, base=0, pattern=[[-1, P]],
            channel_multiplier=1).then_inc(s_const, 1)
        sel(out=before_b[:, :], in_=before_b[:, :], compare_op=ALU.is_gt, fill=0.0, base=0, pattern=[[1, P]],
            channel_multiplier=-1).then_inc(s_const, 1)
        sel(out=future_b[:, :], in_=future_b[:, :], compare_op=ALU.is_ge, fill=-BIG, base=0, pattern=[[-1, P]],
            channel_multiplier=1).then_inc(s_const, 1)
        eng.tensor_copy(iota_e[:, :], itmp_e[:, :]).then_inc(s_const, 1)
        eng.tensor_copy(iota_j[:, :], itmp_j[:, :]).then_inc(s_const, 1)
        n += 9
        eng.wait_ge(s_const, n)
        eng.sem_inc(s_cmask, 2)

        def norm_stage(l, r):
            ne = N[l]
            ne["var"].wait(eng, r.n)
            ne["rstd"].mark(eng.tensor_tensor(rstd[:, :], rstd[:, :], minus_half[:, :], ALU.pow))

        def keep_stage(l, r):
            ne = N[l]
            ne["xT"].wait(eng, r.n)
            ne["keep"].mark(eng.tensor_copy(XT[:, :, bass.ds(r.n * SEQ, SEQ)], xT[r.u][:, :, :]))

        def norm_body(l):
            def body(r):
                norm_stage(l, r)
                keep_stage(l, r)
            return body

        rounds(eng, NSEQ, norm_body(0))

        eng.wait_ge(s_sp, 4)

        def mamba(r):
            M["dec"].wait(eng, r.n, 1)
            av = DTA[:, bass.ds(r.n * CH, CH), :].rearrange("p c h -> p (c h)")
            M["mh"].mark(eng.tensor_tensor(
                MHm.rearrange("p c h t -> p (c h) t"),
                tri_le[:, :].unsqueeze(1).broadcast_to([P, CH * MH, P]),
                av.unsqueeze(2).broadcast_to([P, CH * MH, P]), ALU.mult))
        rounds(eng, NSEQ, mamba)

        def scatter(l):
            eng.wait_ge(s_placed, l + 1)
            eng.wait_ge(s_zero, 32)

            def body(r):
                for k in range(TOPK):
                    c = 2 * r.u + k
                    eng.tensor_copy(ring_idx[:, c:c + 1], dest_i[k][:, bass.ds(r.n, 1)])
                    eng.tensor_copy(ring_tok[:, c:c + 1], token_id[:, bass.ds(r.n, 1)]).then_inc(s_sidx[l].sem, 1)
                s_sidx[l].wait(eng, r.n)
                unfuse(eng)
                for k in range(TOPK):
                    c = 2 * r.u + k
                    eng.indirect_dma_start(lists[l], bass.IndirectOffsetOnAxis(ring_idx[:, c:c + 1], 0),
                                           ring_tok[:, c:c + 1], None).then_inc(s_scat[l][r.u].sem, 16)
                if r.u == 1:
                    for u in range(2):
                        s_scat[l][u].wait(eng, r.i)
            rounds(eng, NT, body)

        def gather_tiles(l):
            x = EX[l]
            eng.wait_ge(s_slots, 16 * (l + 1))
            for u in range(2):
                N[l]["stored"][u].wait(eng, NSEQ // 2 - 1)

            def body(r):
                c = r.u
                x["xt"].wait(eng, r.n, 2)
                x["idx"].mark(eng.tensor_copy(ring_idx[:, c:c + 1], slot_tok[:, bass.ds(r.n, 1)]))
                x["idx"].wait(eng, r.n)
                unfuse(eng)
                x["got"][r.u].mark(eng.indirect_dma_start(
                    XG[r.u], None, xn_rows[l], bass.IndirectOffsetOnAxis(ring_idx[:, c:c + 1], 0)))
            rounds(eng, NJ, body)

        scatter(0)
        gather_tiles(0)

        for u in range(2):
            EX[0]["out"][u].wait(eng, NJ // 2 - 1)

        def fetch_rows(r):
            A["comb"].wait(eng, r.n, 1)
            for c in range(CH):
                for k in range(TOPK):
                    q = c * TOPK + k
                    ins = eng.tensor_copy(ring_idx[:, q:q + 1], slot_i[k][:, bass.ds(r.n * CH + c, 1)])
            s_aidx.mark(ins)
            s_aidx.wait(eng, r.n)
            unfuse(eng)
            for c in range(CH):
                for k in range(TOPK):
                    q = c * TOPK + k
                    A["y"][q].mark(eng.indirect_dma_start(
                        (Y1, Y2)[k][:, c, :], None, y_rows[0],
                        bass.IndirectOffsetOnAxis(ring_idx[:, q:q + 1], 0)))
        EX[0]["dn"].wait(eng, NJ - 1)

        def attention(r):
            fetch_rows(r)
            norm_stage(1, r)
            keep_stage(1, r)
        rounds(eng, NSEQ, attention)
        scatter(1)
        gather_tiles(1)
        for u in range(2):
            EX[1]["out"][u].wait(eng, NJ // 2 - 1)

        def final(r):
            FC.wait(eng, r.n, 2)
            for k in range(TOPK):
                q = 2 * r.u + k
                ins = eng.tensor_copy(ring_idx[:, q:q + 1], slot_i[k][:, bass.ds(r.n, 1)])
            FI.mark(ins)
            FI.wait(eng, r.n)
            unfuse(eng)
            for k in range(TOPK):
                q = 2 * r.u + k
                FY[q].mark(eng.indirect_dma_start(
                    (Y1, Y2)[k][:, r.u, :], None, y_rows[1],
                    bass.IndirectOffsetOnAxis(ring_idx[:, q:q + 1], 0)))
        rounds(eng, NT, final)

    @block.scalar
    def _(eng):
        open_events(eng, "scalar")
        act = eng.activation

        def norm_stage(l, r):
            ne = N[l]
            ne["tr"].wait(eng, r.n)
            ne["lg"].wait(eng, r.n, 2)
            ne["keep"].wait(eng, r.n, 2)
            ne["xT"].mark(act(xT[r.u][:, :, :], bank[0][:, :].rearrange("p (k t) -> p k t", k=KD), ACT.Copy))

        eng.wait_ge(s_small, 96)
        act(a_neg[:, :], a_neg[:, :], ACT.Exp).then_inc(s_prep, 1)
        rounds(eng, NSEQ, lambda r: norm_stage(0, r))
        eng.wait_ge(s_sp, 2)
        flat = DTE[:, :, :].rearrange("p t h -> p (t h)")
        act(flat, flat, ACT.Exp).then_inc(s_spa, 1)
        eng.wait_ge(s_spa, 1)
        act(flat, flat, ACT.Ln, bias=1.0).then_inc(s_spa, 1)
        def exp2(l):
            eng.wait_ge(s_m21, l + 1)
            act(rs[:, 5, :], rs[:, 4, :], ACT.Exp).then_inc(s_exp2, 1)
        exp2(0)

        def mamba(r):
            M["proj"].wait(eng, r.n)
            M["cv"].wait(eng, r.n, 1)
            M["xs"].wait(eng, r.n, 1)
            M["ct"].wait(eng, r.n, 1)
            for c in range(3):
                src = bank[2][:, c * SEQ:(c + 1) * SEQ] if c < 2 else bank[3][:, 0:SEQ]
                ins = act(CV[:, c, :], src, ACT.Identity, bias=conv_b[:, c:c + 1], scale=conv_w[:, c, TAPS - 1:TAPS])
            M["cv0"].mark(ins)
            M["sz"].wait(eng, r.n, 1)
            M["zt"].mark(act(ZT.rearrange("p k t -> p (k t)"), bank[1][:, :], ACT.Tanh, scale=0.5))
            M["dec"].wait(eng, r.n)
            M["wm"].wait(eng, r.n, 1)
            M["xw"].wait(eng, r.n, 1)
            for c in range(CH):
                act(ED[:, c, :, :].rearrange("p h t -> p (h t)"), bank[4 + c][:, :], ACT.Exp)
            M["ce"].wait(eng, r.n, 1)
            M["y"].wait(eng, r.n, 1)
            M["ed"].mark(act(CE.rearrange("p h t -> p (h t)"), bank[6][0:MS, :], ACT.Exp))
            M["cv"].wait(eng, r.n)
            M["th"].mark(act(TH.rearrange("p c t -> p (c t)"), CV.rearrange("p c t -> p (c t)"), ACT.Tanh, scale=0.5))
            M["gtr"].wait(eng, r.n)
            M["gm"].wait(eng, r.n)
            M["st"].wait(eng, r.n, 1)
            M["bs"].mark(act(BS, bank[5][:, SEQ:SEQ + MS], ACT.Copy, scale=0.5))
            M["st"].wait(eng, r.n)
            M["y"].wait(eng, r.n, 1)
            M["ss"].mark(act(SS[0:MS, :], bank[6][0:MS, 0:MH * MP], ACT.Copy, scale=0.5))
        rounds(eng, NSEQ, mamba)

        def ffn(l):
            f, ni = FF[l], FF[l]["ni"]

            def body(r):
                for i in range(ni):
                    n = r.n * ni + i
                    f["gu"].wait(eng, n)
                    f["ht"].wait(eng, n, 2)
                    f["sg"].mark(act(SG[i % 2][:, :], bank[i][:, 0:SEQ], ACT.Silu))
            rounds(eng, NSEQ, body)
        ffn(0)

        def experts(l):
            x = EX[l]

            def xt_copy(r):
                x["xt"].wait(eng, r.n)
                x["h"].wait(eng, r.n, 2)
                x["xtc"].mark(act(XGT[r.u], bank[4][:, 0:KD * P].rearrange("p (k t) -> p k t", k=KD), ACT.Copy))

            def silu(r):
                x["g"].wait(eng, r.n)
                x["h"].wait(eng, r.n, 1)
                w = I0 if l == 0 else I1
                x["sg"].mark(act(SE[:, 0:w], bank[r.u][:, 0:w], ACT.Silu))

            def y_copy(r):
                x["dn"].wait(eng, r.n)
                x["out"][r.u].wait(eng, r.i, 1)
                x["yo"].mark(act(YO[r.u], bank[6 + r.u][:, 0:D], ACT.Copy))

            def body(r):
                xt_copy(r)
                silu(r)
                y_copy(r)
            rounds(eng, NJ, body)
        experts(0)

        def attention(r):
            norm_stage(1, r)
            A["q"].wait(eng, r.n)
            A["pv"].wait(eng, (r.n) * 8 - 1)
            A["qc"].mark(act(QT.rearrange("p k t -> p (k t)"), bank[0][:, :], ACT.Copy))
            A["v"].wait(eng, r.n)
            A["vc"].mark(act(V.rearrange("p k t -> p (k t)"), bank[0][:, :], ACT.Copy))
            for g in range(AH // 2):
                n = r.n * (AH // 2) + g
                A["nm"].wait(eng, n)
                A["pt"].wait(eng, n, 2)
                if g == 0:
                    A["sr"].wait(eng, r.n, 1)
                for h in range(2):
                    b = bank[1 + 2 * (g % 2) + h]
                    for q, (lo, hi) in enumerate(((0, 1), (1, 3))):
                        ins = act(PR[g % 2][:, h, lo:hi, :].rearrange("p b k -> p (b k)"), b[:, lo * P:hi * P], ACT.Exp,
                                  bias=NM[g % 2][:, h, q:q + 1],
                                  accum_out=SM[:, q, 2 * g + h:2 * g + h + 1])
                A["exp"].mark(ins)
            A["ot"].wait(eng, r.n)
            A["wo"].wait(eng, r.n, 1)
            A["otc"].mark(act(OT.rearrange("p k t -> p (k t)"), bank[0][:, :], ACT.Copy))
        rounds(eng, NSEQ, attention)
        exp2(1)
        ffn(1)
        experts(1)

    @block.vector
    def _(eng):
        open_events(eng, "vector")
        tt, ts, stt = eng.tensor_tensor, eng.tensor_scalar, eng.scalar_tensor_tensor

        def norm_stage(l, r):
            ne, ch = N[l], N[l]["chain"]
            ch.start(eng, r.n)
            unfuse(eng)
            for c in range(CH):
                ins = eng.bn_stats(stats[:, c, :], X[:, bass.ds(r.n * CH + c, 1), :].rearrange("p a d -> p (a d)"))
            ch(ins)
            unfuse(eng)
            for c in range(CH):
                ins = eng.bn_aggr(mv[:, c, :], stats[:, c, :])
            ch(ins)
            ch.end()
            ne["var"].mark(ts(rstd[:, :], mv[:, :, 1], EPS, None, ALU.add))
            ne["rstd"].wait(eng, r.n)
            ne["stored"][r.u].wait(eng, r.i, 1)
            ne["tr"].wait(eng, r.n, 2)
            for c in range(CH):
                ins = ts(XN[r.u][:, c, :], X[:, bass.ds(r.n * CH + c, 1), :].rearrange("p a d -> p (a d)"),
                         mv[:, c, 0:1], rstd[:, c:c + 1], ALU.subtract, ALU.mult)
            ne["xn"].mark(ins)
            ne["xn"].wait(eng, r.n)

        def logits_stage(l, r):
            ne = N[l]
            ne["lg"].wait(eng, r.n)
            b = bank[7] if l == 0 else bank[0]
            w = E + MH if l == 0 else E
            src = b[:, 0:CH * w].rearrange("p (c e) -> p c e", c=CH)
            if l == 0:
                tt(DTR[:, bass.ds(r.n * CH, CH), :], src[:, :, E:E + MH],
                   dt_bias[:, :].unsqueeze(1).broadcast_to([P, CH, MH]), ALU.add)
            ne["lgc"].mark(eng.tensor_copy(LG[:, bass.ds(r.n * CH, CH), :], src[:, :, 0:E]))

        eng.wait_ge(s_x, 16)
        eng.wait_ge(s_small, 96)
        rounds(eng, NSEQ, lambda r: (norm_stage(0, r), logits_stage(0, r)))

        N[0]["lgc"].wait(eng, NSEQ - 1)
        flat = lambda t: t[:, :, :].rearrange("p t h -> p (t h)")
        stt(flat(DTE), flat(DTR), -1.0, flat(DTR), ALU.mult, ALU.min).then_inc(s_sp, 1)
        eng.wait_ge(s_prep, 1)
        ts(a_neg[:, :], a_neg[:, :], -1.0, None, ALU.mult).then_inc(s_sp, 1)
        eng.wait_ge(s_spa, 2)
        stt(flat(DTR), flat(DTR), 0.0, flat(DTE), ALU.max, ALU.add).then_inc(s_sp, 1)
        eng.wait_ge(s_sp, 3)
        tt(DTA[:, :, :], DTR[:, :, :], a_neg[:, :].unsqueeze(1).broadcast_to([P, NT, MH]), ALU.mult).then_inc(s_sp, 1)
        eng.wait_ge(s_sp, 4)
        ts(flat(DTE), flat(DTR), 0.5, None, ALU.mult).then_inc(s_prep2, 1)
        ts(d_par[:, :], d_par[:, :], 0.5, None, ALU.mult).then_inc(s_prep2, 1)
        eng.wait_ge(s_w_out, 16)
        ts(w_out[:, :, :].rearrange("p k n -> p (k n)"), w_out[:, :, :].rearrange("p k n -> p (k n)"), 0.5, None,
           ALU.mult).then_inc(s_prep2, 1)

        def route(l):
            s, count = s_route, route_count

            def link(ins):
                count[0] += 1
                ins.then_inc(s, 1)
                eng.wait_ge(s, count[0])
            N[l]["lgc"].wait(eng, NSEQ - 1)
            work, masked = rt[0], rt[1]
            bc_e = lambda v: v.unsqueeze(2).broadcast_to([P, NT, E])
            ie = iota_e[:, :].unsqueeze(1).broadcast_to([P, NT, E])
            for k in range(TOPK):
                lg = LG if k == 0 else masked
                link(eng.tensor_reduce(rs[:, k, :], lg[:, :, :], AX.X, ALU.max))
                link(tt(work[:, :, :], lg[:, :, :], bc_e(rs[:, k, :]), ALU.is_lt))
                link(stt(work[:, :, :], work[:, :, :], float(E), ie, ALU.mult, ALU.add))
                link(eng.tensor_reduce(rs[:, 2, :], work[:, :, :], AX.X, ALU.min))
                link(tt(OH[k], ie, bc_e(rs[:, 2, :]), ALU.is_equal))
                if k == 0:
                    link(stt(masked[:, :, :], OH[0], -3.0e38, LG[:, :, :], ALU.mult, ALU.add))
            tt(rs[:, 4, :], rs[:, 1, :], rs[:, 0, :], ALU.subtract).then_inc(s_m21, 1)
            link(tt(work[:, :, :], OH[0], OH[1], ALU.add))
            eng.tensor_copy(hot_b[:, :, :], work[:, :, :]).then_inc(s_hot, 1)
            eng.wait_ge(s_exp2, l + 1)
            link(ts(rs[:, 6, :], rs[:, 5, :], 1.0, None, ALU.add))
            link(eng.reciprocal(cw[0][:, :], rs[:, 6, :]))
            link(tt(cw[1][:, :], rs[:, 5, :], cw[0][:, :], ALU.mult))
            eng.wait_ge(s_rank, l + 1)
            within = bank[6][:, 0:NT * E].rearrange("p (t e) -> p t e", e=E)
            total = bank[7][:, 0:NT * E].rearrange("p (t e) -> p t e", e=E)
            link(eng.tensor_copy(rt[1][:, :, :], total))
            src, dst = rt[1], rt[2]
            step = 1
            while step < NT:
                eng.tensor_copy(dst[:, 0:step, :], src[:, 0:step, :])
                link(tt(dst[:, step:NT, :], src[:, step:NT, :], src[:, 0:NT - step, :], ALU.add))
                src, dst, step = dst, src, step * 2
            link(ts(ex_i[:, :], src[:, NT - 1, :], float(P - 1), None, ALU.add))
            link(ts(ex_i[:, :], ex_i[:, :], 7, None, ALU.arith_shift_right))
            link(eng.tensor_copy(ex[:, 0, :], ex_i[:, :]))
            a_, b_, step = 0, 1, 1
            while step < E:
                eng.tensor_copy(ex[:, b_, 0:step], ex[:, a_, 0:step])
                link(tt(ex[:, b_, step:E], ex[:, a_, step:E], ex[:, a_, 0:E - step], ALU.add))
                a_, b_, step = b_, (b_ + 1 if b_ < 3 else 3), step * 2
            ends = ex[:, a_, :]
            eng.memset(ex[:, 5, 0:1], 0.0)
            link(ts(ex[:, 5, 1:E], ex[:, a_, 0:E - 1], float(P), None, ALU.mult))
            link(tt(dst[:, :, :], src[:, :, :], total, ALU.subtract))
            link(tt(dst[:, :, :], dst[:, :, :], within, ALU.add))
            link(tt(dst[:, :, :], dst[:, :, :], ex[:, 5, :].unsqueeze(1).broadcast_to([P, NT, E]), ALU.add))
            for k in range(TOPK):
                link(tt(work[:, :, :], dst[:, :, :], OH[k], ALU.mult))
                link(eng.tensor_reduce(rs[:, 7, :], work[:, :, :], AX.X, ALU.add))
                link(eng.tensor_copy(slot_i[k][:, :], rs[:, 7, :]))
                link(ts(dtmp_i[:, :], slot_i[k][:, :], P - 1, None, ALU.bitwise_and))
                link(ts(dest_i[k][:, :], slot_i[k][:, :], 7, None, ALU.arith_shift_right))
                link(stt(dest_i[k][:, :], dtmp_i[:, :], float(NJ), dest_i[k][:, :], ALU.mult, ALU.add))
            link(tt(tile_cmp[:, :, 0:E - 1], iota_j[:, :].unsqueeze(2).broadcast_to([P, NJ, E - 1]),
                    ends[:, 0:E - 1].unsqueeze(1).broadcast_to([P, NJ, E - 1]), ALU.is_ge))
            link(eng.tensor_reduce(tile_e[:, :], tile_cmp[:, :, 0:E - 1], AX.X, ALU.add))
            link(eng.tensor_copy(tile_expert[:, :], tile_e[:, :]))
            eng.wait_ge(s, count[0])
            eng.drain().then_inc(s_placed, 1)
        eng.wait_ge(s_cmask, 3)
        route(0)

        def mamba(r):
            ch = M["chain"]
            ch.start(eng, r.n)
            c0 = r.n * CH
            M["cv0"].wait(eng, r.n)
            for k in range(1, TAPS):
                for c in range(3):
                    src = bank[2][:, c * SEQ:(c + 1) * SEQ] if c < 2 else bank[3][:, 0:SEQ]
                    ins = stt(CV[:, c, k:SEQ], src[:, 0:SEQ - k], conv_w[:, c, TAPS - 1 - k:TAPS - k], CV[:, c, k:SEQ],
                              ALU.mult, ALU.add)
                if k < TAPS - 1:
                    ch(ins)
            M["cv"].mark(ins)
            M["zt"].wait(eng, r.n)
            M["yg"].wait(eng, r.n, 1)
            M["sz"].mark(stt(SZ.rearrange("p k t -> p (k t)"), ZT.rearrange("p k t -> p (k t)"), 1.0, bank[1][:, :],
                             ALU.add, ALU.mult))
            M["th"].wait(eng, r.n)
            M["y"].wait(eng, r.n, 1)
            stt(BT[0:MS, :], TH[0:MS, 2, :], 1.0, CV[0:MS, 2, :], ALU.add, ALU.mult)
            M["ct"].mark(stt(CT[0:MS, :], TH[MS:P, 2, :], 1.0, CV[MS:P, 2, :], ALU.add, ALU.mult))
            M["xs"].mark(stt(XS.rearrange("p k t -> p (k t)"), TH[:, 0:2, :].rearrange("p k t -> p (k t)"), 1.0,
                             CV[:, 0:2, :].rearrange("p k t -> p (k t)"), ALU.add, ALU.mult))
            M["ed"].wait(eng, r.n)
            M["ct"].wait(eng, r.n)
            M["ce"].mark(tt(CE, CE, CT[0:MS, P:SEQ].unsqueeze(1).broadcast_to([MS, MH, P]), ALU.mult))
            M["gtr"].wait(eng, r.n)
            M["gm"].mark(tt(GM, bank[5][:, 0:SEQ].rearrange("p (c t) -> p c t", c=CH),
                            quarter_le[:, :].unsqueeze(1).broadcast_to([P, CH, P]), ALU.mult))
            M["gm"].wait(eng, r.n)
            M["y"].wait(eng, r.n, 1)
            for c in range(CH):
                ins = tt(WM[:, c, :, :], ED[:, c, :, :], GM[:, c, :].unsqueeze(1).broadcast_to([P, MH, P]), ALU.mult)
            M["wm"].mark(ins)
            M["xtr"].wait(eng, r.n)
            dts = DTE[:, bass.ds(c0, CH), :].rearrange("p c h -> p (c h)")
            M["xd"].mark(tt(XD.rearrange("p c h d -> p (c h) d"), bank[4][:, :].rearrange("p (g d) -> p g d", d=MP),
                            dts.unsqueeze(2).broadcast_to([P, CH * MH, MP]), ALU.mult))
            M["xd"].wait(eng, r.n)
            M["xw"].mark(tt(XW, XD[:, 0, :, :], ED[:, 0, :, P - 1:P].broadcast_to([P, MH, MP]), ALU.mult))
            M["y"].wait(eng, r.n)
            M["o"].wait(eng, r.n, 1)
            for j in range(KD):
                ins = stt(YG[:, j, :], XS[:, j, :], d_par[:, j:j + 1], bank[7][:, j * SEQ:(j + 1) * SEQ],
                          ALU.mult, ALU.add)
            ch(ins)
            M["yg"].mark(tt(YG.rearrange("p k t -> p (k t)"), YG.rearrange("p k t -> p (k t)"), SZ.rearrange("p k t -> p (k t)"),
                  ALU.mult))
            M["o"].wait(eng, r.n)
            xs = X[:, bass.ds(c0, CH), :].rearrange("p c d -> p (c d)")
            M["add"].mark(tt(xs, xs, bank[4][:, :], ALU.add))
            ch.end()
        eng.wait_ge(s_prep2, 3)
        rounds(eng, NSEQ, mamba)

        def ffn(l):
            f, ni = FF[l], FF[l]["ni"]

            def body(r):
                for i in range(ni):
                    n = r.n * ni + i
                    f["sg"].wait(eng, n)
                    if i == 0:
                        f["dn"].wait(eng, r.n, 2)
                    f["ht"].mark(tt(HTt[r.u][:, i, :], SG[i % 2][:, :], bank[i][:, SEQ:2 * SEQ], ALU.mult))
                f["dn"].wait(eng, r.n)
                xs = X[:, bass.ds(r.n * CH, CH), :].rearrange("p c d -> p (c d)")
                f["add"].mark(tt(xs, xs, bank[4 + r.u][:, :], ALU.add))
            rounds(eng, NSEQ, body)
        M["add"].wait(eng, NSEQ - 1)
        ffn(0)

        def experts(l):
            x = EX[l]

            def h_stage(r):
                x["sg"].wait(eng, r.n)
                if l == 0:
                    x["u"].wait(eng, r.n)
                x["ht"].wait(eng, r.n, 2)
                if l == 0:
                    up, w = bank[2 + r.u][:, :], I0
                else:
                    up, w = bank[r.u][:, I1:2 * I1], I1
                x["h"].mark(tt(HE[r.u][:, 0:w], SE[:, 0:w], up, ALU.mult))

            def ht_copy(r):
                x["ht"].wait(eng, r.n)
                x["dn"].wait(eng, r.n, 2)
                w = (I0 if l == 0 else I1) // P
                x["htc"].mark(eng.tensor_copy(HET[r.u][:, 0:w, :], bank[5][:, 0:w * P].rearrange("p (c t) -> p c t", c=w)))

            rounds(eng, NJ, lambda r: (h_stage(r), ht_copy(r)))
        experts(0)

        FF[0]["add"].wait(eng, NSEQ - 1)

        def attention(r):
            ch = A["cchain"]
            ch.start(eng, r.n)
            for c in range(CH):
                xs = X[:, bass.ds(r.n * CH + c, 1), :].rearrange("p a d -> p (a d)")
                for k in range(TOPK):
                    A["y"][c * TOPK + k].wait(eng, r.n)
                    ins = stt(xs, (Y1, Y2)[k][:, c, :], cw[k][:, bass.ds(r.n * CH + c, 1)], xs, ALU.mult, ALU.add)
                    if k == 0:
                        ch(ins)
            A["comb"].mark(ins)
            A["comb"].wait(eng, r.n)
            ch.end()
            norm_stage(1, r)
            logits_stage(1, r)
            A["k"].wait(eng, r.n)
            A["pv"].wait(eng, r.n * (AH // 2) - 1)
            for m in range(2):
                ins = ts(KM[m].rearrange("p k t -> p (k t)"), bank[0][:, :], head_mask[:, m:m + 1], None, ALU.mult)
            A["kc"].mark(ins)
            mc = A["mchain"]

            def soft(g):
                n = r.n * (AH // 2) + g
                mc.start(eng, n)
                A["s"].wait(eng, n)
                b0 = 1 + 2 * (g % 2)
                A["exp"].wait(eng, n, 2)
                for h in range(2):
                    ins = eng.tensor_reduce(MX[g % 2][:, h, :], bank[b0 + h][:, 0:3 * P].rearrange("p (b k) -> p b k", b=3),
                                            AX.X, ALU.max)
                mc(ins)
                mc(tt(MX[g % 2][:, :, 1], MX[g % 2][:, :, 1], MX[g % 2][:, :, 2], ALU.max))
                A["nm"].mark(ts(NM[g % 2], MX[g % 2][:, :, 0:2], -1.0, None, ALU.mult))
                mc.end()

            def pt_copy(g):
                n = r.n * (AH // 2) + g
                A["pt"].wait(eng, n)
                A["pv"].wait(eng, n, 2)
                for h in range(2):
                    ins = eng.tensor_copy(PT[g % 2][:, h, :, :], bank[5 + h][:, 0:3 * P].rearrange("p (b k) -> p b k", b=3))
                A["ptc"].mark(ins)
            for g in range(AH // 2):
                soft(g)
                if g:
                    pt_copy(g - 1)
            pt_copy(AH // 2 - 1)
            A["exp"].wait(eng, (r.n + 1) * (AH // 2) - 1)
            A["sr"].mark(eng.reciprocal(SR.rearrange("p c h -> p (c h)"), SM.rearrange("p c h -> p (c h)")))
            A["sr"].wait(eng, r.n)
            A["pv"].wait(eng, (r.n + 1) * (AH // 2) - 1)
            A["ot"].wait(eng, r.n, 1)
            A["on"].mark(tt(ON.rearrange("p c h d -> p (c h) d"), bank[7][:, :].rearrange("p (g d) -> p g d", d=DH),
                            SR.rearrange("p c h -> p (c h)").unsqueeze(2).broadcast_to([P, CH * AH, DH]), ALU.mult))
            A["wo"].wait(eng, r.n)
            xs = X[:, bass.ds(r.n * CH, CH), :].rearrange("p c d -> p (c d)")
            A["add"].mark(tt(xs, xs, bank[0][:, :], ALU.add))
        ts(par_i[:, 1:2], par_i[:, 0:1], DH, None, ALU.bitwise_and).then_inc(s_hmask, 1)
        eng.wait_ge(s_hmask, 1)
        eng.tensor_copy(head_mask[:, 1:2], par_i[:, 1:2]).then_inc(s_hmask, 1)
        eng.wait_ge(s_hmask, 2)
        sc = DH ** -0.5
        ts(head_mask[:, 0:1], head_mask[:, 1:2], -sc / DH, sc, ALU.mult, ALU.add).then_inc(s_hmask, 1)
        eng.wait_ge(s_hmask, 3)
        ts(head_mask[:, 1:2], head_mask[:, 1:2], sc / DH, None, ALU.mult).then_inc(s_hmask, 1)
        eng.wait_ge(s_hmask, 4)
        EX[0]["dn"].wait(eng, NJ - 1)
        rounds(eng, NSEQ, attention)
        route(1)
        A["add"].wait(eng, NSEQ - 1)
        ffn(1)
        experts(1)
        FF[1]["add"].wait(eng, NSEQ - 1)

        def final(r):
            xs = X[:, bass.ds(r.n, 1), :].rearrange("p a d -> p (a d)")
            FCH.start(eng, r.n)
            for k in range(TOPK):
                FY[2 * r.u + k].wait(eng, r.i)
                ins = stt(xs, (Y1, Y2)[k][:, r.u, :], cw[k][:, bass.ds(r.n, 1)], xs, ALU.mult, ALU.add)
                FCH(ins) if k == 0 else FC.mark(ins)
            FCH.end()
        rounds(eng, NT, final)

    @block.tensor
    def _(eng):
        open_events(eng, "tensor")
        eng.wait_ge(s_cmask, 3)

        def mm(o, l, r, start, stop):
            return eng.matmul(o, l, r, start=start, stop=stop)

        def norm_stage(l, r):
            ne = N[l]
            ne["xn"].wait(eng, r.n)
            ne["xT"].wait(eng, r.n, 1)
            if l == 1:
                A["add"].wait(eng, r.n, 1)
            for c in range(CH):
                for k in range(KD):
                    ins = eng.transpose(bank[0][:, k * SEQ + c * P:k * SEQ + (c + 1) * P],
                                        XN[r.u][:, c, k * P:(k + 1) * P], ident[:, :])
            ne["tr"].mark(ins)

        def logits_stage(l, r):
            ne = N[l]
            ne["xT"].wait(eng, r.n)
            ne["lgc"].wait(eng, r.n, 1)
            w, b = (w_r0, bank[7]) if l == 0 else (w_r1, bank[0])
            n = E + MH if l == 0 else E
            for c in range(CH):
                for k in range(KD):
                    ins = mm(b[:, c * n:(c + 1) * n], xT[r.u][:, k, c * P:(c + 1) * P], w[:, k, :], k == 0, k == KD - 1)
            ne["lg"].mark(ins)

        eng.wait_ge(s_w_r0, 32)
        rounds(eng, NSEQ, lambda r: (norm_stage(0, r), logits_stage(0, r)))

        def rank(l):
            N[l]["lgc"].wait(eng, NSEQ - 1)
            eng.wait_ge(s_hot, l + 1)
            hot = hot_b[:, :, :].rearrange("p t e -> p (t e)")
            mm(bank[6][:, 0:NT * E], before_b[:, :], hot, True, True)
            mm(bank[7][:, 0:NT * E], ones_b[:, :], hot, True, True).then_inc(s_rank, 1)
        rank(0)

        def mamba(r):
            tok = bass.ds(r.n * SEQ, SEQ)
            M["sz"].wait(eng, r.n, 1)
            M["cv"].wait(eng, r.n, 1)
            for m in range(5):
                b, at = (bank[1], m * SEQ) if m < 2 else (bank[2], (m - 2) * SEQ) if m < 4 else (bank[3], 0)
                for k in range(KD):
                    ins = mm(b[:, at:at + SEQ], w_in[:, k, m * P:(m + 1) * P], XT[:, k, tok], k == 0, k == KD - 1)
            M["proj"].mark(ins)
            M["mh"].wait(eng, r.n)
            M["add"].wait(eng, r.n, 1)
            M["bs"].wait(eng, r.n, 1)
            M["ss"].wait(eng, r.n, 1)
            for c in range(CH):
                mm(bank[4 + c][:, :], tri_gt[:, :], MHm[:, c, :, :].rearrange("p h t -> p (h t)"), True, True)
            M["dec"].mark(mm(bank[6][0:MS, :], ones[:, :], MHm[:, 1, :, :].rearrange("p h t -> p (h t)"), True, True))
            M["ct"].wait(eng, r.n)
            M["ed"].wait(eng, r.n)
            for c in range(CH):
                mm(bank[5][:, c * P:(c + 1) * P], BT[0:MS, c * P:(c + 1) * P], CT[0:MS, c * P:(c + 1) * P], True, True)
            M["gtr"].mark(eng.transpose(bank[5][:, SEQ:SEQ + MS], BT[0:MS, 0:P], ident[0:MS, 0:MS]))
            M["xs"].wait(eng, r.n)
            for c in range(CH):
                for k in range(KD):
                    ins = eng.transpose(bank[4][:, c * D + k * P:c * D + (k + 1) * P], XS[:, k, c * P:(c + 1) * P],
                                        ident[:, :])
            M["xtr"].mark(ins)
            M["xw"].wait(eng, r.n)
            M["bs"].wait(eng, r.n)
            M["st"].mark(mm(bank[6][0:MS, 0:MH * MP], BS, XW.rearrange("p h d -> p (h d)"), True, True))
            M["wm"].wait(eng, r.n)
            M["yg"].wait(eng, r.n, 1)
            M["ss"].wait(eng, r.n)
            M["ce"].wait(eng, r.n)
            for h in range(MH):
                j, q = h // 2, h % 2
                for c in range(CH):
                    o = bank[7][q * MP:(q + 1) * MP, j * SEQ + c * P:j * SEQ + (c + 1) * P]
                    ins = mm(o, XD[:, c, h, :], WM[:, c, h, :], True, c == 0)
                    if c == 1:
                        ins = mm(o, SS[0:MS, h * MP:(h + 1) * MP], CE[:, h, :], False, True)
            M["y"].mark(ins)
            M["yg"].wait(eng, r.n)
            M["xd"].wait(eng, r.n)
            for c in range(CH):
                for k in range(KD):
                    ins = mm(bank[4][:, c * D:(c + 1) * D], YG[:, k, c * P:(c + 1) * P], w_out[:, k, :], k == 0, k == KD - 1)
            M["o"].mark(ins)
        N[0]["keep"].wait(eng, NSEQ - 1)
        eng.wait_ge(s_w_in, 16)
        eng.wait_ge(s_prep2, 3)
        eng.wait_ge(s_placed, 1)
        rounds(eng, NSEQ, mamba)

        def ffn(l):
            f, ni = FF[l], FF[l]["ni"]
            gu, dn = (sh_gu, sh_dn) if l == 0 else (sh_gu1, sh_dn1)

            def body(r):
                tok = bass.ds(r.n * SEQ, SEQ)
                for i in range(ni):
                    n = r.n * ni + i
                    f["ht"].wait(eng, n, ni)
                    for half in range(2):
                        for k in range(KD):
                            at = half * ni * P + i * P
                            ins = mm(bank[i][:, half * SEQ:(half + 1) * SEQ], gu[:, k, at:at + P], XT[:, k, tok],
                                     k == 0, k == KD - 1)
                    f["gu"].mark(ins)
                f["ht"].wait(eng, (r.n + 1) * ni - 1)
                f["add"].wait(eng, r.n, 2)
                for c in range(CH):
                    for i in range(ni):
                        ins = mm(bank[4 + r.u][:, c * D:(c + 1) * D], HTt[r.u][:, i, c * P:(c + 1) * P], dn[:, i, :],
                                 i == 0, i == ni - 1)
                f["dn"].mark(ins)
            rounds(eng, NSEQ, body)
        M["add"].wait(eng, NSEQ - 1)
        eng.wait_ge(s_sh0, 32)
        ffn(0)

        def experts(l):
            x = EX[l]

            def xt(r):
                x["got"][r.u].wait(eng, r.i)
                x["xtc"].wait(eng, r.n, 1)
                for k in range(KD):
                    ins = eng.transpose(bank[4][:, k * P:(k + 1) * P], XG[r.u][:, k * P:(k + 1) * P], ident[:, :])
                x["xt"].mark(ins)

            def gate_up(r):
                x["xtc"].wait(eng, r.n)
                x["h"].wait(eng, r.n, 2)
                e = eng.value_load(tile_expert[0:1, bass.ds(r.n, 1)], min_val=0, max_val=E - 1)
                for k in range(KD):
                    if l == 0:
                        rhs = wgu0[:, bass.ds(e, 1), k, 0:I0]
                    else:
                        rhs = wgu1[:, bass.ds(e, 1), k, :]
                    w = I0 if l == 0 else 2 * I1
                    ins = mm(bank[r.u][:, 0:w], XGT[r.u][:, k, :], rhs, k == 0, k == KD - 1)
                x["g"].mark(ins)
                if l == 0:
                    for k in range(KD):
                        ins = mm(bank[2 + r.u][:, :], XGT[r.u][:, k, :], wgu0[:, bass.ds(e, 1), k, I0:2 * I0], k == 0, k == KD - 1)
                    x["u"].mark(ins)
                return e

            def down(r, e):
                w = (I0 if l == 0 else I1) // P
                x["h"].wait(eng, r.n)
                x["htc"].wait(eng, r.n, 1)
                for c in range(w):
                    ins = eng.transpose(bank[5][:, c * P:(c + 1) * P], HE[r.u][:, c * P:(c + 1) * P], ident[:, :])
                x["ht"].mark(ins)
                x["htc"].wait(eng, r.n)
                x["yo"].wait(eng, r.n, 2)
                for c in range(w):
                    rhs = wdn0[:, bass.ds(e, 1), c, :] if l == 0 else wdn1[:, bass.ds(e, 1), :]
                    ins = mm(bank[6 + r.u][:, 0:D], HET[r.u][:, c, :], rhs, c == 0, c == w - 1)
                x["dn"].mark(ins)

            def body(r):
                xt(r)
                e = gate_up(r)
                down(r, e)
            rounds(eng, NJ, body)
        eng.wait_ge(s_wgu0, 16 * E)
        eng.wait_ge(s_wdn0, 16 * E)
        FF[0]["add"].wait(eng, NSEQ - 1)
        experts(0)

        def attention(r):
            norm_stage(1, r)
            logits_stage(1, r)
            xt = xT[r.u]
            N[1]["lgc"].wait(eng, r.n)
            for m in range(KD):
                for k in range(KD):
                    ins = mm(bank[0][:, m * SEQ:(m + 1) * SEQ], w_qkv[:, k, m * P:(m + 1) * P], xt[:, k, :], k == 0, k == KD - 1)
            A["q"].mark(ins)
            A["qc"].wait(eng, r.n)
            for c in range(CH):
                for k in range(KD):
                    ins = mm(bank[0][:, c * D:(c + 1) * D], xt[:, k, c * P:(c + 1) * P], w_qkv[:, k, 2 * D:3 * D], k == 0, k == KD - 1)
            A["v"].mark(ins)
            A["vc"].wait(eng, r.n)
            for m in range(KD):
                for k in range(KD):
                    ins = mm(bank[0][:, m * SEQ:(m + 1) * SEQ], w_qkv[:, k, D + m * P:D + (m + 1) * P], xt[:, k, :], k == 0, k == KD - 1)
            A["k"].mark(ins)
            A["kc"].wait(eng, r.n)

            def scores(g):
                n = r.n * (AH // 2) + g
                A["exp"].wait(eng, n, 2)
                for h in range(2):
                    hd = 2 * g + h
                    j, row, par = hd * DH // P, hd * DH % P // 32 * 32, hd % 2
                    b = bank[1 + 2 * (g % 2) + h]
                    for q in range(CH):
                        o = b[:, q * P:q * P + (q + 1) * P]
                        mm(o, QT[row:row + 32, j, q * P:(q + 1) * P], KM[par][row:row + 32, j, 0:(q + 1) * P], True, False)
                        ins = mm(b[:, 2 * q * P:(2 * q + 1) * P], ident_b[:, :], future_b[:, :], False, True)
                A["s"].mark(ins)

            def weigh(g):
                n = r.n * (AH // 2) + g
                A["exp"].wait(eng, n)
                A["ptc"].wait(eng, n, 1)
                for h in range(2):
                    for b in range(3):
                        ins = eng.transpose(bank[5 + h][:, b * P:(b + 1) * P], PR[g % 2][:, h, b, :], ident[:, :])
                A["pt"].mark(ins)
                A["ptc"].wait(eng, n)
                if g == 0:
                    A["on"].wait(eng, r.n, 1)
                for h in range(2):
                    hd = 2 * g + h
                    for b, (q, t) in enumerate(((0, 0), (1, 0), (1, 1))):
                        o = bank[7][:, q * D + hd * DH:q * D + (hd + 1) * DH]
                        ins = mm(o, PT[g % 2][:, h, b, :], V[:, t, hd * DH:(hd + 1) * DH], b != 2, b != 1)
                A["pv"].mark(ins)
            for g in range(AH // 2):
                scores(g)
                if g:
                    weigh(g - 1)
            weigh(AH // 2 - 1)
            A["on"].wait(eng, r.n)
            for c in range(CH):
                for k in range(KD):
                    ins = eng.transpose(bank[0][:, k * SEQ + c * P:k * SEQ + (c + 1) * P],
                                        ON[:, c, k * AH // 2:(k + 1) * AH // 2, :].rearrange("p h d -> p (h d)"), ident[:, :])
            A["ot"].mark(ins)
            A["otc"].wait(eng, r.n)
            for c in range(CH):
                for k in range(KD):
                    ins = mm(bank[0][:, c * D:(c + 1) * D], OT[:, k, c * P:(c + 1) * P], w_o[:, k, :], k == 0, k == KD - 1)
            A["wo"].mark(ins)
        eng.wait_ge(s_l1a, 48)
        rounds(eng, NSEQ, attention)
        A["add"].wait(eng, NSEQ - 1)
        rank(1)
        eng.wait_ge(s_l1b, 16 * (3 + 2 * E + 1))
        N[1]["keep"].wait(eng, NSEQ - 1)
        ffn(1)
        FF[1]["add"].wait(eng, NSEQ - 1)
        eng.wait_ge(s_placed, 2)
        experts(1)


_NAMES = ["u", "w_in", "w_dt", "conv_w", "conv_b", "w_out", "A_log", "D_param", "dt_bias", "gate0", "gu0", "dn0",
          "sh_gu0", "sh_dn0", "qkv", "w_o", "gate1", "wg1", "wu1", "wd1", "sg1", "su1", "sd1"]


def kernel(L0_attn_u, L0_attn_W_in, L0_attn_conv_w, L0_attn_conv_b, L0_attn_W_out, L0_attn_A_log, L0_attn_D_param,
           L0_attn_dt_bias, L0_ffn_gate_w, L0_ffn_w_gate_up, L0_ffn_w_down, L0_ffn_shared_gate_up, L0_ffn_shared_down,
           L1_attn_w_qkv, L1_attn_w_o, L1_ffn_gate_w, L1_ffn_wg, L1_ffn_wu, L1_ffn_wd, L1_ffn_sg, L1_ffn_su, L1_ffn_sd):
    import numpy as np
    import concourse.bacc as bacc
    from concourse.bass_utils import run_bass_kernel_spmd

    ndt = 2 * D + 2 * MS
    given = dict(
        u=np.asarray(L0_attn_u).reshape(NTOK, D), w_in=np.asarray(L0_attn_W_in)[:ndt].T,
        w_dt=np.asarray(L0_attn_W_in)[ndt:].T, 
        conv_w=np.asarray(L0_attn_conv_w).reshape(3, P, TAPS).transpose(1, 0, 2), conv_b=np.asarray(L0_attn_conv_b).reshape(3, P).T,
        w_out=np.asarray(L0_attn_W_out).T, A_log=L0_attn_A_log, D_param=np.asarray(L0_attn_D_param).reshape(KD, 2).T, dt_bias=L0_attn_dt_bias,
        gate0=L0_ffn_gate_w, gu0=L0_ffn_w_gate_up, dn0=L0_ffn_w_down, sh_gu0=L0_ffn_shared_gate_up,
        sh_dn0=L0_ffn_shared_down, qkv=L1_attn_w_qkv, w_o=L1_attn_w_o, gate1=np.asarray(L1_ffn_gate_w).T,
        wg1=L1_ffn_wg, wu1=L1_ffn_wu, wd1=L1_ffn_wd, sg1=L1_ffn_sg, su1=L1_ffn_su, sd1=L1_ffn_sd)
    nc = bacc.Bacc("TRN2", target_bir_lowering=False, num_devices=1)
    arrays, aps = {}, {}
    for name in _NAMES:
        v = np.ascontiguousarray(given[name])
        arrays[f"in_{name}"] = v
        aps[name] = nc.dram_tensor(f"in_{name}", v.shape, mybir.dt.from_np(v.dtype), kind="ExternalInput").ap()
    out = nc.dram_tensor("out", (NTOK, D), F32, kind="ExternalOutput").ap()
    build(nc, aps, out)
    r = run_bass_kernel_spmd(nc, [arrays], core_ids=[0])
    return r.results[0]["out"].reshape(NSEQ, SEQ, D)
```

```python
from contextlib import ExitStack

import concourse.bass as bass
from concourse import mybir

F32, BF16, I32 = mybir.dt.float32, mybir.dt.bfloat16, mybir.dt.int32
ALU, ACT, AX = mybir.AluOpType, mybir.ActivationFunctionType, mybir.AxisListType

P = 128
NSEQ, SEQ, D = 16, 256, 256
NTOK = NSEQ * SEQ
NT = NTOK // P
CH = SEQ // P
KD = D // P
E, TOPK = 8, 2
NJ = (NTOK * TOPK + E * (P - 1)) // P
NJ += NJ % 2
MH, MP, MS, TAPS = 4, 64, 64, 4
I0, I1S, I1 = 512, 256, 128
AH, DH = 16, 16
BIG = 1.0e30
EPS = 1e-5
PAIRS = AH // 2


class Round:

    def __init__(self, i, u):
        self.i, self.u, self.n = i, u, i * 2 + u

    def back(self, k=1):
        u = self.u - k
        return Round(self.i + (u // 2), u % 2)


class Event:

    def __init__(self, sem, credit=0, step=1, base=0):
        self.sem, self.credit, self.step, self.base = sem, credit, step, base

    def open(self, eng):
        if self.credit:
            eng.sem_inc(self.sem, self.credit * self.step)

    def mark(self, ins):
        ins.then_inc(self.sem, self.step)

    def wait(self, eng, n, back=0):
        eng.wait_ge(self.sem, (n + (1 - back + self.credit + self.base)) * self.step)


class Chain:

    def __init__(self, sem, per, before=0):
        self.sem, self.per, self.k, self.before = sem, per, 0, before

    def start(self, eng, n):
        self.eng, self.base, self.k = eng, (n + self.before) * self.per, 0

    def __call__(self, ins):
        self.k += 1
        ins.then_inc(self.sem, 1)
        self.eng.wait_ge(self.sem, self.base + self.k)

    def end(self):
        assert self.k == self.per, (self.k, self.per)


def rounds(eng, count, body):
    with eng.Fori(0, count // 2) as i:
        for u in range(2):
            body(Round(i, u))


def pipelined(eng, count, depth, body):
    def turn(t):
        body(*(Round((t - k) // 2, (t - k) % 2) if 0 <= t - k < count else None for k in range(depth)))
    full = depth // 2
    for t in range(2 * full):
        turn(t)
    with eng.Fori(full, count // 2) as i:
        for u in range(2):
            r = Round(i, u)
            body(*(r.back(k) for k in range(depth)))
    for t in range(count, count + depth - 1):
        turn(t)


def attention(eng, first=None, turns=None, last=None, new_pieces={}, old_pieces={}, done_pieces={}, turns_before=False):
    def body(new, r, old, done):
        def at(f, k, g):
            who = r if g >= k else old
            if f and who:
                f(who, (g - k) % PAIRS)
        for g in range(PAIRS):
            if turns_before:
                at(turns, 1, g)
                at(first, 0, g)
            else:
                at(first, 0, g)
                at(turns, 1, g)
            at(last, 2, g)
            for who, pieces in ((old, old_pieces), (done, done_pieces), (new, new_pieces)):
                if who and g in pieces:
                    pieces[g](who)
    pipelined(eng, NSEQ, 4, body)


def build(nc, a, out):
    ctx = ExitStack()
    with ctx:
        program(nc, ctx, a, out)


def program(nc, ctx, a, out):
    def sb(name, shape, dt=F32):
        return ctx.enter_context(nc.sbuf_tensor(name, shape, dt))

    def sem(name):
        return ctx.enter_context(nc.semaphore(name))

    named, engines = {}, {}

    def ev(name, credit=0, step=1, by=None, base=0):
        first = name not in named
        if first:
            named[name] = sem(name)
        e = Event(named[name], credit, step, base)
        if first and by:
            engines.setdefault(by, []).append(e)
        return e

    bank = [ctx.enter_context(nc.psum_tensor(f"bank{i}", [P, 512], F32)) for i in range(8)]

    xn_rows = [nc.dram_tensor(f"xn_rows{l}", (NTOK, D), F32, kind="Internal").ap() for l in range(2)]
    y_rows = [nc.dram_tensor(f"y_rows{l}", (NJ * P, D), F32, kind="Internal").ap() for l in range(2)]
    lists = [nc.dram_tensor(f"slot_token{l}", (P * NJ, 1), I32, kind="Internal").ap() for l in range(2)]

    ident = sb("ident", [P, P])
    tri_le = sb("tri_le", [P, P])
    tri_gt = sb("tri_gt", [P, P])
    ones = sb("ones", [P, MS])
    quarter_le = sb("quarter_le", [P, P])
    ones_b = sb("ones_b", [P, P], BF16)
    before_b = sb("before_b", [P, P], BF16)
    ident_b = sb("ident_b", [P, P], BF16)
    future_b = sb("future_b", [P, P], BF16)
    iota_e = sb("iota_e", [P, E])
    iota_j = sb("iota_j", [P, NJ])
    token_id = sb("token_id", [P, NT], I32)
    head_mask = sb("head_mask", [P, 2])
    minus_half = sb("minus_half", [P, CH])
    zero_i = sb("zero_i", [P, NJ], I32)
    itmp_e = sb("itmp_e", [P, E], I32)

    par_i = sb("par_i", [P, 2], I32)

    X = sb("X", [P, NT, D])
    XT = sb("XT", [P, KD, NTOK])
    WGU = sb("WGU", [P, E * KD * 2 * I0])
    ARENA = sb("ARENA", [P, E * I0 // P * D])
    w_in = sb("w_in", [P, KD, 2 * D + 2 * MS])
    w_r0 = sb("w_r0", [P, KD, E + MH])
    w_out = sb("w_out", [P, KD, D])
    sh_gu = sb("sh_gu", [P, KD, 2 * I0])
    sh_dn = sb("sh_dn", [P, I0 // P, D])

    class Area:

        def __init__(self, t):
            self.t, self.at = t, 0

        def take(self, *shape):
            n = 1
            for s in shape:
                n *= s
            v = self.t[:, self.at:self.at + n]
            self.at += n
            assert self.at <= self.t.shape[1]
            names = "abcde"[:len(shape)]
            if len(shape) > 1:
                v = v.rearrange(f"p ({' '.join(names)}) -> p {' '.join(names)}",
                                **{c: s for c, s in zip(names, shape)})
            return v

    wgu0 = WGU[:, :].rearrange("p (e k n) -> p e k n", e=E, k=KD)
    wdn0 = ARENA[:, :].rearrange("p (e c n) -> p e c n", e=E, c=I0 // P)

    XN = [sb(f"XN{u}", [P, CH, D]) for u in range(2)]
    xT = [sb(f"xT{u}", [P, KD, SEQ]) for u in range(2)]
    stats = sb("stats", [P, CH, 6])
    mv = sb("mv", [P, CH, 2])
    rstd = sb("rstd", [P, CH])
    LG = sb("LG", [P, NT, E])
    DTR = sb("DTR", [P, NT, MH])
    DTA = sb("DTA", [P, NT, MH])
    DTE = sb("DTE", [P, NT, MH])
    dt_bias = sb("dt_bias", [P, MH])
    a_neg = sb("a_neg", [P, MH])
    conv_w = sb("conv_w", [P, 3, TAPS])
    conv_b = sb("conv_b", [P, 3])
    d_par = sb("d_par", [P, KD])
    hot_b = sb("hot_b", [P, NT, E], BF16)
    rs = sb("route_small", [P, 8, NT])
    ex = sb("route_experts", [P, 8, E])
    ex_i = sb("route_experts_i", [P, E], I32)
    tile_e = sb("tile_e", [P, NJ])
    tile_expert = sb("tile_expert", [P, NJ], I32)
    slot_i = [sb(f"slot{k}", [P, NT], I32) for k in range(TOPK)]
    dest_i = [sb(f"dest{k}", [P, NT], I32) for k in range(TOPK)]
    dtmp_i = sb("dtmp_i", [P, NT], I32)
    cw = [sb(f"cw{k}", [P, NT]) for k in range(TOPK)]
    ring_idx = sb("ring_idx", [P, 8], I32)
    ring_tok = sb("ring_tok", [P, 8], I32)
    slot_tok = sb("slot_tok", [P, NJ], I32)
    itmp_j = slot_tok

    rr = Area(ARENA)
    rr.at = 1024
    OH = [rr.take(NT, E) for k in range(TOPK)]
    rt = [rr.take(NT, E) for n in range(3)]
    tile_cmp = rr.take(NJ, E)

    ar = Area(ARENA)
    MHm = ar.take(CH, MH, P)
    ED = ar.take(CH, MH, P)
    CV = ar.take(3, SEQ)
    TH = ar.take(3, SEQ)
    XS = ar.take(KD, SEQ)
    ZT = ar.take(KD, SEQ)
    SZ = ar.take(KD, SEQ)
    XD = ar.take(CH, MH, MP)
    XW = ar.take(MH, MP)
    YG = ar.take(KD, SEQ)
    GM = ar.take(CH, P)
    BS = ar.take(MS)
    BT = ar.take(SEQ)
    CT = ar.take(SEQ)
    SS = ar.take(MH * MP)
    CE = ar.take(MH, P)[0:MS]

    wa = Area(WGU)
    wgu1 = wa.take(E, KD, 2 * I1)
    wdn1 = wa.take(E, D)
    sh_gu1 = wa.take(KD, 2 * I1S)
    sh_dn1 = wa.take(I1S // P, D)
    w_qkv = wa.take(KD, 3 * D)
    w_o = wa.take(KD, D)
    w_r1 = wa.take(KD, E)
    Y1 = wa.take(CH, D)
    Y2 = wa.take(CH, D)
    OT = wa.take(KD, SEQ)
    aa = Area(ARENA)
    QT = [aa.take(KD, SEQ) for _ in range(2)]
    KM = [[aa.take(KD, SEQ) for _ in range(2)] for _ in range(2)]
    V = [aa.take(CH, D) for _ in range(2)]
    PR = [aa.take(2, 3, P) for _ in range(2)]
    PT = [aa.take(2, 3, P) for _ in range(2)]
    SM = [aa.take(CH, AH) for _ in range(2)]
    SR = aa.take(CH, AH)
    MX = [aa.take(2, 3) for _ in range(2)]
    NM = [aa.take(2, 2) for _ in range(2)]
    ON = aa.take(CH, AH, DH)

    SG = [sb(f"SG{u}", [P, SEQ]) for u in range(2)]
    HTt = [sb(f"HT{u}", [P, I0 // P, SEQ]) for u in range(2)]
    WM = HTt[0][:, :, :].rearrange("p i (a t) -> p (i a) t", t=P).rearrange("p (c h) t -> p c h t", h=MH)
    XG = [XN[u][:, 0, :] for u in range(2)]
    XGT = [xT[u][:, :, 0:P] for u in range(2)]
    SGE = [SG[u] for u in range(2)]
    shf = sh_gu[:, :, :].rearrange("p k n -> p (k n)")
    HE = [shf[:, u * I0:(u + 1) * I0] for u in range(2)]
    SE = shf[:, 2 * I0:3 * I0]
    HET = [HTt[u][:, :, 0:P] for u in range(2)]
    YO = [XN[u][:, 1, :] for u in range(2)]

    s_const, s_cmask = sem("const"), sem("const_masks")
    s_x = sem("load_x")
    s_w_r0, s_small, s_w_in, s_w_out = sem("load_router0"), sem("load_small"), sem("load_w_in"), sem("load_w_out")
    s_sh0, s_wgu0, s_wdn0 = sem("load_shared0"), sem("load_gate_up0"), sem("load_down0")
    s_l1a, s_l1b = sem("load_attention1"), sem("load_experts1")
    s_zero = sem("lists_zeroed")
    s_prep, s_prep2 = sem("prepare"), sem("prepare2")

    def norm_events(l):
        b = l * NSEQ
        n = {name: ev(f"norm_{name}", credit, 1, eng, b) for name, credit, eng in (
            ("var", 0, None), ("rstd", 0, None), ("xn", 0, None), ("tr", 2, "tensor"), ("xT", 1, "scalar"),
            ("keep", 2, "gpsimd"), ("lg", 2, "tensor"), ("lgc", 1, "vector"))}
        n["stored"] = [ev(f"norm_stored{u}", 1, 16, "sync", b // 2) for u in range(2)]
        n["chain"] = Chain(norm_chain, 2, b)
        return n

    norm_chain = sem("norm_chain")
    N = [norm_events(0), norm_events(1)]

    def ffn_events(l, ni, parts_before):
        return dict(ni=ni, gu=ev("ffn_gate_up", 0, 1, None, parts_before), sg=ev("ffn_silu", 2, 1, "scalar", parts_before),
                    ht=ev("ffn_inner", 4, 1, "vector", parts_before), dn=ev("ffn_down", 2, 1, "tensor", l * NSEQ),
                    add=ev("ffn_added", 2, 1, "vector", l * NSEQ))

    FF = [ffn_events(0, I0 // P, 0), ffn_events(1, I1S // P, NSEQ * I0 // P)]

    def expert_events(l):
        b = l * NJ
        x = {name: ev(f"expert_{name}", credit, 1, eng, b) for name, credit, eng in (
            ("idx", 0, "gpsimd"), ("xt", 2, "tensor"), ("xtc", 1, "scalar"), ("g", 0, "tensor"), ("u", 0, "tensor"),
            ("sg", 1, "scalar"), ("h", 2, "vector"), ("ht", 2, "tensor"), ("htc", 1, "vector"), ("dn", 2, "tensor"),
            ("yo", 2, "scalar"))}
        x["got"] = [ev(f"expert_got{u}", 0, 16, None, b // 2) for u in range(2)]
        x["out"] = [ev(f"expert_out{u}", 1, 16, "sync", b // 2) for u in range(2)]
        return x

    EX = [expert_events(0), expert_events(1)]

    s_route, s_rank, s_hot, s_exp2, s_m21, s_placed = (sem(n) for n in (
        "route_chain", "rank", "hot", "exp2", "m21", "placed"))
    route_count = [0]
    s_scat = [[ev(f"scatter{u}", 0, 16 * TOPK, None, l * NT // 2) for u in range(2)] for l in range(2)]
    s_sidx = [ev("scatter_idx", 0, TOPK, None, l * NT) for l in range(2)]
    s_slots = sem("slots")
    s_nop = sem("unfused_wait")
    s_sp = sem("softplus")
    s_spa = sem("softplus_act")
    M = {}
    for name, credit, eng in (
            ("proj", 0, "tensor"), ("mh", 1, "gpsimd"), ("dec", 1, "tensor"), ("ed", 1, "scalar"), ("ce", 1, "vector"),
            ("cv0", 1, "scalar"), ("cv", 1, "vector"), ("th", 1, "scalar"), ("zt", 1, "scalar"), ("sz", 1, "vector"),
            ("xs", 1, "vector"), ("ct", 1, "vector"), ("xtr", 1, "tensor"), ("gtr", 1, "tensor"), ("gm", 1, "vector"), ("bs", 1, "scalar"),
            ("xd", 1, "vector"), ("xw", 1, "vector"), ("wm", 1, "vector"), ("st", 1, "tensor"), ("ss", 1, "scalar"),
            ("y", 1, "tensor"), ("yg", 1, "vector"), ("o", 1, "tensor"), ("add", 1, "vector")):
        M[name] = ev(f"m_{name}", credit, 1, eng)
    M["chain"] = Chain(sem("m_chain"), TAPS - 2 + 1)
    A = {}
    for name, credit, eng in (
            ("q", 1, "tensor"), ("qc", 1, "scalar"), ("k", 1, "tensor"), ("kc", 1, "vector"), ("v", 1, "tensor"), ("vc", 1, "scalar"),
            ("s", 0, "tensor"), ("max", 2, "vector"), ("nm", 2, "vector"), ("exp", 2, "scalar"), ("pt", 2, "tensor"), ("ptc0", 2, "vector"), ("ptc1", 2, "scalar"),
            ("pv", 2, "tensor"), ("sr", 2, "vector"), ("on", 2, "vector"), ("ot", 1, "tensor"), ("otc", 1, "scalar"),
            ("wo", 1, "tensor"), ("add", 3, "vector"), ("comb", 1, "vector")):
        A[name] = ev(f"a_{name}", credit, 1, eng)
    A["mchain"] = Chain(sem("a_max_chain"), 2)
    A["cchain"] = Chain(sem("a_combine_chain"), CH)
    A["y"] = [ev(f"a_y{k}", 0, 16) for k in range(CH * TOPK)]
    s_aidx = ev("a_idx")
    s_hmask = sem("head_mask")
    FY = [ev(f"fin_y{k}", 0, 16) for k in range(4)]
    FO = [ev(f"fin_out{k}", 1, 16, "sync") for k in range(2)]
    FC = ev("fin_done", 2, 1, "vector")
    FI = ev("fin_index")
    FCH = Chain(sem("fin_ch"), 1)

    block = ctx.enter_context(nc.Block())

    def unfuse(eng):
        eng.sem_inc(s_nop, 1)

    def open_events(eng, name):
        for e in engines.get(name, []):
            e.open(eng)

    x_in = a["u"].rearrange("(t p) d -> p t d", p=P)
    x_out = out.rearrange("(t p) d -> p t d", p=P)

    @block.sync
    def _(eng):
        open_events(eng, "sync")
        eng.dma_start(X[:, :, :], x_in).then_inc(s_x, 16)
        eng.dma_start(w_r0[:, :, 0:E], a["gate0"].rearrange("(k p) n -> p k n", p=P)).then_inc(s_w_r0, 16)
        eng.dma_start(w_r0[:, :, E:E + MH], a["w_dt"].rearrange("(k p) n -> p k n", p=P)).then_inc(s_w_r0, 16)
        eng.dma_start(dt_bias[:, :], a["dt_bias"].partition_broadcast(P)).then_inc(s_small, 16)
        eng.dma_start(a_neg[:, :], a["A_log"].partition_broadcast(P)).then_inc(s_small, 16)
        eng.dma_start(conv_w[:, :, :], a["conv_w"]).then_inc(s_small, 16)
        eng.dma_start(conv_b[:, :], a["conv_b"]).then_inc(s_small, 16)
        for q in range(2):
            eng.dma_start(d_par[q * MP:(q + 1) * MP, :], a["D_param"][q, :].partition_broadcast(MP)).then_inc(s_small, 16)
        eng.dma_start(w_in[:, :, :], a["w_in"].rearrange("(k p) n -> p k n", p=P)).then_inc(s_w_in, 16)
        eng.dma_start(w_out[:, :, :], a["w_out"].rearrange("(k p) n -> p k n", p=P)).then_inc(s_w_out, 16)
        eng.dma_start(sh_gu[:, :, :], a["sh_gu0"].rearrange("(k p) n -> p k n", p=P)).then_inc(s_sh0, 16)
        eng.dma_start(sh_dn[:, :, :], a["sh_dn0"].rearrange("(c p) n -> p c n", p=P)).then_inc(s_sh0, 16)
        eng.wait_ge(s_cmask, 3)
        for l in range(2):
            eng.dma_start(lists[l].rearrange("(p j) o -> p (j o)", p=P), zero_i[:, :]).then_inc(s_zero, 16)
        for e in range(E):
            eng.dma_start(wgu0[:, e, :, :], a["gu0"][e].rearrange("(k p) n -> p k n", p=P)).then_inc(s_wgu0, 16)

        def store_xn(l):
            def body(r):
                N[l]["xn"].wait(eng, r.n)
                rows = xn_rows[l].rearrange("(t p) d -> p t d", p=P)
                N[l]["stored"][r.u].mark(eng.dma_start(rows[:, bass.ds(r.n * CH, CH), :], XN[r.u][:, :, :]))
            rounds(eng, NSEQ, body)

        def lists_back(l):
            for u in range(2):
                s_scat[l][u].wait(eng, NT // 2 - 1)
            eng.dma_start(slot_tok[:, :], lists[l].rearrange("(p j) o -> p (j o)", p=P)).then_inc(s_slots, 16)

        def store_y(l):
            def body(r):
                EX[l]["yo"].wait(eng, r.n)
                rows = y_rows[l].rearrange("(j p) d -> p j d", p=P)
                EX[l]["out"][r.u].mark(eng.dma_start(rows[:, bass.ds(r.n, 1), :], YO[r.u].unsqueeze(1)))
            rounds(eng, NJ, body)

        store_xn(0)
        M["add"].wait(eng, NSEQ - 1)
        for e in range(E):
            eng.dma_start(wdn0[:, e, :, :], a["dn0"][e].rearrange("(c p) n -> p c n", p=P)).then_inc(s_wdn0, 16)
        lists_back(0)
        store_y(0)
        EX[0]["u"].wait(eng, NJ - 1)
        eng.dma_start(w_r1, a["gate1"].rearrange("(k p) n -> p k n", p=P)).then_inc(s_l1a, 16)
        eng.dma_start(w_qkv, a["qkv"].rearrange("(k p) n -> p k n", p=P)).then_inc(s_l1a, 16)
        eng.dma_start(w_o, a["w_o"].rearrange("(k p) n -> p k n", p=P)).then_inc(s_l1a, 16)
        eng.dma_start(sh_gu1[:, :, 0:I1S], a["sg1"].rearrange("(k p) n -> p k n", p=P)).then_inc(s_l1b, 16)
        eng.dma_start(sh_gu1[:, :, I1S:2 * I1S], a["su1"].rearrange("(k p) n -> p k n", p=P)).then_inc(s_l1b, 16)
        eng.dma_start(sh_dn1, a["sd1"].rearrange("(c p) n -> p c n", p=P)).then_inc(s_l1b, 16)
        for e in range(E):
            eng.dma_start(wgu1[:, e, :, 0:I1], a["wg1"][e].rearrange("(k p) n -> p k n", p=P)).then_inc(s_l1b, 16)
            eng.dma_start(wgu1[:, e, :, I1:2 * I1], a["wu1"][e].rearrange("(k p) n -> p k n", p=P)).then_inc(s_l1b, 16)
        eng.dma_start(wdn1, a["wd1"].rearrange("e p n -> p e n")).then_inc(s_l1b, 16)
        store_xn(1)
        lists_back(1)
        store_y(1)

        def store_out(r):
            FC.wait(eng, r.n)
            FO[r.u].mark(eng.dma_start(x_out[:, bass.ds(r.n, 1), :], X[:, bass.ds(r.n, 1), :]))
        rounds(eng, NT, store_out)
        for u in range(2):
            FO[u].wait(eng, NT // 2 - 1)

    @block.gpsimd
    def _(eng):
        open_events(eng, "gpsimd")
        eng.memset(zero_i[:, :], 0).then_inc(s_cmask, 1)
        n = 0
        for t, v in ((ident, 0.0), (tri_le, 1.0), (tri_gt, 1.0), (ones, 1.0), (quarter_le, 0.25), (ident_b, 0.0),
                     (ones_b, 1.0), (before_b, 1.0), (future_b, 0.0), (minus_half, -0.5)):
            eng.memset(t[:, :], v).then_inc(s_const, 1)
            n += 1
        eng.iota(itmp_e[:, :], [[1, E]], base=0, channel_multiplier=0).then_inc(s_const, 1)
        eng.iota(itmp_j[:, :], [[1, NJ]], base=0, channel_multiplier=0).then_inc(s_const, 1)
        eng.iota(token_id[:, :], [[P, NT]], base=0, channel_multiplier=1).then_inc(s_const, 1)
        eng.iota(par_i[:, 0:1], [[0, 1]], base=0, channel_multiplier=1).then_inc(s_const, 1)
        n += 4
        eng.wait_ge(s_const, n)
        sel = eng.affine_select
        for t, op, fill, sign in ((ident, ALU.not_equal, 1.0, -1), (ident_b, ALU.not_equal, 1.0, -1)):
            sel(out=t[:, :], in_=t[:, :], compare_op=op, fill=fill, base=0, pattern=[[-1, P]],
                channel_multiplier=1).then_inc(s_const, 1)
        sel(out=tri_le[:, :], in_=tri_le[:, :], compare_op=ALU.is_ge, fill=0.0, base=0, pattern=[[1, P]],
            channel_multiplier=-1).then_inc(s_const, 1)
        sel(out=quarter_le[:, :], in_=quarter_le[:, :], compare_op=ALU.is_ge, fill=0.0, base=0, pattern=[[1, P]],
            channel_multiplier=-1).then_inc(s_const, 1)
        sel(out=tri_gt[:, :], in_=tri_gt[:, :], compare_op=ALU.is_gt, fill=0.0, base=0, pattern=[[-1, P]],
            channel_multiplier=1).then_inc(s_const, 1)
        sel(out=before_b[:, :], in_=before_b[:, :], compare_op=ALU.is_gt, fill=0.0, base=0, pattern=[[1, P]],
            channel_multiplier=-1).then_inc(s_const, 1)
        sel(out=future_b[:, :], in_=future_b[:, :], compare_op=ALU.is_ge, fill=-BIG, base=0, pattern=[[-1, P]],
            channel_multiplier=1).then_inc(s_const, 1)
        eng.tensor_copy(iota_e[:, :], itmp_e[:, :]).then_inc(s_const, 1)
        eng.tensor_copy(iota_j[:, :], itmp_j[:, :]).then_inc(s_const, 1)
        n += 9
        eng.wait_ge(s_const, n)
        eng.sem_inc(s_cmask, 2)

        def norm_stage(l, r):
            ne = N[l]
            ne["var"].wait(eng, r.n)
            ne["rstd"].mark(eng.tensor_tensor(rstd[:, :], rstd[:, :], minus_half[:, :], ALU.pow))

        def keep_stage(l, r):
            ne = N[l]
            ne["xT"].wait(eng, r.n)
            ne["keep"].mark(eng.tensor_copy(XT[:, :, bass.ds(r.n * SEQ, SEQ)], xT[r.u][:, :, :]))

        def norm_body(l):
            def body(r):
                norm_stage(l, r)
                keep_stage(l, r)
            return body

        rounds(eng, NSEQ, norm_body(0))

        eng.wait_ge(s_sp, 4)

        def mamba(r):
            M["dec"].wait(eng, r.n, 1)
            av = DTA[:, bass.ds(r.n * CH, CH), :].rearrange("p c h -> p (c h)")
            M["mh"].mark(eng.tensor_tensor(
                MHm.rearrange("p c h t -> p (c h) t"),
                tri_le[:, :].unsqueeze(1).broadcast_to([P, CH * MH, P]),
                av.unsqueeze(2).broadcast_to([P, CH * MH, P]), ALU.mult))
        rounds(eng, NSEQ, mamba)

        def scatter(l):
            eng.wait_ge(s_placed, l + 1)
            eng.wait_ge(s_zero, 32)

            def body(r):
                for k in range(TOPK):
                    c = 2 * r.u + k
                    eng.tensor_copy(ring_idx[:, c:c + 1], dest_i[k][:, bass.ds(r.n, 1)])
                    eng.tensor_copy(ring_tok[:, c:c + 1], token_id[:, bass.ds(r.n, 1)]).then_inc(s_sidx[l].sem, 1)
                s_sidx[l].wait(eng, r.n)
                unfuse(eng)
                for k in range(TOPK):
                    c = 2 * r.u + k
                    eng.indirect_dma_start(lists[l], bass.IndirectOffsetOnAxis(ring_idx[:, c:c + 1], 0),
                                           ring_tok[:, c:c + 1], None).then_inc(s_scat[l][r.u].sem, 16)
                if r.u == 1:
                    for u in range(2):
                        s_scat[l][u].wait(eng, r.i)
            rounds(eng, NT, body)

        def gather_tiles(l):
            x = EX[l]
            eng.wait_ge(s_slots, 16 * (l + 1))
            for u in range(2):
                N[l]["stored"][u].wait(eng, NSEQ // 2 - 1)

            def body(r):
                c = r.u
                x["xt"].wait(eng, r.n, 2)
                x["idx"].mark(eng.tensor_copy(ring_idx[:, c:c + 1], slot_tok[:, bass.ds(r.n, 1)]))
                x["idx"].wait(eng, r.n)
                unfuse(eng)
                x["got"][r.u].mark(eng.indirect_dma_start(
                    XG[r.u], None, xn_rows[l], bass.IndirectOffsetOnAxis(ring_idx[:, c:c + 1], 0)))
            rounds(eng, NJ, body)

        scatter(0)
        gather_tiles(0)

        for u in range(2):
            EX[0]["out"][u].wait(eng, NJ // 2 - 1)

        def fetch_rows(r):
            A["comb"].wait(eng, r.n, 1)
            for c in range(CH):
                for k in range(TOPK):
                    q = c * TOPK + k
                    ins = eng.tensor_copy(ring_idx[:, q:q + 1], slot_i[k][:, bass.ds(r.n * CH + c, 1)])
            s_aidx.mark(ins)
            s_aidx.wait(eng, r.n)
            unfuse(eng)
            for c in range(CH):
                for k in range(TOPK):
                    q = c * TOPK + k
                    A["y"][q].mark(eng.indirect_dma_start(
                        (Y1, Y2)[k][:, c, :], None, y_rows[0],
                        bass.IndirectOffsetOnAxis(ring_idx[:, q:q + 1], 0)))
        EX[0]["dn"].wait(eng, NJ - 1)

        def attention(r):
            fetch_rows(r)
            norm_stage(1, r)
            keep_stage(1, r)
        rounds(eng, NSEQ, attention)
        scatter(1)
        gather_tiles(1)
        for u in range(2):
            EX[1]["out"][u].wait(eng, NJ // 2 - 1)

        def final(r):
            FC.wait(eng, r.n, 2)
            for k in range(TOPK):
                q = 2 * r.u + k
                ins = eng.tensor_copy(ring_idx[:, q:q + 1], slot_i[k][:, bass.ds(r.n, 1)])
            FI.mark(ins)
            FI.wait(eng, r.n)
            unfuse(eng)
            for k in range(TOPK):
                q = 2 * r.u + k
                FY[q].mark(eng.indirect_dma_start(
                    (Y1, Y2)[k][:, r.u, :], None, y_rows[1],
                    bass.IndirectOffsetOnAxis(ring_idx[:, q:q + 1], 0)))
        rounds(eng, NT, final)

    @block.scalar
    def _(eng):
        open_events(eng, "scalar")
        act = eng.activation

        def norm_stage(l, r):
            ne = N[l]
            ne["tr"].wait(eng, r.n)
            ne["lg"].wait(eng, r.n, 2)
            ne["keep"].wait(eng, r.n, 2)
            ne["xT"].mark(act(xT[r.u][:, :, :], bank[0][:, :].rearrange("p (k t) -> p k t", k=KD), ACT.Copy))

        eng.wait_ge(s_small, 96)
        act(a_neg[:, :], a_neg[:, :], ACT.Exp).then_inc(s_prep, 1)
        rounds(eng, NSEQ, lambda r: norm_stage(0, r))
        eng.wait_ge(s_sp, 2)
        flat = DTE[:, :, :].rearrange("p t h -> p (t h)")
        act(flat, flat, ACT.Exp).then_inc(s_spa, 1)
        eng.wait_ge(s_spa, 1)
        act(flat, flat, ACT.Ln, bias=1.0).then_inc(s_spa, 1)
        def exp2(l):
            eng.wait_ge(s_m21, l + 1)
            act(rs[:, 5, :], rs[:, 4, :], ACT.Exp).then_inc(s_exp2, 1)
        exp2(0)

        def mamba(r):
            M["proj"].wait(eng, r.n)
            M["cv"].wait(eng, r.n, 1)
            M["xs"].wait(eng, r.n, 1)
            M["ct"].wait(eng, r.n, 1)
            for c in range(3):
                src = bank[2][:, c * SEQ:(c + 1) * SEQ] if c < 2 else bank[3][:, 0:SEQ]
                ins = act(CV[:, c, :], src, ACT.Identity, bias=conv_b[:, c:c + 1], scale=conv_w[:, c, TAPS - 1:TAPS])
            M["cv0"].mark(ins)
            M["sz"].wait(eng, r.n, 1)
            M["zt"].mark(act(ZT.rearrange("p k t -> p (k t)"), bank[1][:, :], ACT.Tanh, scale=0.5))
            M["dec"].wait(eng, r.n)
            M["wm"].wait(eng, r.n, 1)
            M["xw"].wait(eng, r.n, 1)
            for c in range(CH):
                act(ED[:, c, :, :].rearrange("p h t -> p (h t)"), bank[4 + c][:, :], ACT.Exp)
            M["ce"].wait(eng, r.n, 1)
            M["y"].wait(eng, r.n, 1)
            M["ed"].mark(act(CE.rearrange("p h t -> p (h t)"), bank[6][0:MS, :], ACT.Exp))
            M["cv"].wait(eng, r.n)
            M["th"].mark(act(TH.rearrange("p c t -> p (c t)"), CV.rearrange("p c t -> p (c t)"), ACT.Tanh, scale=0.5))
            M["gtr"].wait(eng, r.n)
            M["gm"].wait(eng, r.n)
            M["st"].wait(eng, r.n, 1)
            M["bs"].mark(act(BS, bank[5][:, SEQ:SEQ + MS], ACT.Copy, scale=0.5))
            M["st"].wait(eng, r.n)
            M["y"].wait(eng, r.n, 1)
            M["ss"].mark(act(SS[0:MS, :], bank[6][0:MS, 0:MH * MP], ACT.Copy, scale=0.5))
        rounds(eng, NSEQ, mamba)

        def ffn(l):
            f, ni = FF[l], FF[l]["ni"]

            def body(r):
                for i in range(ni):
                    n = r.n * ni + i
                    f["gu"].wait(eng, n)
                    f["ht"].wait(eng, n, 2)
                    f["sg"].mark(act(SG[i % 2][:, :], bank[i][:, 0:SEQ], ACT.Silu))
            rounds(eng, NSEQ, body)
        ffn(0)

        def experts(l):
            x = EX[l]

            def xt_copy(r):
                x["xt"].wait(eng, r.n)
                x["h"].wait(eng, r.n, 2)
                x["xtc"].mark(act(XGT[r.u], bank[4][:, 0:KD * P].rearrange("p (k t) -> p k t", k=KD), ACT.Copy))

            def silu(r):
                x["g"].wait(eng, r.n)
                x["h"].wait(eng, r.n, 1)
                w = I0 if l == 0 else I1
                x["sg"].mark(act(SE[:, 0:w], bank[r.u][:, 0:w], ACT.Silu))

            def y_copy(r):
                x["dn"].wait(eng, r.n)
                x["out"][r.u].wait(eng, r.i, 1)
                x["yo"].mark(act(YO[r.u], bank[6 + r.u][:, 0:D], ACT.Copy))

            def body(new, r, old):
                if r:
                    silu(r)
                if old:
                    y_copy(old)
                if new:
                    xt_copy(new)
            pipelined(eng, NJ, 3, body)
        experts(0)

        def exps(r, g):
            n = r.n * PAIRS + g
            A["nm"].wait(eng, n)
            A["pt"].wait(eng, n, 2)
            if g == 0:
                A["sr"].wait(eng, r.n, 2)
            for h in range(2):
                b = bank[1 + 2 * (g % 2) + h]
                for q, (lo, hi) in enumerate(((0, 1), (1, 3))):
                    ins = act(PR[g % 2][:, h, lo:hi, :].rearrange("p b k -> p (b k)"), b[:, lo * P:hi * P], ACT.Exp,
                              bias=NM[g % 2][:, h, q:q + 1],
                              accum_out=SM[r.u][:, q, 2 * g + h:2 * g + h + 1])
            A["exp"].mark(ins)

        def pt_copy(r, g):
            n = r.n * PAIRS + g
            A["pt"].wait(eng, n)
            A["pv"].wait(eng, n, 2)
            A["ptc1"].mark(act(PT[g % 2][:, 1, :, :], bank[6][:, 0:3 * P].rearrange("p (b k) -> p b k", b=3), ACT.Copy))

        def q_copy(r):
            A["q"].wait(eng, r.n)
            A["on"].wait(eng, r.n, 2)
            A["qc"].mark(act(QT[r.u].rearrange("p k t -> p (k t)"), bank[0][:, :], ACT.Copy))

        def v_copy(r):
            A["v"].wait(eng, r.n)
            A["vc"].mark(act(V[r.u].rearrange("p k t -> p (k t)"), bank[0][:, :], ACT.Copy))

        def o_copy(r):
            A["ot"].wait(eng, r.n)
            A["wo"].wait(eng, r.n, 1)
            A["otc"].mark(act(OT.rearrange("p k t -> p (k t)"), bank[0][:, :], ACT.Copy))

        attention(eng, turns=pt_copy, first=exps, new_pieces={2: lambda r: norm_stage(1, r), 4: q_copy, 5: v_copy},
                  done_pieces={0: o_copy}, turns_before=True)
        exp2(1)
        ffn(1)
        experts(1)

    @block.vector
    def _(eng):
        open_events(eng, "vector")
        tt, ts, stt = eng.tensor_tensor, eng.tensor_scalar, eng.scalar_tensor_tensor

        def norm_stats(l, r):
            ne, ch = N[l], N[l]["chain"]
            ch.start(eng, r.n)
            unfuse(eng)
            for c in range(CH):
                ins = eng.bn_stats(stats[:, c, :], X[:, bass.ds(r.n * CH + c, 1), :].rearrange("p a d -> p (a d)"))
            ch(ins)
            unfuse(eng)
            for c in range(CH):
                ins = eng.bn_aggr(mv[:, c, :], stats[:, c, :])
            ch(ins)
            ch.end()
            ne["var"].mark(ts(rstd[:, :], mv[:, :, 1], EPS, None, ALU.add))

        def norm_apply(l, r):
            ne = N[l]
            ne["rstd"].wait(eng, r.n)
            ne["stored"][r.u].wait(eng, r.i, 1)
            ne["tr"].wait(eng, r.n, 2)
            for c in range(CH):
                ins = ts(XN[r.u][:, c, :], X[:, bass.ds(r.n * CH + c, 1), :].rearrange("p a d -> p (a d)"),
                         mv[:, c, 0:1], rstd[:, c:c + 1], ALU.subtract, ALU.mult)
            ne["xn"].mark(ins)
            ne["xn"].wait(eng, r.n)

        def logits_stage(l, r):
            ne = N[l]
            ne["lg"].wait(eng, r.n)
            b = bank[7] if l == 0 else bank[0]
            w = E + MH if l == 0 else E
            src = b[:, 0:CH * w].rearrange("p (c e) -> p c e", c=CH)
            if l == 0:
                tt(DTR[:, bass.ds(r.n * CH, CH), :], src[:, :, E:E + MH],
                   dt_bias[:, :].unsqueeze(1).broadcast_to([P, CH, MH]), ALU.add)
            ne["lgc"].mark(eng.tensor_copy(LG[:, bass.ds(r.n * CH, CH), :], src[:, :, 0:E]))

        eng.wait_ge(s_x, 16)
        eng.wait_ge(s_small, 96)
        rounds(eng, NSEQ, lambda r: (norm_stats(0, r), norm_apply(0, r), logits_stage(0, r)))

        N[0]["lgc"].wait(eng, NSEQ - 1)
        flat = lambda t: t[:, :, :].rearrange("p t h -> p (t h)")
        stt(flat(DTE), flat(DTR), -1.0, flat(DTR), ALU.mult, ALU.min).then_inc(s_sp, 1)
        eng.wait_ge(s_prep, 1)
        ts(a_neg[:, :], a_neg[:, :], -1.0, None, ALU.mult).then_inc(s_sp, 1)
        eng.wait_ge(s_spa, 2)
        stt(flat(DTR), flat(DTR), 0.0, flat(DTE), ALU.max, ALU.add).then_inc(s_sp, 1)
        eng.wait_ge(s_sp, 3)
        tt(DTA[:, :, :], DTR[:, :, :], a_neg[:, :].unsqueeze(1).broadcast_to([P, NT, MH]), ALU.mult).then_inc(s_sp, 1)
        eng.wait_ge(s_sp, 4)
        ts(flat(DTE), flat(DTR), 0.5, None, ALU.mult).then_inc(s_prep2, 1)
        ts(d_par[:, :], d_par[:, :], 0.5, None, ALU.mult).then_inc(s_prep2, 1)
        eng.wait_ge(s_w_out, 16)
        ts(w_out[:, :, :].rearrange("p k n -> p (k n)"), w_out[:, :, :].rearrange("p k n -> p (k n)"), 0.5, None,
           ALU.mult).then_inc(s_prep2, 1)

        def route(l):
            s, count = s_route, route_count

            def link(ins):
                count[0] += 1
                ins.then_inc(s, 1)
                eng.wait_ge(s, count[0])
            N[l]["lgc"].wait(eng, NSEQ - 1)
            work, masked = rt[0], rt[1]
            bc_e = lambda v: v.unsqueeze(2).broadcast_to([P, NT, E])
            ie = iota_e[:, :].unsqueeze(1).broadcast_to([P, NT, E])
            for k in range(TOPK):
                lg = LG if k == 0 else masked
                link(eng.tensor_reduce(rs[:, k, :], lg[:, :, :], AX.X, ALU.max))
                link(tt(work[:, :, :], lg[:, :, :], bc_e(rs[:, k, :]), ALU.is_lt))
                link(stt(work[:, :, :], work[:, :, :], float(E), ie, ALU.mult, ALU.add))
                link(eng.tensor_reduce(rs[:, 2, :], work[:, :, :], AX.X, ALU.min))
                link(tt(OH[k], ie, bc_e(rs[:, 2, :]), ALU.is_equal))
                if k == 0:
                    link(stt(masked[:, :, :], OH[0], -3.0e38, LG[:, :, :], ALU.mult, ALU.add))
            tt(rs[:, 4, :], rs[:, 1, :], rs[:, 0, :], ALU.subtract).then_inc(s_m21, 1)
            link(tt(work[:, :, :], OH[0], OH[1], ALU.add))
            eng.tensor_copy(hot_b[:, :, :], work[:, :, :]).then_inc(s_hot, 1)
            eng.wait_ge(s_exp2, l + 1)
            link(ts(rs[:, 6, :], rs[:, 5, :], 1.0, None, ALU.add))
            link(eng.reciprocal(cw[0][:, :], rs[:, 6, :]))
            link(tt(cw[1][:, :], rs[:, 5, :], cw[0][:, :], ALU.mult))
            eng.wait_ge(s_rank, l + 1)
            within = bank[6][:, 0:NT * E].rearrange("p (t e) -> p t e", e=E)
            total = bank[7][:, 0:NT * E].rearrange("p (t e) -> p t e", e=E)
            link(eng.tensor_copy(rt[1][:, :, :], total))
            src, dst = rt[1], rt[2]
            step = 1
            while step < NT:
                eng.tensor_copy(dst[:, 0:step, :], src[:, 0:step, :])
                link(tt(dst[:, step:NT, :], src[:, step:NT, :], src[:, 0:NT - step, :], ALU.add))
                src, dst, step = dst, src, step * 2
            link(ts(ex_i[:, :], src[:, NT - 1, :], float(P - 1), None, ALU.add))
            link(ts(ex_i[:, :], ex_i[:, :], 7, None, ALU.arith_shift_right))
            link(eng.tensor_copy(ex[:, 0, :], ex_i[:, :]))
            a_, b_, step = 0, 1, 1
            while step < E:
                eng.tensor_copy(ex[:, b_, 0:step], ex[:, a_, 0:step])
                link(tt(ex[:, b_, step:E], ex[:, a_, step:E], ex[:, a_, 0:E - step], ALU.add))
                a_, b_, step = b_, (b_ + 1 if b_ < 3 else 3), step * 2
            ends = ex[:, a_, :]
            eng.memset(ex[:, 5, 0:1], 0.0)
            link(ts(ex[:, 5, 1:E], ex[:, a_, 0:E - 1], float(P), None, ALU.mult))
            link(tt(dst[:, :, :], src[:, :, :], total, ALU.subtract))
            link(tt(dst[:, :, :], dst[:, :, :], within, ALU.add))
            link(tt(dst[:, :, :], dst[:, :, :], ex[:, 5, :].unsqueeze(1).broadcast_to([P, NT, E]), ALU.add))
            for k in range(TOPK):
                link(tt(work[:, :, :], dst[:, :, :], OH[k], ALU.mult))
                link(eng.tensor_reduce(rs[:, 7, :], work[:, :, :], AX.X, ALU.add))
                link(eng.tensor_copy(slot_i[k][:, :], rs[:, 7, :]))
                link(ts(dtmp_i[:, :], slot_i[k][:, :], P - 1, None, ALU.bitwise_and))
                link(ts(dest_i[k][:, :], slot_i[k][:, :], 7, None, ALU.arith_shift_right))
                link(stt(dest_i[k][:, :], dtmp_i[:, :], float(NJ), dest_i[k][:, :], ALU.mult, ALU.add))
            link(tt(tile_cmp[:, :, 0:E - 1], iota_j[:, :].unsqueeze(2).broadcast_to([P, NJ, E - 1]),
                    ends[:, 0:E - 1].unsqueeze(1).broadcast_to([P, NJ, E - 1]), ALU.is_ge))
            link(eng.tensor_reduce(tile_e[:, :], tile_cmp[:, :, 0:E - 1], AX.X, ALU.add))
            link(eng.tensor_copy(tile_expert[:, :], tile_e[:, :]))
            eng.wait_ge(s, count[0])
            eng.drain().then_inc(s_placed, 1)
        eng.wait_ge(s_cmask, 3)
        route(0)

        def mamba(r):
            ch = M["chain"]
            ch.start(eng, r.n)
            c0 = r.n * CH
            M["cv0"].wait(eng, r.n)
            for k in range(1, TAPS):
                for c in range(3):
                    src = bank[2][:, c * SEQ:(c + 1) * SEQ] if c < 2 else bank[3][:, 0:SEQ]
                    ins = stt(CV[:, c, k:SEQ], src[:, 0:SEQ - k], conv_w[:, c, TAPS - 1 - k:TAPS - k], CV[:, c, k:SEQ],
                              ALU.mult, ALU.add)
                if k < TAPS - 1:
                    ch(ins)
            M["cv"].mark(ins)
            M["zt"].wait(eng, r.n)
            M["yg"].wait(eng, r.n, 1)
            M["sz"].mark(stt(SZ.rearrange("p k t -> p (k t)"), ZT.rearrange("p k t -> p (k t)"), 1.0, bank[1][:, :],
                             ALU.add, ALU.mult))
            M["th"].wait(eng, r.n)
            M["y"].wait(eng, r.n, 1)
            stt(BT[0:MS, :], TH[0:MS, 2, :], 1.0, CV[0:MS, 2, :], ALU.add, ALU.mult)
            M["ct"].mark(stt(CT[0:MS, :], TH[MS:P, 2, :], 1.0, CV[MS:P, 2, :], ALU.add, ALU.mult))
            M["xs"].mark(stt(XS.rearrange("p k t -> p (k t)"), TH[:, 0:2, :].rearrange("p k t -> p (k t)"), 1.0,
                             CV[:, 0:2, :].rearrange("p k t -> p (k t)"), ALU.add, ALU.mult))
            M["ed"].wait(eng, r.n)
            M["ct"].wait(eng, r.n)
            M["ce"].mark(tt(CE, CE, CT[0:MS, P:SEQ].unsqueeze(1).broadcast_to([MS, MH, P]), ALU.mult))
            M["gtr"].wait(eng, r.n)
            M["gm"].mark(tt(GM, bank[5][:, 0:SEQ].rearrange("p (c t) -> p c t", c=CH),
                            quarter_le[:, :].unsqueeze(1).broadcast_to([P, CH, P]), ALU.mult))
            M["gm"].wait(eng, r.n)
            M["y"].wait(eng, r.n, 1)
            for c in range(CH):
                ins = tt(WM[:, c, :, :], ED[:, c, :, :], GM[:, c, :].unsqueeze(1).broadcast_to([P, MH, P]), ALU.mult)
            M["wm"].mark(ins)
            M["xtr"].wait(eng, r.n)
            dts = DTE[:, bass.ds(c0, CH), :].rearrange("p c h -> p (c h)")
            M["xd"].mark(tt(XD.rearrange("p c h d -> p (c h) d"), bank[4][:, :].rearrange("p (g d) -> p g d", d=MP),
                            dts.unsqueeze(2).broadcast_to([P, CH * MH, MP]), ALU.mult))
            M["xd"].wait(eng, r.n)
            M["xw"].mark(tt(XW, XD[:, 0, :, :], ED[:, 0, :, P - 1:P].broadcast_to([P, MH, MP]), ALU.mult))
            M["y"].wait(eng, r.n)
            M["o"].wait(eng, r.n, 1)
            for j in range(KD):
                ins = stt(YG[:, j, :], XS[:, j, :], d_par[:, j:j + 1], bank[7][:, j * SEQ:(j + 1) * SEQ],
                          ALU.mult, ALU.add)
            ch(ins)
            M["yg"].mark(tt(YG.rearrange("p k t -> p (k t)"), YG.rearrange("p k t -> p (k t)"), SZ.rearrange("p k t -> p (k t)"),
                  ALU.mult))
            M["o"].wait(eng, r.n)
            xs = X[:, bass.ds(c0, CH), :].rearrange("p c d -> p (c d)")
            M["add"].mark(tt(xs, xs, bank[4][:, :], ALU.add))
            ch.end()
        eng.wait_ge(s_prep2, 3)
        rounds(eng, NSEQ, mamba)

        def ffn(l):
            f, ni = FF[l], FF[l]["ni"]

            def body(r):
                for i in range(ni):
                    n = r.n * ni + i
                    f["sg"].wait(eng, n)
                    if i == 0:
                        f["dn"].wait(eng, r.n, 2)
                    f["ht"].mark(tt(HTt[r.u][:, i, :], SG[i % 2][:, :], bank[i][:, SEQ:2 * SEQ], ALU.mult))

            def add(r):
                f["dn"].wait(eng, r.n)
                xs = X[:, bass.ds(r.n * CH, CH), :].rearrange("p c d -> p (c d)")
                f["add"].mark(tt(xs, xs, bank[4 + r.u][:, :], ALU.add))

            def both(new, old):
                if new:
                    body(new)
                if old:
                    add(old)
            pipelined(eng, NSEQ, 2, both)
        M["add"].wait(eng, NSEQ - 1)
        ffn(0)

        def experts(l):
            x = EX[l]

            def h_stage(r):
                x["sg"].wait(eng, r.n)
                if l == 0:
                    x["u"].wait(eng, r.n)
                x["ht"].wait(eng, r.n, 2)
                if l == 0:
                    up, w = bank[2 + r.u][:, :], I0
                else:
                    up, w = bank[r.u][:, I1:2 * I1], I1
                x["h"].mark(tt(HE[r.u][:, 0:w], SE[:, 0:w], up, ALU.mult))

            def ht_copy(r):
                x["ht"].wait(eng, r.n)
                x["dn"].wait(eng, r.n, 2)
                w = (I0 if l == 0 else I1) // P
                x["htc"].mark(eng.tensor_copy(HET[r.u][:, 0:w, :], bank[5][:, 0:w * P].rearrange("p (c t) -> p c t", c=w)))

            def body(new, r, old):
                if old:
                    ht_copy(old)
                if r:
                    h_stage(r)
            pipelined(eng, NJ, 3, body)
        experts(0)

        FF[0]["add"].wait(eng, NSEQ - 1)

        def combine(r):
            ch = A["cchain"]
            ch.start(eng, r.n)
            for c in range(CH):
                xs = X[:, bass.ds(r.n * CH + c, 1), :].rearrange("p a d -> p (a d)")
                for k in range(TOPK):
                    A["y"][c * TOPK + k].wait(eng, r.n)
                    ins = stt(xs, (Y1, Y2)[k][:, c, :], cw[k][:, bass.ds(r.n * CH + c, 1)], xs, ALU.mult, ALU.add)
                    if k == 0:
                        ch(ins)
            A["comb"].mark(ins)
            A["comb"].wait(eng, r.n)
            ch.end()
            norm_stats(1, r)

        def k_copy(r):
            A["k"].wait(eng, r.n)
            A["on"].wait(eng, r.n, 2)
            for m in range(2):
                ins = ts(KM[r.u][m].rearrange("p k t -> p (k t)"), bank[0][:, :], head_mask[:, m:m + 1], None, ALU.mult)
            A["kc"].mark(ins)

        def maxima(r, g):
            n = r.n * PAIRS + g
            mc = A["mchain"]
            mc.start(eng, n)
            A["s"].wait(eng, n)
            b0 = 1 + 2 * (g % 2)
            A["exp"].wait(eng, n, 2)
            for h in range(2):
                ins = eng.tensor_reduce(MX[g % 2][:, h, :], bank[b0 + h][:, 0:3 * P].rearrange("p (b k) -> p b k", b=3),
                                        AX.X, ALU.max)
            mc(ins)
            mc(tt(MX[g % 2][:, :, 1], MX[g % 2][:, :, 1], MX[g % 2][:, :, 2], ALU.max))
            A["nm"].mark(ts(NM[g % 2], MX[g % 2][:, :, 0:2], -1.0, None, ALU.mult))
            mc.end()

        def pt_copy(r, g):
            n = r.n * PAIRS + g
            A["pt"].wait(eng, n)
            A["pv"].wait(eng, n, 2)
            A["ptc0"].mark(eng.tensor_copy(PT[g % 2][:, 0, :, :], bank[5][:, 0:3 * P].rearrange("p (b k) -> p b k", b=3)))

        def normalise(r):
            A["exp"].wait(eng, (r.n + 1) * PAIRS - 1)
            A["sr"].mark(eng.reciprocal(SR.rearrange("p c h -> p (c h)"), SM[r.u].rearrange("p c h -> p (c h)")))
            A["sr"].wait(eng, r.n)
            A["pv"].wait(eng, (r.n + 1) * PAIRS - 1)
            A["ot"].wait(eng, r.n, 1)
            A["on"].mark(tt(ON.rearrange("p c h d -> p (c h) d"), bank[7][:, :].rearrange("p (g d) -> p g d", d=DH),
                            SR.rearrange("p c h -> p (c h)").unsqueeze(2).broadcast_to([P, CH * AH, DH]), ALU.mult))

        def add_out(r):
            A["wo"].wait(eng, r.n)
            xs = X[:, bass.ds(r.n * CH, CH), :].rearrange("p c d -> p (c d)")
            A["add"].mark(tt(xs, xs, bank[0][:, :], ALU.add))
        ts(par_i[:, 1:2], par_i[:, 0:1], DH, None, ALU.bitwise_and).then_inc(s_hmask, 1)
        eng.wait_ge(s_hmask, 1)
        eng.tensor_copy(head_mask[:, 1:2], par_i[:, 1:2]).then_inc(s_hmask, 1)
        eng.wait_ge(s_hmask, 2)
        sc = DH ** -0.5
        ts(head_mask[:, 0:1], head_mask[:, 1:2], -sc / DH, sc, ALU.mult, ALU.add).then_inc(s_hmask, 1)
        eng.wait_ge(s_hmask, 3)
        ts(head_mask[:, 1:2], head_mask[:, 1:2], sc / DH, None, ALU.mult).then_inc(s_hmask, 1)
        eng.wait_ge(s_hmask, 4)
        EX[0]["dn"].wait(eng, NJ - 1)
        attention(eng, turns=pt_copy, first=maxima, old_pieces={1: normalise}, done_pieces={1: add_out},
                  new_pieces={0: combine, 1: lambda r: norm_apply(1, r), 3: lambda r: logits_stage(1, r), 6: k_copy})
        route(1)
        A["add"].wait(eng, NSEQ - 1)
        ffn(1)
        experts(1)
        FF[1]["add"].wait(eng, NSEQ - 1)

        def final(r):
            xs = X[:, bass.ds(r.n, 1), :].rearrange("p a d -> p (a d)")
            FCH.start(eng, r.n)
            for k in range(TOPK):
                FY[2 * r.u + k].wait(eng, r.i)
                ins = stt(xs, (Y1, Y2)[k][:, r.u, :], cw[k][:, bass.ds(r.n, 1)], xs, ALU.mult, ALU.add)
                FCH(ins) if k == 0 else FC.mark(ins)
            FCH.end()
        rounds(eng, NT, final)

    @block.tensor
    def _(eng):
        open_events(eng, "tensor")
        eng.wait_ge(s_cmask, 3)

        def mm(o, l, r, start, stop):
            return eng.matmul(o, l, r, start=start, stop=stop)

        def norm_stage(l, r):
            ne = N[l]
            ne["xn"].wait(eng, r.n)
            ne["xT"].wait(eng, r.n, 1)
            if l == 1:
                A["add"].wait(eng, r.n, 3)
            for c in range(CH):
                for k in range(KD):
                    ins = eng.transpose(bank[0][:, k * SEQ + c * P:k * SEQ + (c + 1) * P],
                                        XN[r.u][:, c, k * P:(k + 1) * P], ident[:, :])
            ne["tr"].mark(ins)

        def logits_stage(l, r):
            ne = N[l]
            ne["xT"].wait(eng, r.n)
            ne["lgc"].wait(eng, r.n, 1)
            w, b = (w_r0, bank[7]) if l == 0 else (w_r1, bank[0])
            n = E + MH if l == 0 else E
            for c in range(CH):
                for k in range(KD):
                    ins = mm(b[:, c * n:(c + 1) * n], xT[r.u][:, k, c * P:(c + 1) * P], w[:, k, :], k == 0, k == KD - 1)
            ne["lg"].mark(ins)

        eng.wait_ge(s_w_r0, 32)
        rounds(eng, NSEQ, lambda r: (norm_stage(0, r), logits_stage(0, r)))

        def rank(l):
            N[l]["lgc"].wait(eng, NSEQ - 1)
            eng.wait_ge(s_hot, l + 1)
            hot = hot_b[:, :, :].rearrange("p t e -> p (t e)")
            mm(bank[6][:, 0:NT * E], before_b[:, :], hot, True, True)
            mm(bank[7][:, 0:NT * E], ones_b[:, :], hot, True, True).then_inc(s_rank, 1)
        rank(0)

        def mamba(r):
            tok = bass.ds(r.n * SEQ, SEQ)
            M["sz"].wait(eng, r.n, 1)
            M["cv"].wait(eng, r.n, 1)
            for m in range(5):
                b, at = (bank[1], m * SEQ) if m < 2 else (bank[2], (m - 2) * SEQ) if m < 4 else (bank[3], 0)
                for k in range(KD):
                    ins = mm(b[:, at:at + SEQ], w_in[:, k, m * P:(m + 1) * P], XT[:, k, tok], k == 0, k == KD - 1)
            M["proj"].mark(ins)
            M["mh"].wait(eng, r.n)
            M["add"].wait(eng, r.n, 1)
            M["bs"].wait(eng, r.n, 1)
            M["ss"].wait(eng, r.n, 1)
            for c in range(CH):
                mm(bank[4 + c][:, :], tri_gt[:, :], MHm[:, c, :, :].rearrange("p h t -> p (h t)"), True, True)
            M["dec"].mark(mm(bank[6][0:MS, :], ones[:, :], MHm[:, 1, :, :].rearrange("p h t -> p (h t)"), True, True))
            M["ct"].wait(eng, r.n)
            M["ed"].wait(eng, r.n)
            for c in range(CH):
                mm(bank[5][:, c * P:(c + 1) * P], BT[0:MS, c * P:(c + 1) * P], CT[0:MS, c * P:(c + 1) * P], True, True)
            M["gtr"].mark(eng.transpose(bank[5][:, SEQ:SEQ + MS], BT[0:MS, 0:P], ident[0:MS, 0:MS]))
            M["xs"].wait(eng, r.n)
            for c in range(CH):
                for k in range(KD):
                    ins = eng.transpose(bank[4][:, c * D + k * P:c * D + (k + 1) * P], XS[:, k, c * P:(c + 1) * P],
                                        ident[:, :])
            M["xtr"].mark(ins)
            M["xw"].wait(eng, r.n)
            M["bs"].wait(eng, r.n)
            M["st"].mark(mm(bank[6][0:MS, 0:MH * MP], BS, XW.rearrange("p h d -> p (h d)"), True, True))
            M["wm"].wait(eng, r.n)
            M["yg"].wait(eng, r.n, 1)
            M["ss"].wait(eng, r.n)
            M["ce"].wait(eng, r.n)
            for h in range(MH):
                j, q = h // 2, h % 2
                for c in range(CH):
                    o = bank[7][q * MP:(q + 1) * MP, j * SEQ + c * P:j * SEQ + (c + 1) * P]
                    ins = mm(o, XD[:, c, h, :], WM[:, c, h, :], True, c == 0)
                    if c == 1:
                        ins = mm(o, SS[0:MS, h * MP:(h + 1) * MP], CE[:, h, :], False, True)
            M["y"].mark(ins)
            M["yg"].wait(eng, r.n)
            M["xd"].wait(eng, r.n)
            for c in range(CH):
                for k in range(KD):
                    ins = mm(bank[4][:, c * D:(c + 1) * D], YG[:, k, c * P:(c + 1) * P], w_out[:, k, :], k == 0, k == KD - 1)
            M["o"].mark(ins)
        N[0]["keep"].wait(eng, NSEQ - 1)
        eng.wait_ge(s_w_in, 16)
        eng.wait_ge(s_prep2, 3)
        eng.wait_ge(s_placed, 1)
        rounds(eng, NSEQ, mamba)

        def ffn(l):
            f, ni = FF[l], FF[l]["ni"]
            gu, dn = (sh_gu, sh_dn) if l == 0 else (sh_gu1, sh_dn1)

            def body(r):
                tok = bass.ds(r.n * SEQ, SEQ)
                for i in range(ni):
                    n = r.n * ni + i
                    f["ht"].wait(eng, n, ni)
                    for half in range(2):
                        for k in range(KD):
                            at = half * ni * P + i * P
                            ins = mm(bank[i][:, half * SEQ:(half + 1) * SEQ], gu[:, k, at:at + P], XT[:, k, tok],
                                     k == 0, k == KD - 1)
                    f["gu"].mark(ins)

            def down(r):
                f["ht"].wait(eng, (r.n + 1) * ni - 1)
                f["add"].wait(eng, r.n, 2)
                for c in range(CH):
                    for i in range(ni):
                        ins = mm(bank[4 + r.u][:, c * D:(c + 1) * D], HTt[r.u][:, i, c * P:(c + 1) * P], dn[:, i, :],
                                 i == 0, i == ni - 1)
                f["dn"].mark(ins)

            def both(new, old):
                if new:
                    body(new)
                if old:
                    down(old)
            pipelined(eng, NSEQ, 2, both)
        M["add"].wait(eng, NSEQ - 1)
        eng.wait_ge(s_sh0, 32)
        ffn(0)

        def experts(l):
            x = EX[l]

            def xt(r):
                x["got"][r.u].wait(eng, r.i)
                x["xtc"].wait(eng, r.n, 1)
                for k in range(KD):
                    ins = eng.transpose(bank[4][:, k * P:(k + 1) * P], XG[r.u][:, k * P:(k + 1) * P], ident[:, :])
                x["xt"].mark(ins)

            def expert_of(r):
                unfuse(eng)
                return eng.value_load(tile_expert[0:1, bass.ds(r.n, 1)], min_val=0, max_val=E - 1)

            def gate(r):
                x["xtc"].wait(eng, r.n)
                x["h"].wait(eng, r.n, 2)
                e = expert_of(r)
                for k in range(KD):
                    rhs = wgu0[:, bass.ds(e, 1), k, 0:I0] if l == 0 else wgu1[:, bass.ds(e, 1), k, :]
                    w = I0 if l == 0 else 2 * I1
                    ins = mm(bank[r.u][:, 0:w], XGT[r.u][:, k, :], rhs, k == 0, k == KD - 1)
                x["g"].mark(ins)
                return e

            def up(r, e):
                for k in range(KD):
                    ins = mm(bank[2 + r.u][:, :], XGT[r.u][:, k, :], wgu0[:, bass.ds(e, 1), k, I0:2 * I0], k == 0, k == KD - 1)
                x["u"].mark(ins)

            def turn_h(r):
                w = (I0 if l == 0 else I1) // P
                x["h"].wait(eng, r.n)
                x["htc"].wait(eng, r.n, 1)
                for c in range(w):
                    ins = eng.transpose(bank[5][:, c * P:(c + 1) * P], HE[r.u][:, c * P:(c + 1) * P], ident[:, :])
                x["ht"].mark(ins)

            def down(r):
                w = (I0 if l == 0 else I1) // P
                x["htc"].wait(eng, r.n)
                x["yo"].wait(eng, r.n, 2)
                e = expert_of(r)
                for c in range(w):
                    rhs = wdn0[:, bass.ds(e, 1), c, :] if l == 0 else wdn1[:, bass.ds(e, 1), :]
                    ins = mm(bank[6 + r.u][:, 0:D], HET[r.u][:, c, :], rhs, c == 0, c == w - 1)
                x["dn"].mark(ins)

            def body(new, r, old):
                if r:
                    e = gate(r)
                if old:
                    turn_h(old)
                if r and l == 0:
                    up(r, e)
                if new and l == 1:
                    xt(new)
                if old:
                    down(old)
                if new and l == 0:
                    xt(new)
            pipelined(eng, NJ, 3, body)
        eng.wait_ge(s_wgu0, 16 * E)
        eng.wait_ge(s_wdn0, 16 * E)
        FF[0]["add"].wait(eng, NSEQ - 1)
        experts(0)

        def queries(r):
            N[1]["lgc"].wait(eng, r.n)
            for m in range(KD):
                for k in range(KD):
                    ins = mm(bank[0][:, m * SEQ:(m + 1) * SEQ], w_qkv[:, k, m * P:(m + 1) * P], xT[r.u][:, k, :], k == 0, k == KD - 1)
            A["q"].mark(ins)

        def values(r):
            A["qc"].wait(eng, r.n)
            for c in range(CH):
                for k in range(KD):
                    ins = mm(bank[0][:, c * D:(c + 1) * D], xT[r.u][:, k, c * P:(c + 1) * P], w_qkv[:, k, 2 * D:3 * D], k == 0, k == KD - 1)
            A["v"].mark(ins)

        def keys(r):
            A["vc"].wait(eng, r.n)
            for m in range(KD):
                for k in range(KD):
                    ins = mm(bank[0][:, m * SEQ:(m + 1) * SEQ], w_qkv[:, k, D + m * P:D + (m + 1) * P], xT[r.u][:, k, :], k == 0, k == KD - 1)
            A["k"].mark(ins)

        def scores(r, g):
            n = r.n * PAIRS + g
            if g == 0:
                A["kc"].wait(eng, r.n)
            A["exp"].wait(eng, n, 2)
            for h in range(2):
                hd = 2 * g + h
                j, row, par = hd * DH // P, hd * DH % P // 32 * 32, hd % 2
                b = bank[1 + 2 * (g % 2) + h]
                for q in range(CH):
                    o = b[:, q * P:q * P + (q + 1) * P]
                    mm(o, QT[r.u][row:row + 32, j, q * P:(q + 1) * P], KM[r.u][par][row:row + 32, j, 0:(q + 1) * P], True, False)
                    ins = mm(b[:, 2 * q * P:(2 * q + 1) * P], ident_b[:, :], future_b[:, :], False, True)
            A["s"].mark(ins)

        def turn_probs(r, g):
            n = r.n * PAIRS + g
            A["exp"].wait(eng, n)
            A["ptc0"].wait(eng, n, 1)
            A["ptc1"].wait(eng, n, 1)
            for h in range(2):
                for b in range(3):
                    ins = eng.transpose(bank[5 + h][:, b * P:(b + 1) * P], PR[g % 2][:, h, b, :], ident[:, :])
            A["pt"].mark(ins)

        def weigh(r, g):
            n = r.n * PAIRS + g
            A["ptc0"].wait(eng, n)
            A["ptc1"].wait(eng, n)
            if g == 0:
                A["on"].wait(eng, r.n, 1)
            for h in range(2):
                hd = 2 * g + h
                for b, (q, t) in enumerate(((0, 0), (1, 0), (1, 1))):
                    o = bank[7][:, q * D + hd * DH:q * D + (hd + 1) * DH]
                    ins = mm(o, PT[g % 2][:, h, b, :], V[r.u][:, t, hd * DH:(hd + 1) * DH], b != 2, b != 1)
            A["pv"].mark(ins)

        def turn_out(r):
            A["on"].wait(eng, r.n)
            A["add"].wait(eng, r.n, 1)
            for c in range(CH):
                for k in range(KD):
                    ins = eng.transpose(bank[0][:, k * SEQ + c * P:k * SEQ + (c + 1) * P],
                                        ON[:, c, k * AH // 2:(k + 1) * AH // 2, :].rearrange("p h d -> p (h d)"), ident[:, :])
            A["ot"].mark(ins)

        def project_out(r):
            A["otc"].wait(eng, r.n)
            for c in range(CH):
                for k in range(KD):
                    ins = mm(bank[0][:, c * D:(c + 1) * D], OT[:, k, c * P:(c + 1) * P], w_o[:, k, :], k == 0, k == KD - 1)
            A["wo"].mark(ins)
        eng.wait_ge(s_l1a, 48)
        attention(eng, first=scores, turns=turn_probs, last=weigh, done_pieces={0: turn_out, 1: project_out},
                  new_pieces={2: lambda r: norm_stage(1, r), 3: lambda r: logits_stage(1, r), 4: queries, 5: values, 6: keys})
        A["add"].wait(eng, NSEQ - 1)
        rank(1)
        eng.wait_ge(s_l1b, 16 * (3 + 2 * E + 1))
        N[1]["keep"].wait(eng, NSEQ - 1)
        ffn(1)
        FF[1]["add"].wait(eng, NSEQ - 1)
        eng.wait_ge(s_placed, 2)
        experts(1)


_NAMES = ["u", "w_in", "w_dt", "conv_w", "conv_b", "w_out", "A_log", "D_param", "dt_bias", "gate0", "gu0", "dn0",
          "sh_gu0", "sh_dn0", "qkv", "w_o", "gate1", "wg1", "wu1", "wd1", "sg1", "su1", "sd1"]


def kernel(L0_attn_u, L0_attn_W_in, L0_attn_conv_w, L0_attn_conv_b, L0_attn_W_out, L0_attn_A_log, L0_attn_D_param,
           L0_attn_dt_bias, L0_ffn_gate_w, L0_ffn_w_gate_up, L0_ffn_w_down, L0_ffn_shared_gate_up, L0_ffn_shared_down,
           L1_attn_w_qkv, L1_attn_w_o, L1_ffn_gate_w, L1_ffn_wg, L1_ffn_wu, L1_ffn_wd, L1_ffn_sg, L1_ffn_su, L1_ffn_sd):
    import numpy as np
    import concourse.bacc as bacc
    from concourse.bass_utils import run_bass_kernel_spmd

    ndt = 2 * D + 2 * MS
    given = dict(
        u=np.asarray(L0_attn_u).reshape(NTOK, D), w_in=np.asarray(L0_attn_W_in)[:ndt].T,
        w_dt=np.asarray(L0_attn_W_in)[ndt:].T, 
        conv_w=np.asarray(L0_attn_conv_w).reshape(3, P, TAPS).transpose(1, 0, 2), conv_b=np.asarray(L0_attn_conv_b).reshape(3, P).T,
        w_out=np.asarray(L0_attn_W_out).T, A_log=L0_attn_A_log, D_param=np.asarray(L0_attn_D_param).reshape(KD, 2).T, dt_bias=L0_attn_dt_bias,
        gate0=L0_ffn_gate_w, gu0=L0_ffn_w_gate_up, dn0=L0_ffn_w_down, sh_gu0=L0_ffn_shared_gate_up,
        sh_dn0=L0_ffn_shared_down, qkv=L1_attn_w_qkv, w_o=L1_attn_w_o, gate1=np.asarray(L1_ffn_gate_w).T,
        wg1=L1_ffn_wg, wu1=L1_ffn_wu, wd1=L1_ffn_wd, sg1=L1_ffn_sg, su1=L1_ffn_su, sd1=L1_ffn_sd)
    nc = bacc.Bacc("TRN2", target_bir_lowering=False, num_devices=1)
    arrays, aps = {}, {}
    for name in _NAMES:
        v = np.ascontiguousarray(given[name])
        arrays[f"in_{name}"] = v
        aps[name] = nc.dram_tensor(f"in_{name}", v.shape, mybir.dt.from_np(v.dtype), kind="ExternalInput").ap()
    out = nc.dram_tensor("out", (NTOK, D), F32, kind="ExternalOutput").ap()
    build(nc, aps, out)
    r = run_bass_kernel_spmd(nc, [arrays], core_ids=[0])
    return r.results[0]["out"].reshape(NSEQ, SEQ, D)
```

```python
from contextlib import ExitStack

import concourse.bass as bass
from concourse import mybir

F32, BF16, I32 = mybir.dt.float32, mybir.dt.bfloat16, mybir.dt.int32
ALU, ACT, AX = mybir.AluOpType, mybir.ActivationFunctionType, mybir.AxisListType

P = 128
NSEQ, SEQ, D = 16, 256, 256
NTOK = NSEQ * SEQ
NT = NTOK // P
CH = SEQ // P
KD = D // P
E, TOPK = 8, 2
LATE = 2
RING = 4
NJ = -(-((NTOK * TOPK + E * (P - 1)) // P) // RING) * RING
MH, MP, MS, TAPS = 4, 64, 64, 4
I0, I1S, I1 = 512, 256, 128
AH, DH = 16, 16
BIG = 1.0e30
EPS = 1e-5
PAIRS = AH // 2
BAND = 4
LOGITS_SLOT = 4


class Round:

    def __init__(self, i, v, per=2):
        self.i, self.v, self.per, self.u, self.n = i, v, per, v % 2, i * per + v
        self.half = i * (per // 2) + v // 2

    def back(self, k=1):
        v = self.v - k
        return Round(self.i + (v // self.per), v % self.per, self.per)


class Event:

    def __init__(self, sem, credit=0, step=1, base=0):
        self.sem, self.credit, self.step, self.base = sem, credit, step, base

    def open(self, eng):
        if self.credit:
            eng.sem_inc(self.sem, self.credit * self.step)

    def mark(self, ins):
        ins.then_inc(self.sem, self.step)

    def wait(self, eng, n, back=0):
        eng.wait_ge(self.sem, (n + (1 - back + self.credit + self.base)) * self.step)


class Chain:

    def __init__(self, sem, per, before=0):
        self.sem, self.per, self.k, self.before = sem, per, 0, before

    def start(self, eng, n):
        self.eng, self.base, self.k = eng, (n + self.before) * self.per, 0

    def __call__(self, ins):
        self.k += 1
        ins.then_inc(self.sem, 1)
        self.eng.wait_ge(self.sem, self.base + self.k)

    def end(self):
        assert self.k == self.per, (self.k, self.per)


def rounds(eng, count, body, per=2):
    with eng.Fori(0, count // per) as i:
        for v in range(per):
            body(Round(i, v, per))


def pipelined(eng, count, depth, body, per=2):
    def turn(t):
        body(*(Round((t - k) // per, (t - k) % per, per) if 0 <= t - k < count else None for k in range(depth)))
    full = -(-(depth - 1) // per)
    for t in range(per * full):
        turn(t)
    with eng.Fori(full, count // per) as i:
        for v in range(per):
            r = Round(i, v, per)
            body(*(r.back(k) for k in range(depth)))
    for t in range(count, count + depth - 1):
        turn(t)


def late_rounds():
    return [Round(n // 2, n % 2) for n in range(NSEQ - LATE, NSEQ)]


def attention(eng, first=None, turns=None, last=None, new_pieces={}, old_pieces={}, done_pieces={}, turns_before=False,
              tail={}):
    def body(new, r, old, done):
        def at(f, k, g, *more):
            who = r if g >= k else old
            if f and (who or any(more)):
                f(who, (g - k) % PAIRS, *more)
        for g in range(PAIRS):
            with_logits = new if g == LOGITS_SLOT else None
            if not turns_before:
                at(first, 0, g, with_logits)
            at(turns, 1, g)
            if turns_before:
                at(first, 0, g, with_logits)
            at(last, 2, g)
            for who, pieces in ((old, old_pieces), (done, done_pieces), (new, new_pieces)):
                if who and g in pieces:
                    pieces[g](who)
            if r and not new and g in tail:
                tail[g]()
    pipelined(eng, NSEQ, 4, body)


def build(nc, a, out):
    ctx = ExitStack()
    with ctx:
        program(nc, ctx, a, out)


def program(nc, ctx, a, out):
    def sb(name, shape, dt=F32):
        return ctx.enter_context(nc.sbuf_tensor(name, shape, dt))

    def sem(name):
        return ctx.enter_context(nc.semaphore(name))

    named, engines = {}, {}

    def ev(name, credit=0, step=1, by=None, base=0):
        first = name not in named
        if first:
            named[name] = sem(name)
        e = Event(named[name], credit, step, base)
        if first and by:
            engines.setdefault(by, []).append(e)
        return e

    bank = [ctx.enter_context(nc.psum_tensor(f"bank{i}", [P, 512], F32)) for i in range(8)]

    xn_rows = [nc.dram_tensor(f"xn_rows{l}", (NTOK, D), F32, kind="Internal").ap() for l in range(2)]
    y_rows = [nc.dram_tensor(f"y_rows{l}", (NJ * P, D), F32, kind="Internal").ap() for l in range(2)]

    ident = sb("ident", [P, P])
    tri_le = sb("tri_le", [P, P])
    tri_gt = sb("tri_gt", [P, P])
    ones = sb("ones", [P, MS])
    quarter_le = sb("quarter_le", [P, P])
    ones_b = sb("ones_b", [P, P], BF16)
    before_b = sb("before_b", [P, P], BF16)
    ident_b = sb("ident_b", [P, P], BF16)
    future_b = sb("future_b", [P, P], BF16)
    iota_e = sb("iota_e", [P, E])
    iota_j = sb("iota_j", [P, P])
    part_no = sb("part_no", [P, 1])
    head_mask = sb("head_mask", [P, BAND + 1])
    minus_half = sb("minus_half", [P, CH])
    itmp_e = sb("itmp_e", [P, E], I32)

    par_i = sb("par_i", [P, 2], I32)

    X = sb("X", [P, NT, D])
    XT = sb("XT", [P, KD, NTOK])
    WGU = sb("WGU", [P, E * KD * 2 * I0])
    ARENA = sb("ARENA", [P, E * I0 // P * D])
    itmp_j = ARENA[:, 0:P].bitcast(I32)
    w_in = sb("w_in", [P, KD, 2 * D + 2 * MS])
    w_r0 = sb("w_r0", [P, KD, E + MH])
    w_out = sb("w_out", [P, KD, D])
    sh_gu = sb("sh_gu", [P, KD, 2 * I0])
    sh_dn = sb("sh_dn", [P, I0 // P, D])

    class Area:

        def __init__(self, t):
            self.t, self.at = t, 0

        def take(self, *shape):
            n = 1
            for s in shape:
                n *= s
            v = self.t[:, self.at:self.at + n]
            self.at += n
            assert self.at <= self.t.shape[1]
            names = "abcde"[:len(shape)]
            if len(shape) > 1:
                v = v.rearrange(f"p ({' '.join(names)}) -> p {' '.join(names)}",
                                **{c: s for c, s in zip(names, shape)})
            return v

    wgu0 = WGU[:, :].rearrange("p (e k n) -> p e k n", e=E, k=KD)
    wdn0 = ARENA[:, :].rearrange("p (e c n) -> p e c n", e=E, c=I0 // P)

    XN = [sb(f"XN{u}", [P, CH, D]) for u in range(2)]
    xT = [sb(f"xT{u}", [P, KD, SEQ]) for u in range(2)]
    stats = sb("stats", [P, CH, 6])
    mv = [sb(f"mv{u}", [P, CH, 2]) for u in range(2)]
    rstd = [sb(f"rstd{u}", [P, CH]) for u in range(2)]
    LG = sb("LG", [P, NT, E])
    DTR = sb("DTR", [P, NT, MH])
    DTA = sb("DTA", [P, NT, MH])
    DTE = sb("DTE", [P, NT, MH])
    dt_bias = sb("dt_bias", [P, MH])
    a_neg = sb("a_neg", [P, MH])
    conv_w = sb("conv_w", [P, 3, TAPS])
    conv_b = sb("conv_b", [P, 3])
    d_par = sb("d_par", [P, KD])
    hot_b = sb("hot_b", [P, NT, E], BF16)
    rs = sb("route_small", [P, 8, NT])
    ex = sb("route_experts", [P, 8, E])
    ex_i = sb("route_experts_i", [P, E], I32)
    tile_e = sb("tile_e", [P, NJ])
    tile_expert = sb("tile_expert", [P, NJ], I32)
    slot_i = [sb(f"slot{k}", [P, NT], I32) for k in range(TOPK)]
    slot_row = [sb(f"slot_row{k}", [P, NT]) for k in range(TOPK)]
    slot_tile = [sb(f"slot_tile{k}", [P, NT]) for k in range(TOPK)]
    NH = TOPK * CH
    as_b = [xT[u][:, :, :].rearrange("p k t -> p (k t)").bitcast(BF16) for u in range(2)]
    tile_hot = [as_b[u][:, 0:NH * NJ].rearrange("p (q j) -> p q j", q=NH) for u in range(2)]
    tile_val = [as_b[u][:, NH * NJ:3 * NH * NJ].rearrange("p (q j) -> p q j", q=NH) for u in range(2)]
    row_hot = [w_out[:, u, :].bitcast(BF16).rearrange("p (a b) -> p a b", b=P) for u in range(2)]
    dtmp_i = sb("dtmp_i", [P, NT], I32)
    cw = [sb(f"cw{k}", [P, NT]) for k in range(TOPK)]
    ring_idx = sb("ring_idx", [P, 8], I32)
    slot_tok = sb("slot_tok", [P, NJ], I32)

    rr = Area(ARENA)
    rr.at = 1024
    def take_route(area):
        return [area.take(NT, E) for k in range(TOPK)], [area.take(NT, E) for n in range(3)], area.take(NJ, E)

    route_space = [take_route(rr)]

    ar = Area(ARENA)
    MHm = ar.take(CH, MH, P)
    ED = ar.take(CH, MH, P)
    CV = ar.take(3, SEQ)
    TH = ar.take(3, SEQ)
    XS1 = ar.take(KD, SEQ)
    ZT = ar.take(KD, SEQ)
    SZ = ar.take(KD, SEQ)
    XD = ar.take(CH, MH, MP)
    XW = ar.take(MH, MP)
    YG = ar.take(KD, SEQ)
    GM = ar.take(CH, P)
    BS = ar.take(MS)
    BT1 = ar.take(SEQ)
    CT1 = ar.take(SEQ)
    SS = ar.take(MH * MP)
    CE = ar.take(MH, P)[0:MS]

    wa = Area(WGU)
    wgu1 = wa.take(E, KD, 2 * I1)
    wdn1 = wa.take(E, D)
    sh_gu1 = wa.take(KD, 2 * I1S)
    sh_dn1 = wa.take(I1S // P, D)
    w_qkv = wa.take(KD, 3 * D)
    w_o = wa.take(KD, D)
    w_r1 = wa.take(KD, E)
    Y1 = wa.take(CH, D)
    Y2 = wa.take(CH, D)
    YF = [[Y1, Y2], [wa.take(CH, D) for k in range(TOPK)]]
    OT = wa.take(KD, SEQ)
    route_space.append(take_route(wa))
    aa = Area(ARENA)
    QT = [aa.take(KD, SEQ) for _ in range(2)]
    KM = [[a_.take(KD, SEQ) for _ in range(BAND)] for a_ in (aa, wa)]
    V = [aa.take(CH, D) for _ in range(2)]
    PR = [aa.take(2, 3, P) for _ in range(2)]
    PT = [aa.take(2, 3, P) for _ in range(2)]
    SM = [aa.take(CH, AH) for _ in range(2)]
    SR = aa.take(CH, AH)
    MX = [aa.take(2, 3) for _ in range(2)]
    NM = [aa.take(2, 2) for _ in range(2)]
    ON = aa.take(CH, AH, DH)

    as_counts = lambda b: b.rearrange("p (t e) -> p t e", e=E)
    rank_space = [(as_counts(bank[6][:, 0:NT * E]), as_counts(bank[7][:, 0:NT * E])),
                  (as_counts(bank[0][:, 0:NT * E]), as_counts(bank[0][:, NT * E:2 * NT * E]))]

    SG = [sb(f"SG{u}", [P, SEQ]) for u in range(2)]
    HTt = [sb(f"HT{u}", [P, I0 // P, SEQ]) for u in range(2)]
    XS = [xT[0][:, :, :], XS1]
    BT = [SG[0][:, :], BT1]
    CT = [SG[1][:, :], CT1]
    WM = HTt[0][:, :, :].rearrange("p i (a t) -> p (i a) t", t=P).rearrange("p (c h) t -> p c h t", h=MH)
    XG = [XN[v % 2][:, v // 2, :] for v in range(RING)]
    XGT = [xT[u][:, :, 0:P] for u in range(2)]
    HE = [HTt[u][:, :, P:2 * P] for u in range(2)]
    SE = w_out[:, :, :].rearrange("p k n -> p (k n)")
    HET = [HTt[u][:, :, 0:P] for u in range(2)]
    YO = [w_in[:, v // 2, v % 2 * D:(v % 2 + 1) * D] for v in range(RING)]

    s_const, s_cmask = sem("const"), sem("const_masks")
    XL = [ev(f"load_x{part}", 0, 16) for part in range(2)]
    s_w_r0, s_small, s_w_in, s_w_out = sem("load_router0"), sem("load_small"), sem("load_w_in"), sem("load_w_out")
    s_sh0, s_wgu0, s_wdn0 = sem("load_shared0"), sem("load_gate_up0"), sem("load_down0")
    s_l1a, s_l1b = sem("load_attention1"), sem("load_experts1")
    s_prep, s_prep2 = sem("prepare"), sem("prepare2")

    def norm_events(l):
        b = l * NSEQ
        n = {name: ev(f"norm_{name}", credit, 1, eng, b) for name, credit, eng in (
            ("var", 0, None), ("rstd", 0, None), ("xn", 0, None), ("tr", 2, "tensor"), ("xT", 2, "scalar"),
            ("lg", 2, "tensor"), ("lgc", 2, "vector"))}
        n["stored"] = [ev(f"norm_stored{u}", 1, 16, "sync", b // 2) for u in range(2)]
        n["chain"] = Chain(norm_chain, 2, b)
        return n

    norm_chain = sem("norm_chain")
    N = [norm_events(0), norm_events(1)]

    def ffn_events(l, ni, parts_before):
        return dict(ni=ni, gu=ev("ffn_gate_up", 0, 1, None, parts_before), sg=ev("ffn_silu", 2, 1, "scalar", parts_before),
                    ht=ev("ffn_inner", 4, 1, "vector", parts_before), dn=ev("ffn_down", 2, 1, "tensor", l * NSEQ),
                    add=ev("ffn_added", 2, 1, "vector", l * NSEQ))

    FF = [ffn_events(0, I0 // P, 0), ffn_events(1, I1S // P, NSEQ * I0 // P)]

    def expert_events(l):
        b = l * NJ
        x = {name: ev(f"expert_{name}", credit, 1, eng, b) for name, credit, eng in (
            ("idx", 0, "gpsimd"), ("xt", RING, "tensor"), ("xtc", 1, "scalar"), ("g", 0, "tensor"), ("u", 0, "tensor"),
            ("sg", 1, "scalar"), ("h", 2, "vector"), ("ht", 2, "tensor"), ("htc", 1, "vector"), ("dn", 2, "tensor"),
            ("yo", 2, "scalar"))}
        x["got"] = [ev(f"expert_got{v}", 0, 16, None, b // RING) for v in range(RING)]
        x["out"] = [ev(f"expert_out{v}", 1, 16, "sync", b // RING) for v in range(RING)]
        return x

    EX = [expert_events(0), expert_events(1)]

    s_route, s_rank, s_hot, s_exp2, s_m21, s_placed = (sem(n) for n in (
        "route_chain", "rank", "hot", "exp2", "m21", "placed"))
    route_count = [0]
    LS = [{name: ev(f"list_{name}", credit, 1, eng, l * NSEQ) for name, credit, eng in (
        ("hot", 0, None), ("val", 2, "gpsimd"), ("sum", 2, "tensor"))} for l in range(2)]
    s_slots = sem("slots")
    s_nop = sem("unfused_wait")
    s_sp = sem("softplus")
    s_spa = sem("softplus_act")
    M = {}
    for name, credit, eng in (
            ("proj", 0, "tensor"), ("mh", 1, "gpsimd"), ("dec", 1, "tensor"), ("ed", 1, "scalar"), ("ce", 1, "gpsimd"),
            ("cv0", 1, "scalar"), ("cv", 1, "vector"), ("th", 1, "scalar"), ("z", 0, "tensor"), ("zt", 1, "scalar"), ("sz", 1, "vector"),
            ("xs", 1, "vector"), ("ct", 1, "vector"), ("xtr", 1, "tensor"), ("gtr", 1, "tensor"), ("gm", 1, "vector"), ("bs", 1, "scalar"),
            ("xd", 1, "vector"), ("xw", 1, "vector"), ("wm", 1, "vector"), ("wm1", 1, "gpsimd"), ("st", 1, "tensor"), ("ss", 1, "scalar"),
            ("y", 2, "tensor"), ("yg", 1, "vector"), ("o", 1, "tensor"), ("add", 1, "vector")):
        M[name] = ev(f"m_{name}", credit, 1, eng)
    M["chain"] = Chain(sem("m_chain"), TAPS - 2)
    ych = Chain(sem("m_y_chain"), 1)
    A = {}
    for name, credit, eng in (
            ("q", 1, "tensor"), ("qc", 1, "scalar"), ("k", 1, "tensor"), ("kc", 1, "vector"), ("v", 1, "tensor"), ("vc", 1, "scalar"),
            ("s", 0, "tensor"), ("max", 2, "vector"), ("nm", 2, "vector"), ("exp", 2, "scalar"), ("pt", 2, "tensor"), ("ptc0", 2, "vector"), ("ptc1", 2, "scalar"),
            ("pv", 2, "tensor"), ("sr", 2, "vector"), ("on", 2, "vector"), ("ot", 1, "tensor"), ("otc", 1, "scalar"),
            ("wo", 1, "tensor"), ("add", 3, "vector"), ("comb", 1, "vector")):
        A[name] = ev(f"a_{name}", credit, 1, eng)
    A["mchain"] = Chain(sem("a_max_chain"), 2)
    A["cchain"] = Chain(sem("a_combine_chain"), CH)
    A["y"] = [ev(f"a_y{k}", 0, 16) for k in range(CH * TOPK)]
    s_aidx = ev("a_idx")
    s_hmask = sem("head_mask")
    FY = [ev(f"fin_y{u}", 0, 16 * CH * TOPK) for u in range(2)]
    FO = [ev(f"fin_out{k}", 1, 16, "sync") for k in range(2)]
    FC = ev("fin_done", 2, 1, "vector")
    FI = ev("fin_index")
    FCH = Chain(sem("fin_ch"), 1)

    block = ctx.enter_context(nc.Block())

    def unfuse(eng):
        eng.sem_inc(s_nop, 1)

    def open_events(eng, name):
        for e in engines.get(name, []):
            e.open(eng)

    x_in = a["u"].rearrange("(t p) d -> p t d", p=P)
    x_out = out.rearrange("(t p) d -> p t d", p=P)

    @block.sync
    def _(eng):
        open_events(eng, "sync")

        def load_pair(n):
            at = n * 2 * CH
            XL[n % 2].mark(eng.dma_start(X[:, at:at + 2 * CH, :], x_in[:, at:at + 2 * CH, :]))
        load_pair(0)
        eng.dma_start(w_r0[:, :, 0:E], a["gate0"].rearrange("(k p) n -> p k n", p=P)).then_inc(s_w_r0, 16)
        eng.dma_start(w_r0[:, :, E:E + MH], a["w_dt"].rearrange("(k p) n -> p k n", p=P)).then_inc(s_w_r0, 16)
        eng.dma_start(dt_bias[:, :], a["dt_bias"].partition_broadcast(P)).then_inc(s_small, 16)
        eng.dma_start(a_neg[:, :], a["A_log"].partition_broadcast(P)).then_inc(s_small, 16)
        eng.dma_start(conv_w[:, :, :], a["conv_w"]).then_inc(s_small, 16)
        eng.dma_start(conv_b[:, :], a["conv_b"]).then_inc(s_small, 16)
        for q in range(2):
            eng.dma_start(d_par[q * MP:(q + 1) * MP, :], a["D_param"][q, :].partition_broadcast(MP)).then_inc(s_small, 16)
        load_pair(1)
        for n in range(2, NSEQ // 2):
            XL[n % 2].wait(eng, n // 2 - 1)
            load_pair(n)
        eng.dma_start(w_in[:, :, :], a["w_in"].rearrange("(k p) n -> p k n", p=P)).then_inc(s_w_in, 16)
        eng.dma_start(w_out[:, :, :], a["w_out"].rearrange("(k p) n -> p k n", p=P)).then_inc(s_w_out, 16)
        eng.dma_start(sh_gu[:, :, :], a["sh_gu0"].rearrange("(k p) n -> p k n", p=P)).then_inc(s_sh0, 16)
        eng.dma_start(sh_dn[:, :, :], a["sh_dn0"].rearrange("(c p) n -> p c n", p=P)).then_inc(s_sh0, 16)
        def store_xn(l):
            def body(r):
                N[l]["xn"].wait(eng, r.n)
                rows = xn_rows[l].rearrange("(t p) d -> p t d", p=P)
                N[l]["stored"][r.u].mark(eng.dma_start(rows[:, bass.ds(r.n * CH, CH), :], XN[r.u][:, :, :]))
            rounds(eng, NSEQ, body)

        def store_y(l):
            def body(r):
                EX[l]["yo"].wait(eng, r.n)
                rows = y_rows[l].rearrange("(j p) d -> p j d", p=P)
                EX[l]["out"][r.v].mark(eng.dma_start(rows[:, bass.ds(r.n, 1), :], YO[r.v].unsqueeze(1)))
            rounds(eng, NJ, body, RING)

        store_xn(0)
        for e in range(E):
            eng.dma_start(wgu0[:, e, :, :], a["gu0"][e].rearrange("(k p) n -> p k n", p=P)).then_inc(s_wgu0, 16)
        M["add"].wait(eng, NSEQ - 1)
        for e in range(E):
            eng.dma_start(wdn0[:, e, :, :], a["dn0"][e].rearrange("(c p) n -> p c n", p=P)).then_inc(s_wdn0, 16)
        store_y(0)
        EX[0]["u"].wait(eng, NJ - 1)
        eng.dma_start(w_r1, a["gate1"].rearrange("(k p) n -> p k n", p=P)).then_inc(s_l1a, 16)
        eng.dma_start(w_qkv, a["qkv"].rearrange("(k p) n -> p k n", p=P)).then_inc(s_l1a, 16)
        eng.dma_start(w_o, a["w_o"].rearrange("(k p) n -> p k n", p=P)).then_inc(s_l1a, 16)
        eng.dma_start(sh_gu1[:, :, 0:I1S], a["sg1"].rearrange("(k p) n -> p k n", p=P)).then_inc(s_l1b, 16)
        eng.dma_start(sh_gu1[:, :, I1S:2 * I1S], a["su1"].rearrange("(k p) n -> p k n", p=P)).then_inc(s_l1b, 16)
        eng.dma_start(sh_dn1, a["sd1"].rearrange("(c p) n -> p c n", p=P)).then_inc(s_l1b, 16)
        for e in range(E):
            eng.dma_start(wgu1[:, e, :, 0:I1], a["wg1"][e].rearrange("(k p) n -> p k n", p=P)).then_inc(s_l1b, 16)
            eng.dma_start(wgu1[:, e, :, I1:2 * I1], a["wu1"][e].rearrange("(k p) n -> p k n", p=P)).then_inc(s_l1b, 16)
        eng.dma_start(wdn1, a["wd1"].rearrange("e p n -> p e n")).then_inc(s_l1b, 16)
        store_xn(1)
        store_y(1)

        def store_out(r):
            FC.wait(eng, r.n)
            FO[r.u].mark(eng.dma_start(x_out[:, bass.ds(r.n * CH, CH), :], X[:, bass.ds(r.n * CH, CH), :]))
        rounds(eng, NSEQ, store_out)
        for u in range(2):
            FO[u].wait(eng, NSEQ // 2 - 1)

    @block.gpsimd
    def _(eng):
        open_events(eng, "gpsimd")
        n = 0
        for t, v in ((ident, 0.0), (tri_le, 1.0), (tri_gt, 1.0), (ones, 1.0), (quarter_le, 0.25), (ident_b, 0.0),
                     (ones_b, 1.0), (before_b, 1.0), (future_b, 0.0), (minus_half, -0.5)):
            eng.memset(t[:, :], v).then_inc(s_const, 1)
            n += 1
        eng.iota(itmp_e[:, :], [[1, E]], base=0, channel_multiplier=0).then_inc(s_const, 1)
        eng.iota(itmp_j, [[1, P]], base=0, channel_multiplier=0).then_inc(s_const, 1)
        eng.iota(par_i[:, 0:1], [[0, 1]], base=0, channel_multiplier=1).then_inc(s_const, 1)
        n += 3
        eng.wait_ge(s_const, n)
        sel = eng.affine_select
        for t, op, fill, sign in ((ident, ALU.not_equal, 1.0, -1), (ident_b, ALU.not_equal, 1.0, -1)):
            sel(out=t[:, :], in_=t[:, :], compare_op=op, fill=fill, base=0, pattern=[[-1, P]],
                channel_multiplier=1).then_inc(s_const, 1)
        sel(out=tri_le[:, :], in_=tri_le[:, :], compare_op=ALU.is_ge, fill=0.0, base=0, pattern=[[1, P]],
            channel_multiplier=-1).then_inc(s_const, 1)
        sel(out=quarter_le[:, :], in_=quarter_le[:, :], compare_op=ALU.is_ge, fill=0.0, base=0, pattern=[[1, P]],
            channel_multiplier=-1).then_inc(s_const, 1)
        sel(out=tri_gt[:, :], in_=tri_gt[:, :], compare_op=ALU.is_gt, fill=0.0, base=0, pattern=[[-1, P]],
            channel_multiplier=1).then_inc(s_const, 1)
        sel(out=before_b[:, :], in_=before_b[:, :], compare_op=ALU.is_gt, fill=0.0, base=0, pattern=[[1, P]],
            channel_multiplier=-1).then_inc(s_const, 1)
        sel(out=future_b[:, :], in_=future_b[:, :], compare_op=ALU.is_ge, fill=-BIG, base=0, pattern=[[-1, P]],
            channel_multiplier=1).then_inc(s_const, 1)
        eng.tensor_copy(iota_e[:, :], itmp_e[:, :]).then_inc(s_const, 1)
        eng.tensor_copy(iota_j[:, :], itmp_j).then_inc(s_const, 1)
        eng.tensor_copy(part_no[:, :], par_i[:, 0:1]).then_inc(s_const, 1)
        n += 10
        eng.wait_ge(s_const, n)
        eng.sem_inc(s_cmask, 1)

        def norm_stage(l, r):
            ne = N[l]
            ne["var"].wait(eng, r.n)
            ne["rstd"].mark(eng.tensor_tensor(rstd[r.u][:, :], rstd[r.u][:, :], minus_half[:, :], ALU.pow))

        rounds(eng, NSEQ, lambda r: norm_stage(0, r))

        eng.wait_ge(s_sp, 4)

        def mamba(r):
            M["dec"].wait(eng, r.n, 1)
            av = DTA[:, bass.ds(r.n * CH, CH), :].rearrange("p c h -> p (c h)")
            M["mh"].mark(eng.tensor_tensor(
                MHm.rearrange("p c h t -> p (c h) t"),
                tri_le[:, :].unsqueeze(1).broadcast_to([P, CH * MH, P]),
                av.unsqueeze(2).broadcast_to([P, CH * MH, P]), ALU.mult))
            M["ed"].wait(eng, r.n)
            M["ct"].wait(eng, r.n)
            M["ce"].mark(eng.tensor_tensor(CE, CE, CT[r.u][0:MS, P:SEQ].unsqueeze(1).broadcast_to([MS, MH, P]), ALU.mult))
            M["gm"].wait(eng, r.n)
            M["y"].wait(eng, r.n, 1)
            M["wm1"].mark(eng.tensor_tensor(WM[:, 1, :, :], ED[:, 1, :, :],
                                            GM[:, 1, :].unsqueeze(1).broadcast_to([P, MH, P]), ALU.mult))
        rounds(eng, NSEQ, mamba)

        def list_values(l):
            ls = LS[l]

            def body(r):
                ls["hot"].wait(eng, r.n)
                ls["sum"].wait(eng, r.n, 2)
                for k in range(TOPK):
                    hot = tile_hot[r.u][:, k * CH:(k + 1) * CH, :]
                    number = iota_j[:, bass.ds(r.n * CH, CH)].unsqueeze(2).broadcast_to([P, CH, NJ])
                    eng.tensor_tensor(tile_val[r.u][:, k * CH:(k + 1) * CH, 0:NJ], hot, number, ALU.mult)
                    ins = eng.tensor_tensor(tile_val[r.u][:, k * CH:(k + 1) * CH, NJ:2 * NJ], hot,
                                            part_no[:, :].unsqueeze(2).broadcast_to([P, CH, NJ]), ALU.mult)
                ls["val"].mark(ins)
            rounds(eng, NSEQ, body)

        def gather_tiles(l):
            x = EX[l]
            eng.wait_ge(s_slots, l + 1)
            for u in range(2):
                N[l]["stored"][u].wait(eng, NSEQ // 2 - 1)

            def body(r):
                c = r.v
                x["xt"].wait(eng, r.n, RING)
                x["idx"].mark(eng.tensor_copy(ring_idx[:, c:c + 1], slot_tok[:, bass.ds(r.n, 1)]))
                x["idx"].wait(eng, r.n)
                unfuse(eng)
                x["got"][r.v].mark(eng.indirect_dma_start(
                    XG[r.v], None, xn_rows[l], bass.IndirectOffsetOnAxis(ring_idx[:, c:c + 1], 0)))
            rounds(eng, NJ, body, RING)

        list_values(0)
        gather_tiles(0)

        for v in range(RING):
            EX[0]["out"][v].wait(eng, NJ // RING - 1)

        def fetch_rows(r):
            A["comb"].wait(eng, r.n, 1)
            for c in range(CH):
                for k in range(TOPK):
                    q = c * TOPK + k
                    ins = eng.tensor_copy(ring_idx[:, q:q + 1], slot_i[k][:, bass.ds(r.n * CH + c, 1)])
            s_aidx.mark(ins)
            s_aidx.wait(eng, r.n)
            unfuse(eng)
            for c in range(CH):
                for k in range(TOPK):
                    q = c * TOPK + k
                    A["y"][q].mark(eng.indirect_dma_start(
                        (Y1, Y2)[k][:, c, :], None, y_rows[0],
                        bass.IndirectOffsetOnAxis(ring_idx[:, q:q + 1], 0)))
        EX[0]["dn"].wait(eng, NJ - 1)

        def attention(r):
            fetch_rows(r)
            norm_stage(1, r)
        rounds(eng, NSEQ, attention)
        list_values(1)
        gather_tiles(1)
        for v in range(RING):
            EX[1]["out"][v].wait(eng, NJ // RING - 1)

        def final(r):
            FC.wait(eng, r.n, 2)
            for c in range(CH):
                for k in range(TOPK):
                    q = (r.u * CH + c) * TOPK + k
                    ins = eng.tensor_copy(ring_idx[:, q:q + 1], slot_i[k][:, bass.ds(r.n * CH + c, 1)])
            FI.mark(ins)
            FI.wait(eng, r.n)
            unfuse(eng)
            for c in range(CH):
                for k in range(TOPK):
                    q = (r.u * CH + c) * TOPK + k
                    eng.indirect_dma_start(YF[r.u][k][:, c, :], None, y_rows[1],
                                           bass.IndirectOffsetOnAxis(ring_idx[:, q:q + 1], 0)).then_inc(FY[r.u].sem, 16)
        rounds(eng, NSEQ, final)

    @block.scalar
    def _(eng):
        open_events(eng, "scalar")
        act = eng.activation

        def norm_stage(l, r):
            ne = N[l]
            ne["tr"].wait(eng, r.n)
            ne["lg"].wait(eng, r.n, 2)
            src = bank[r.u if l == 0 else 0][:, :].rearrange("p (k t) -> p k t", k=KD)
            act(xT[r.u][:, :, :], src, ACT.Copy)
            ne["xT"].mark(act(XT[:, :, bass.ds(r.n * SEQ, SEQ)], src, ACT.Copy))

        eng.wait_ge(s_small, 96)
        act(a_neg[:, :], a_neg[:, :], ACT.Exp).then_inc(s_prep, 1)
        rounds(eng, NSEQ, lambda r: norm_stage(0, r))
        eng.wait_ge(s_sp, 2)
        flat = DTE[:, :, :].rearrange("p t h -> p (t h)")
        act(flat, flat, ACT.Exp).then_inc(s_spa, 1)
        eng.wait_ge(s_spa, 1)
        act(flat, flat, ACT.Ln, bias=1.0).then_inc(s_spa, 1)
        def exp2(l):
            eng.wait_ge(s_m21, l + 1)
            act(rs[:, 5, :], rs[:, 4, :], ACT.Exp).then_inc(s_exp2, 1)
        exp2(0)

        def decays(r):
            M["dec"].wait(eng, r.n)
            M["wm"].wait(eng, r.n, 1)
            M["wm1"].wait(eng, r.n, 1)
            M["xw"].wait(eng, r.n, 1)
            for c in range(CH):
                act(ED[:, c, :, :].rearrange("p h t -> p (h t)"), bank[4 + c][:, :], ACT.Exp)
            M["ce"].wait(eng, r.n, 1)
            M["y"].wait(eng, r.n, 1)
            M["ed"].mark(act(CE.rearrange("p h t -> p (h t)"), bank[6][0:MS, :], ACT.Exp))
            M["gtr"].wait(eng, r.n)
            M["st"].wait(eng, r.n, 1)
            M["bs"].mark(act(BS, bank[6][:, SEQ:SEQ + MS], ACT.Copy, scale=0.5))

        def conv_tanh(r):
            M["cv"].wait(eng, r.n)
            M["xs"].wait(eng, r.n, 1)
            M["th"].mark(act(TH.rearrange("p c t -> p (c t)"), CV.rearrange("p c t -> p (c t)"), ACT.Tanh, scale=0.5))

        def conv_first(r):
            M["proj"].wait(eng, r.n)
            M["xs"].wait(eng, r.n, 1)
            for c in range(3):
                src = bank[2][:, c * SEQ:(c + 1) * SEQ] if c < 2 else bank[3][:, 0:SEQ]
                ins = act(CV[:, c, :], src, ACT.Identity, bias=conv_b[:, c:c + 1], scale=conv_w[:, c, TAPS - 1:TAPS])
            M["cv0"].mark(ins)

        def state_copy(r):
            M["st"].wait(eng, r.n)
            M["y"].wait(eng, r.n, 1)
            M["ss"].mark(act(SS[0:MS, :], bank[6][0:MS, 0:MH * MP], ACT.Copy, scale=0.5))

        def z_tanh(r):
            M["z"].wait(eng, r.n)
            M["sz"].wait(eng, r.n, 1)
            M["zt"].mark(act(ZT.rearrange("p k t -> p (k t)"), bank[1][:, :], ACT.Tanh, scale=0.5))

        def mamba(new, conv, r, old):
            if r:
                decays(r)
            if conv:
                conv_tanh(conv)
            if r:
                state_copy(r)
            if new:
                conv_first(new)
            if r:
                z_tanh(r)
        pipelined(eng, NSEQ, 4, mamba)

        def ffn(l):
            f, ni = FF[l], FF[l]["ni"]

            def body(r):
                for i in range(ni):
                    n = r.n * ni + i
                    f["gu"].wait(eng, n)
                    f["ht"].wait(eng, n, 2)
                    f["sg"].mark(act(SG[i % 2][:, :], bank[i][:, 0:SEQ], ACT.Silu))
            rounds(eng, NSEQ if l == 1 else NSEQ - LATE, body)
            return body
        late_part = ffn(0)

        def experts(l):
            x = EX[l]

            def xt_copy(r):
                x["xt"].wait(eng, r.n)
                x["h"].wait(eng, r.n, 2)
                x["xtc"].mark(act(XGT[r.u], bank[4][:, 0:KD * P].rearrange("p (k t) -> p k t", k=KD), ACT.Copy))

            def silu(r):
                x["g"].wait(eng, r.n)
                x["h"].wait(eng, r.n, 1)
                w = I0 if l == 0 else I1
                x["sg"].mark(act(SE[:, 0:w], bank[r.u][:, 0:w], ACT.Silu))

            def y_copy(r):
                x["dn"].wait(eng, r.n)
                x["out"][r.v].wait(eng, r.i, 1)
                x["yo"].mark(act(YO[r.v], bank[6 + r.u][:, 0:D], ACT.Copy))

            def body(new, r, old, older):
                if r:
                    silu(r)
                if new:
                    xt_copy(new)
                if older:
                    y_copy(older)
            pipelined(eng, NJ, 4, body, RING)
        experts(0)
        for r in late_rounds():
            late_part(r)

        def exps(r, g, new):
            if not r:
                return
            n = r.n * PAIRS + g
            A["nm"].wait(eng, n)
            A["pt"].wait(eng, n, 2)
            if g == 0:
                A["sr"].wait(eng, r.n, 2)
            for h in range(2):
                b = bank[1 + 2 * (g % 2) + h]
                for q, (lo, hi) in enumerate(((0, 1), (1, 3))):
                    ins = act(PR[g % 2][:, h, lo:hi, :].rearrange("p b k -> p (b k)"), b[:, lo * P:hi * P], ACT.Exp,
                              bias=NM[g % 2][:, h, q:q + 1],
                              accum_out=SM[r.u][:, q, 2 * g + h:2 * g + h + 1])
            A["exp"].mark(ins)

        def pt_copy(r, g):
            n = r.n * PAIRS + g
            A["pt"].wait(eng, n)
            A["pv"].wait(eng, n, 2)
            A["ptc1"].mark(act(PT[g % 2][:, 1, :, :], bank[6][:, 0:3 * P].rearrange("p (b k) -> p b k", b=3), ACT.Copy))

        def q_copy(r):
            A["q"].wait(eng, r.n)
            A["on"].wait(eng, r.n, 2)
            A["qc"].mark(act(QT[r.u].rearrange("p k t -> p (k t)"), bank[0][:, :], ACT.Copy))

        def v_copy(r):
            A["v"].wait(eng, r.n)
            A["vc"].mark(act(V[r.u].rearrange("p k t -> p (k t)"), bank[0][:, :], ACT.Copy))

        def o_copy(r):
            A["ot"].wait(eng, r.n)
            A["wo"].wait(eng, r.n, 1)
            A["otc"].mark(act(OT.rearrange("p k t -> p (k t)"), bank[0][:, :], ACT.Copy))

        attention(eng, turns=pt_copy, first=exps, new_pieces={2: lambda r: norm_stage(1, r), 3: q_copy, 4: v_copy},
                  done_pieces={0: o_copy}, turns_before=True, tail={2: lambda: exp2(1)})
        experts(1)
        ffn(1)

    @block.vector
    def _(eng):
        open_events(eng, "vector")
        tt, ts, stt = eng.tensor_tensor, eng.tensor_scalar, eng.scalar_tensor_tensor

        def norm_stats(l, r):
            ne, ch = N[l], N[l]["chain"]
            ch.start(eng, r.n)
            unfuse(eng)
            for c in range(CH):
                ins = eng.bn_stats(stats[:, c, :], X[:, bass.ds(r.n * CH + c, 1), :].rearrange("p a d -> p (a d)"))
            ch(ins)
            unfuse(eng)
            for c in range(CH):
                ins = eng.bn_aggr(mv[r.u][:, c, :], stats[:, c, :])
            ch(ins)
            ch.end()
            ne["var"].mark(ts(rstd[r.u][:, :], mv[r.u][:, :, 1], EPS, None, ALU.add))

        def norm_apply(l, r):
            ne = N[l]
            ne["rstd"].wait(eng, r.n)
            ne["stored"][r.u].wait(eng, r.half, 1)
            ne["tr"].wait(eng, r.n, 2)
            for c in range(CH):
                ins = ts(XN[r.u][:, c, :], X[:, bass.ds(r.n * CH + c, 1), :].rearrange("p a d -> p (a d)"),
                         mv[r.u][:, c, 0:1], rstd[r.u][:, c:c + 1], ALU.subtract, ALU.mult)
            ne["xn"].mark(ins)
            ne["xn"].wait(eng, r.n)

        def logits_stage(l, r):
            ne = N[l]
            ne["lg"].wait(eng, r.n)
            b = bank[6 + r.u] if l == 0 else bank[1][:, 3 * P:4 * P]
            w = E + MH if l == 0 else E
            src = b[:, 0:CH * w].rearrange("p (c e) -> p c e", c=CH)
            if l == 0:
                tt(DTR[:, bass.ds(r.n * CH, CH), :], src[:, :, E:E + MH],
                   dt_bias[:, :].unsqueeze(1).broadcast_to([P, CH, MH]), ALU.add)
            ne["lgc"].mark(eng.tensor_copy(LG[:, bass.ds(r.n * CH, CH), :], src[:, :, 0:E]))

        eng.wait_ge(s_small, 96)

        def norm_turn(new, r, old, older):
            if new:
                XL[new.v // 2].wait(eng, new.i)
                norm_stats(0, new)
            if r:
                norm_apply(0, r)
            if older:
                logits_stage(0, older)
        pipelined(eng, NSEQ, 4, norm_turn, 4)

        N[0]["lgc"].wait(eng, NSEQ - 1)
        flat = lambda t: t[:, :, :].rearrange("p t h -> p (t h)")
        stt(flat(DTE), flat(DTR), -1.0, flat(DTR), ALU.mult, ALU.min).then_inc(s_sp, 1)
        eng.wait_ge(s_prep, 1)
        ts(a_neg[:, :], a_neg[:, :], -1.0, None, ALU.mult).then_inc(s_sp, 1)
        eng.wait_ge(s_spa, 2)
        stt(flat(DTR), flat(DTR), 0.0, flat(DTE), ALU.max, ALU.add).then_inc(s_sp, 1)
        eng.wait_ge(s_sp, 3)
        tt(DTA[:, :, :], DTR[:, :, :], a_neg[:, :].unsqueeze(1).broadcast_to([P, NT, MH]), ALU.mult).then_inc(s_sp, 1)
        eng.wait_ge(s_sp, 4)
        ts(flat(DTE), flat(DTR), 0.5, None, ALU.mult).then_inc(s_prep2, 1)
        ts(d_par[:, :], d_par[:, :], 0.5, None, ALU.mult).then_inc(s_prep2, 1)
        eng.wait_ge(s_w_out, 16)
        ts(w_out[:, :, :].rearrange("p k n -> p (k n)"), w_out[:, :, :].rearrange("p k n -> p (k n)"), 0.5, None,
           ALU.mult).then_inc(s_prep2, 1)

        def route(l):
            s, count = s_route, route_count

            def link(ins):
                count[0] += 1
                ins.then_inc(s, 1)
                eng.wait_ge(s, count[0])
            N[l]["lgc"].wait(eng, NSEQ - 1)
            OH, rt, tile_cmp = route_space[l]
            work, masked = rt[0], rt[1]
            within, total = rank_space[l]
            bc_e = lambda v: v.unsqueeze(2).broadcast_to([P, NT, E])
            ie = iota_e[:, :].unsqueeze(1).broadcast_to([P, NT, E])
            for k in range(TOPK):
                lg = LG if k == 0 else masked
                yield link(eng.tensor_reduce(rs[:, k, :], lg[:, :, :], AX.X, ALU.max))
                yield link(tt(work[:, :, :], lg[:, :, :], bc_e(rs[:, k, :]), ALU.is_lt))
                yield link(stt(work[:, :, :], work[:, :, :], float(E), ie, ALU.mult, ALU.add))
                yield link(eng.tensor_reduce(rs[:, 2, :], work[:, :, :], AX.X, ALU.min))
                yield link(tt(OH[k], ie, bc_e(rs[:, 2, :]), ALU.is_equal))
                if k == 0:
                    yield link(stt(masked[:, :, :], OH[0], -3.0e38, LG[:, :, :], ALU.mult, ALU.add))
            tt(rs[:, 4, :], rs[:, 1, :], rs[:, 0, :], ALU.subtract).then_inc(s_m21, 1)
            yield link(tt(work[:, :, :], OH[0], OH[1], ALU.add))
            eng.tensor_copy(hot_b[:, :, :], work[:, :, :]).then_inc(s_hot, 1)
            eng.wait_ge(s_exp2, l + 1)
            yield link(ts(rs[:, 6, :], rs[:, 5, :], 1.0, None, ALU.add))
            yield link(eng.reciprocal(cw[0][:, :], rs[:, 6, :]))
            yield link(tt(cw[1][:, :], rs[:, 5, :], cw[0][:, :], ALU.mult))
            eng.wait_ge(s_rank, l + 1)
            yield link(eng.tensor_copy(rt[1][:, :, :], total))
            src, dst = rt[1], rt[2]
            step = 1
            while step < NT:
                eng.tensor_copy(dst[:, 0:step, :], src[:, 0:step, :])
                yield link(tt(dst[:, step:NT, :], src[:, step:NT, :], src[:, 0:NT - step, :], ALU.add))
                src, dst, step = dst, src, step * 2
            yield link(ts(ex_i[:, :], src[:, NT - 1, :], float(P - 1), None, ALU.add))
            yield link(ts(ex_i[:, :], ex_i[:, :], 7, None, ALU.arith_shift_right))
            yield link(eng.tensor_copy(ex[:, 0, :], ex_i[:, :]))
            a_, b_, step = 0, 1, 1
            while step < E:
                eng.tensor_copy(ex[:, b_, 0:step], ex[:, a_, 0:step])
                yield link(tt(ex[:, b_, step:E], ex[:, a_, step:E], ex[:, a_, 0:E - step], ALU.add))
                a_, b_, step = b_, (b_ + 1 if b_ < 3 else 3), step * 2
            ends = ex[:, a_, :]
            eng.memset(ex[:, 5, 0:1], 0.0)
            yield link(ts(ex[:, 5, 1:E], ex[:, a_, 0:E - 1], float(P), None, ALU.mult))
            yield link(tt(dst[:, :, :], src[:, :, :], total, ALU.subtract))
            yield link(tt(dst[:, :, :], dst[:, :, :], within, ALU.add))
            yield link(tt(dst[:, :, :], dst[:, :, :], ex[:, 5, :].unsqueeze(1).broadcast_to([P, NT, E]), ALU.add))
            for k in range(TOPK):
                yield link(tt(work[:, :, :], dst[:, :, :], OH[k], ALU.mult))
                yield link(eng.tensor_reduce(rs[:, 7, :], work[:, :, :], AX.X, ALU.add))
                yield link(eng.tensor_copy(slot_i[k][:, :], rs[:, 7, :]))
                yield link(ts(dtmp_i[:, :], slot_i[k][:, :], P - 1, None, ALU.bitwise_and))
                yield link(eng.tensor_copy(slot_row[k][:, :], dtmp_i[:, :]))
                yield link(ts(dtmp_i[:, :], slot_i[k][:, :], 7, None, ALU.arith_shift_right))
                yield link(eng.tensor_copy(slot_tile[k][:, :], dtmp_i[:, :]))
            yield link(tt(tile_cmp[:, :, 0:E - 1], iota_j[:, 0:NJ].unsqueeze(2).broadcast_to([P, NJ, E - 1]),
                    ends[:, 0:E - 1].unsqueeze(1).broadcast_to([P, NJ, E - 1]), ALU.is_ge))
            yield link(eng.tensor_reduce(tile_e[:, :], tile_cmp[:, :, 0:E - 1], AX.X, ALU.add))
            yield link(eng.tensor_copy(tile_expert[:, :], tile_e[:, :]))
            eng.wait_ge(s, count[0])
            eng.drain().then_inc(s_placed, 1)

        def list_hot(l, r):
            ls = LS[l]
            ls["sum"].wait(eng, r.n, 2)
            ls["val"].wait(eng, r.n, 2)
            for k in range(TOPK):
                for hot, n, place in ((row_hot, P, slot_row), (tile_hot, NJ, slot_tile)):
                    ins = tt(hot[r.u][:, k * CH:(k + 1) * CH, :], iota_j[:, 0:n].unsqueeze(1).broadcast_to([P, CH, n]),
                             place[k][:, bass.ds(r.n * CH, CH)].unsqueeze(2).broadcast_to([P, CH, n]), ALU.is_equal)
            ls["hot"].mark(ins)

        def list_end(l):
            LS[l]["sum"].wait(eng, NSEQ - 1)
            s, count = s_route, route_count
            eng.tensor_copy(tile_e[:, :], bank[6][:, 0:NJ]).then_inc(s, 1)
            eng.wait_ge(s, count[0] + 1)
            stt(tile_e[:, :], tile_e[:, :], float(P), bank[6][:, NJ:2 * NJ], ALU.mult, ALU.add).then_inc(s, 1)
            eng.wait_ge(s, count[0] + 2)
            count[0] += 2
            eng.tensor_copy(slot_tok[:, :], tile_e[:, :]).then_inc(s_slots, 1)

        eng.wait_ge(s_cmask, 1)
        for _ in route(0):
            pass

        def gate_y(r):
            M["y"].wait(eng, r.n)
            M["o"].wait(eng, r.n, 1)
            for j in range(KD):
                ins = stt(YG[:, j, :], XS[r.u][:, j, :], d_par[:, j:j + 1], bank[7][:, j * SEQ:(j + 1) * SEQ],
                          ALU.mult, ALU.add)
            ych.start(eng, r.n)
            ych(ins)
            ych.end()
            M["yg"].mark(tt(YG.rearrange("p k t -> p (k t)"), YG.rearrange("p k t -> p (k t)"), SZ.rearrange("p k t -> p (k t)"),
                            ALU.mult))

        def conv_taps(r):
            ch = M["chain"]
            ch.start(eng, r.n)
            M["cv0"].wait(eng, r.n)
            for k in range(1, TAPS):
                for c in range(3):
                    src = bank[2][:, c * SEQ:(c + 1) * SEQ] if c < 2 else bank[3][:, 0:SEQ]
                    ins = stt(CV[:, c, k:SEQ], src[:, 0:SEQ - k], conv_w[:, c, TAPS - 1 - k:TAPS - k], CV[:, c, k:SEQ],
                              ALU.mult, ALU.add)
                if k < TAPS - 1:
                    ch(ins)
            M["cv"].mark(ins)
            ch.end()

        def scan_parts(r):
            M["ed"].wait(eng, r.n)
            M["xtr"].wait(eng, r.n)
            M["y"].wait(eng, r.n, 1)
            dts = DTE[:, bass.ds(r.n * CH, CH), :].rearrange("p c h -> p (c h)")
            M["xd"].mark(tt(XD.rearrange("p c h d -> p (c h) d"), bank[4][:, :].rearrange("p (g d) -> p g d", d=MP),
                            dts.unsqueeze(2).broadcast_to([P, CH * MH, MP]), ALU.mult))
            M["xd"].wait(eng, r.n)
            M["xw"].mark(tt(XW, XD[:, 0, :, :], ED[:, 0, :, P - 1:P].broadcast_to([P, MH, MP]), ALU.mult))
            M["gtr"].wait(eng, r.n)
            M["wm1"].wait(eng, r.n, 1)
            M["gm"].mark(tt(GM, bank[5][:, 0:SEQ].rearrange("p (c t) -> p c t", c=CH),
                            quarter_le[:, :].unsqueeze(1).broadcast_to([P, CH, P]), ALU.mult))
            M["gm"].wait(eng, r.n)
            M["wm"].mark(tt(WM[:, 0, :, :], ED[:, 0, :, :], GM[:, 0, :].unsqueeze(1).broadcast_to([P, MH, P]), ALU.mult))

        def conv_silu(r):
            M["th"].wait(eng, r.n)
            M["y"].wait(eng, r.n, 2)
            stt(BT[r.u][0:MS, :], TH[0:MS, 2, :], 1.0, CV[0:MS, 2, :], ALU.add, ALU.mult)
            M["ct"].mark(stt(CT[r.u][0:MS, :], TH[MS:P, 2, :], 1.0, CV[MS:P, 2, :], ALU.add, ALU.mult))
            M["xs"].mark(stt(XS[r.u].rearrange("p k t -> p (k t)"), TH[:, 0:2, :].rearrange("p k t -> p (k t)"), 1.0,
                             CV[:, 0:2, :].rearrange("p k t -> p (k t)"), ALU.add, ALU.mult))

        def z_silu(r):
            M["zt"].wait(eng, r.n)
            M["yg"].wait(eng, r.n, 1)
            M["sz"].mark(stt(SZ.rearrange("p k t -> p (k t)"), ZT.rearrange("p k t -> p (k t)"), 1.0, bank[1][:, :],
                             ALU.add, ALU.mult))

        def add_y(r):
            M["o"].wait(eng, r.n)
            xs = X[:, bass.ds(r.n * CH, CH), :].rearrange("p c d -> p (c d)")
            M["add"].mark(tt(xs, xs, bank[0][:, :], ALU.add))

        def mamba(new, conv, r, old):
            if old:
                gate_y(old)
            if conv:
                conv_taps(conv)
            if r:
                scan_parts(r)
            if conv:
                conv_silu(conv)
            if old:
                add_y(old)
            if r:
                z_silu(r)
        eng.wait_ge(s_prep2, 3)
        pipelined(eng, NSEQ, 4, mamba)

        def ffn(l):
            f, ni = FF[l], FF[l]["ni"]

            def body(r):
                for i in range(ni):
                    n = r.n * ni + i
                    f["sg"].wait(eng, n)
                    if i == 0:
                        f["dn"].wait(eng, r.n, 2)
                    f["ht"].mark(tt(HTt[r.u][:, i, :], SG[i % 2][:, :], bank[i][:, SEQ:2 * SEQ], ALU.mult))

            def add(r):
                f["dn"].wait(eng, r.n)
                xs = X[:, bass.ds(r.n * CH, CH), :].rearrange("p c d -> p (c d)")
                f["add"].mark(tt(xs, xs, bank[4 + r.u][:, :], ALU.add))

            def finish(r):
                f["add"].wait(eng, r.n)
                FY[r.u].wait(eng, r.half)
                FCH.start(eng, r.n)
                for k in range(TOPK):
                    for c in range(CH):
                        xs = X[:, bass.ds(r.n * CH + c, 1), :].rearrange("p a d -> p (a d)")
                        ins = stt(xs, YF[r.u][k][:, c, :], cw[k][:, bass.ds(r.n * CH + c, 1)], xs, ALU.mult, ALU.add)
                    FCH(ins) if k == 0 else FC.mark(ins)
                FCH.end()

            def both(new, old):
                if new:
                    body(new)
                    if l == 0:
                        list_hot(0, new)
                if old:
                    add(old)
                    if l == 1:
                        finish(old)
            pipelined(eng, NSEQ if l == 1 else NSEQ - LATE, 2, both)
            return body, add
        M["add"].wait(eng, NSEQ - 1)
        late_body, late_add = ffn(0)
        for r in late_rounds():
            list_hot(0, r)
        list_end(0)

        def experts(l):
            x = EX[l]

            def h_stage(r):
                x["sg"].wait(eng, r.n)
                if l == 0:
                    x["u"].wait(eng, r.n)
                x["ht"].wait(eng, r.n, 2)
                if l == 0:
                    up, w = bank[2 + r.u][:, :], I0
                else:
                    up, w = bank[r.u][:, I1:2 * I1], I1
                parts = lambda v: v.rearrange("p (c n) -> p c n", n=P)
                x["h"].mark(tt(HE[r.u][:, 0:w // P, :], parts(SE[:, 0:w]), parts(up), ALU.mult))

            def ht_copy(r):
                x["ht"].wait(eng, r.n)
                x["dn"].wait(eng, r.n, 2)
                w = (I0 if l == 0 else I1) // P
                x["htc"].mark(eng.tensor_copy(HET[r.u][:, 0:w, :], bank[5][:, 0:w * P].rearrange("p (c t) -> p c t", c=w)))

            def body(new, r, old):
                if old:
                    ht_copy(old)
                if r:
                    h_stage(r)
            pipelined(eng, NJ, 3, body)
        experts(0)
        EX[0]["dn"].wait(eng, NJ - 1)
        for r in late_rounds():
            late_body(r)
        for r in late_rounds():
            late_add(r)

        FF[0]["add"].wait(eng, NSEQ - 1)

        def combine(r):
            ch = A["cchain"]
            ch.start(eng, r.n)
            for c in range(CH):
                xs = X[:, bass.ds(r.n * CH + c, 1), :].rearrange("p a d -> p (a d)")
                for k in range(TOPK):
                    A["y"][c * TOPK + k].wait(eng, r.n)
                    ins = stt(xs, (Y1, Y2)[k][:, c, :], cw[k][:, bass.ds(r.n * CH + c, 1)], xs, ALU.mult, ALU.add)
                    if k == 0:
                        ch(ins)
            A["comb"].mark(ins)
            A["comb"].wait(eng, r.n)
            ch.end()
            norm_stats(1, r)

        def k_copy(r, half):
            A["k"].wait(eng, r.n)
            A["on"].wait(eng, r.n, 2)
            for m in range(half * BAND // 2, (half + 1) * BAND // 2):
                ins = ts(KM[r.u][m].rearrange("p k t -> p (k t)"), bank[0][:, :], head_mask[:, m:m + 1], None, ALU.mult)
            if half == 1:
                A["kc"].mark(ins)

        def maxima(r, g, new):
            if r:
                n = r.n * PAIRS + g
                A["s"].wait(eng, n)
            if new:
                logits_stage(1, new)
            if not r:
                return
            mc = A["mchain"]
            mc.start(eng, n)
            b0 = 1 + 2 * (g % 2)
            A["exp"].wait(eng, n, 2)
            for h in range(2):
                ins = eng.tensor_reduce(MX[g % 2][:, h, :], bank[b0 + h][:, 0:3 * P].rearrange("p (b k) -> p b k", b=3),
                                        AX.X, ALU.max)
            mc(ins)
            mc(tt(MX[g % 2][:, :, 1], MX[g % 2][:, :, 1], MX[g % 2][:, :, 2], ALU.max))
            A["nm"].mark(ts(NM[g % 2], MX[g % 2][:, :, 0:2], -1.0, None, ALU.mult))
            mc.end()

        def pt_copy(r, g):
            n = r.n * PAIRS + g
            A["pt"].wait(eng, n)
            A["pv"].wait(eng, n, 2)
            A["ptc0"].mark(eng.tensor_copy(PT[g % 2][:, 0, :, :], bank[5][:, 0:3 * P].rearrange("p (b k) -> p b k", b=3)))

        def normalise(r):
            A["exp"].wait(eng, (r.n + 1) * PAIRS - 1)
            A["sr"].mark(eng.reciprocal(SR.rearrange("p c h -> p (c h)"), SM[r.u].rearrange("p c h -> p (c h)")))
            A["sr"].wait(eng, r.n)
            A["pv"].wait(eng, (r.n + 1) * PAIRS - 1)
            A["ot"].wait(eng, r.n, 1)
            A["on"].mark(tt(ON.rearrange("p c h d -> p (c h) d"), bank[7][:, :].rearrange("p (g d) -> p g d", d=DH),
                            SR.rearrange("p c h -> p (c h)").unsqueeze(2).broadcast_to([P, CH * AH, DH]), ALU.mult))

        def add_out(r):
            A["wo"].wait(eng, r.n)
            xs = X[:, bass.ds(r.n * CH, CH), :].rearrange("p c d -> p (c d)")
            A["add"].mark(tt(xs, xs, bank[0][:, :], ALU.add))
        ts(par_i[:, 1:2], par_i[:, 0:1], (BAND - 1) * DH, None, ALU.bitwise_and).then_inc(s_hmask, 1)
        eng.wait_ge(s_hmask, 1)
        eng.tensor_copy(head_mask[:, BAND:BAND + 1], par_i[:, 1:2]).then_inc(s_hmask, 1)
        eng.wait_ge(s_hmask, 2)
        for m in range(BAND):
            ts(head_mask[:, m:m + 1], head_mask[:, BAND:BAND + 1], float(m * DH), DH ** -0.5, ALU.is_equal,
               ALU.mult).then_inc(s_hmask, 1)
        eng.wait_ge(s_hmask, 2 + BAND)
        EX[0]["dn"].wait(eng, NJ - 1)
        late_route = route(1)

        def route_steps(g):
            share = (6, 6, 3, 0, 10, 10, 10, 1000)
            for _ in range(share[g]):
                if next(late_route, late_route) is late_route:
                    break
        attention(eng, turns=pt_copy, first=maxima, old_pieces={1: normalise}, done_pieces={1: add_out},
                  new_pieces={0: combine, 1: lambda r: norm_apply(1, r), 5: lambda r: k_copy(r, 0), 6: lambda r: k_copy(r, 1)},
                  tail={g: lambda g=g: route_steps(g) for g in range(PAIRS)})
        rounds(eng, NSEQ, lambda r: list_hot(1, r))
        list_end(1)
        experts(1)
        EX[1]["dn"].wait(eng, NJ - 1)
        ffn(1)

    @block.tensor
    def _(eng):
        open_events(eng, "tensor")
        eng.wait_ge(s_cmask, 1)

        def mm(o, l, r, start, stop):
            return eng.matmul(o, l, r, start=start, stop=stop)

        def norm_stage(l, r):
            ne = N[l]
            ne["xn"].wait(eng, r.n)
            ne["xT"].wait(eng, r.n, 2 if l == 0 else 1)
            b = bank[r.u if l == 0 else 0]
            if l == 1:
                A["add"].wait(eng, r.n, 3)
            for c in range(CH):
                for k in range(KD):
                    ins = eng.transpose(b[:, k * SEQ + c * P:k * SEQ + (c + 1) * P],
                                        XN[r.u][:, c, k * P:(k + 1) * P], ident[:, :])
            ne["tr"].mark(ins)

        def logits_stage(l, r):
            ne = N[l]
            ne["xT"].wait(eng, r.n)
            ne["lgc"].wait(eng, r.n, 2 if l == 0 else 1)
            w, b = (w_r0, bank[6 + r.u]) if l == 0 else (w_r1, bank[1][:, 3 * P:4 * P])
            n = E + MH if l == 0 else E
            for c in range(CH):
                for k in range(KD):
                    ins = mm(b[:, c * n:(c + 1) * n], xT[r.u][:, k, c * P:(c + 1) * P], w[:, k, :], k == 0, k == KD - 1)
            ne["lg"].mark(ins)

        eng.wait_ge(s_w_r0, 32)

        def norm_turn(new, old):
            if new:
                norm_stage(0, new)
            if old:
                logits_stage(0, old)
        pipelined(eng, NSEQ, 2, norm_turn)

        def rank(l):
            N[l]["lgc"].wait(eng, NSEQ - 1)
            eng.wait_ge(s_hot, l + 1)
            hot = hot_b[:, :, :].rearrange("p t e -> p (t e)")
            within, total = (v.rearrange("p t e -> p (t e)") for v in rank_space[l])
            mm(within, before_b[:, :], hot, True, True)
            mm(total, ones_b[:, :], hot, True, True).then_inc(s_rank, 1)
        rank(0)

        def project(r, parts):
            tok = bass.ds(r.n * SEQ, SEQ)
            for m in parts:
                b, at = (bank[1], m * SEQ) if m < 2 else (bank[2], (m - 2) * SEQ) if m < 4 else (bank[3], 0)
                for k in range(KD):
                    ins = mm(b[:, at:at + SEQ], w_in[:, k, m * P:(m + 1) * P], XT[:, k, tok], k == 0, k == KD - 1)
            return ins

        def decay_sums(r):
            M["mh"].wait(eng, r.n)
            M["xd"].wait(eng, r.n, 1)
            M["gm"].wait(eng, r.n, 1)
            M["ss"].wait(eng, r.n, 1)
            for c in range(CH):
                mm(bank[4 + c][:, :], tri_gt[:, :], MHm[:, c, :, :].rearrange("p h t -> p (h t)"), True, True)
            M["dec"].mark(mm(bank[6][0:MS, :], ones[:, :], MHm[:, 1, :, :].rearrange("p h t -> p (h t)"), True, True))

        def project_y(r):
            M["yg"].wait(eng, r.n)
            M["add"].wait(eng, r.n, 1)
            for c in range(CH):
                for k in range(KD):
                    ins = mm(bank[0][:, c * D:(c + 1) * D], YG[:, k, c * P:(c + 1) * P], w_out[:, k, :], k == 0, k == KD - 1)
            M["o"].mark(ins)

        def turn_parts(r):
            M["xs"].wait(eng, r.n)
            M["ed"].wait(eng, r.n)
            for c in range(CH):
                for k in range(KD):
                    ins = eng.transpose(bank[4][:, c * D + k * P:c * D + (k + 1) * P], XS[r.u][:, k, c * P:(c + 1) * P],
                                        ident[:, :])
            M["xtr"].mark(ins)
            eng.transpose(bank[6][:, SEQ:SEQ + MS], BT[r.u][0:MS, 0:P], ident[0:MS, 0:MS])
            for c in range(CH):
                ins = mm(bank[5][:, c * P:(c + 1) * P], BT[r.u][0:MS, c * P:(c + 1) * P], CT[r.u][0:MS, c * P:(c + 1) * P],
                         True, True)
            M["gtr"].mark(ins)

        def state(r):
            M["xw"].wait(eng, r.n)
            M["bs"].wait(eng, r.n)
            M["st"].mark(mm(bank[6][0:MS, 0:MH * MP], BS, XW.rearrange("p h d -> p (h d)"), True, True))

        def scan_y(r):
            M["wm"].wait(eng, r.n)
            M["wm1"].wait(eng, r.n)
            M["yg"].wait(eng, r.n, 1)
            M["ss"].wait(eng, r.n)
            M["ce"].wait(eng, r.n)
            for h in range(MH):
                j, q = h // 2, h % 2
                for c in range(CH):
                    o = bank[7][q * MP:(q + 1) * MP, j * SEQ + c * P:j * SEQ + (c + 1) * P]
                    ins = mm(o, XD[:, c, h, :], WM[:, c, h, :], True, c == 0)
                    if c == 1:
                        ins = mm(o, SS[0:MS, h * MP:(h + 1) * MP], CE[:, h, :], False, True)
            M["y"].mark(ins)

        def mamba(new, conv, r, old):
            if r:
                decay_sums(r)
            if old:
                project_y(old)
            if r:
                turn_parts(r)
            if new:
                M["cv"].wait(eng, new.n, 1)
                M["proj"].mark(project(new, (2, 3, 4)))
            if r:
                state(r)
                M["sz"].wait(eng, r.n, 1)
                M["z"].mark(project(r, (0, 1)))
                scan_y(r)
        N[0]["xT"].wait(eng, NSEQ - 1)
        eng.wait_ge(s_w_in, 16)
        eng.wait_ge(s_prep2, 3)
        eng.wait_ge(s_placed, 1)
        pipelined(eng, NSEQ, 4, mamba)

        def list_sum(l, r):
            ls = LS[l]
            ls["val"].wait(eng, r.n)
            first, last = (isinstance(r.n, int) and r.n == n for n in (0, NSEQ - 1))
            for q in range(TOPK * CH):
                ins = mm(bank[6][:, 0:2 * NJ], row_hot[r.u][:, q, :], tile_val[r.u][:, q, :], first and q == 0,
                         last and q == TOPK * CH - 1)
            ls["sum"].mark(ins)

        def ffn(l):
            f, ni = FF[l], FF[l]["ni"]
            gu, dn = (sh_gu, sh_dn) if l == 0 else (sh_gu1, sh_dn1)

            def body(r):
                tok = bass.ds(r.n * SEQ, SEQ)
                for i in range(ni):
                    n = r.n * ni + i
                    f["ht"].wait(eng, n, ni)
                    for half in range(2):
                        for k in range(KD):
                            at = half * ni * P + i * P
                            ins = mm(bank[i][:, half * SEQ:(half + 1) * SEQ], gu[:, k, at:at + P], XT[:, k, tok],
                                     k == 0, k == KD - 1)
                    f["gu"].mark(ins)

            def down(r):
                f["ht"].wait(eng, (r.n + 1) * ni - 1)
                f["add"].wait(eng, r.n, 2)
                for c in range(CH):
                    for i in range(ni):
                        ins = mm(bank[4 + r.u][:, c * D:(c + 1) * D], HTt[r.u][:, i, c * P:(c + 1) * P], dn[:, i, :],
                                 i == 0, i == ni - 1)
                f["dn"].mark(ins)

            def both(new, old):
                if new:
                    body(new)
                if old:
                    down(old)
                if old and l == 0:
                    list_sum(0, old)
            pipelined(eng, NSEQ if l == 1 else NSEQ - LATE, 2, both)
            return body, down
        M["add"].wait(eng, NSEQ - 1)
        eng.wait_ge(s_sh0, 32)
        late_body, late_down = ffn(0)
        for r in late_rounds():
            list_sum(0, r)

        def experts(l):
            x = EX[l]

            def xt(r):
                x["got"][r.v].wait(eng, r.i)
                x["xtc"].wait(eng, r.n, 1)
                for k in range(KD):
                    ins = eng.transpose(bank[4][:, k * P:(k + 1) * P], XG[r.v][:, k * P:(k + 1) * P], ident[:, :])
                x["xt"].mark(ins)

            regs = [eng.alloc_register(f"expert{l}_{q}") for q in range(RING + 2)]
            of_tile = {}

            def load_experts(new):
                eng.load(regs, tile_expert[0:1, bass.ds(new.n - 3, RING + 2)])
                for q in range(RING + 2):
                    of_tile[q] = nc.s_assert_within(
                        bass.RuntimeValue.of_register_unchecked(regs[q]), 0, E - 1,
                        skip_runtime_bounds_check_because="a sum of E - 1 comparisons")

            def expert_of(r, v, back):
                if isinstance(r.n, int):
                    unfuse(eng)
                    return eng.value_load(tile_expert[0:1, r.n:r.n + 1], min_val=0, max_val=E - 1)
                return of_tile[v + 3 - back]

            def gate(r, e):
                x["xtc"].wait(eng, r.n)
                x["h"].wait(eng, r.n, 2)
                for k in range(KD):
                    rhs = wgu0[:, bass.ds(e, 1), k, 0:I0] if l == 0 else wgu1[:, bass.ds(e, 1), k, :]
                    w = I0 if l == 0 else 2 * I1
                    ins = mm(bank[r.u][:, 0:w], XGT[r.u][:, k, :], rhs, k == 0, k == KD - 1)
                x["g"].mark(ins)

            def up(r, e):
                for k in range(KD):
                    ins = mm(bank[2 + r.u][:, :], XGT[r.u][:, k, :], wgu0[:, bass.ds(e, 1), k, I0:2 * I0], k == 0, k == KD - 1)
                x["u"].mark(ins)

            def turn_h(r):
                w = (I0 if l == 0 else I1) // P
                x["h"].wait(eng, r.n)
                x["htc"].wait(eng, r.n, 1)
                for c in range(w):
                    ins = eng.transpose(bank[5][:, c * P:(c + 1) * P], HE[r.u][:, c, :], ident[:, :])
                x["ht"].mark(ins)

            def down(r, e):
                w = (I0 if l == 0 else I1) // P
                x["htc"].wait(eng, r.n)
                x["yo"].wait(eng, r.n, 2)
                for c in range(w):
                    rhs = wdn0[:, bass.ds(e, 1), c, :] if l == 0 else wdn1[:, bass.ds(e, 1), :]
                    ins = mm(bank[6 + r.u][:, 0:D], HET[r.u][:, c, :], rhs, c == 0, c == w - 1)
                x["dn"].mark(ins)

            def body(new, r, old, older):
                v = new.v if new else 0
                if new and v == 0 and not isinstance(new.n, int):
                    load_experts(new)
                if r:
                    e = expert_of(r, v, 1)
                    gate(r, e)
                if old:
                    turn_h(old)
                if r and l == 0:
                    up(r, e)
                if new:
                    xt(new)
                if older:
                    down(older, expert_of(older, v, 3))
            pipelined(eng, NJ, 4, body, RING)
        eng.wait_ge(s_wgu0, 16 * E)
        eng.wait_ge(s_wdn0, 16 * E)
        FF[0]["add"].wait(eng, NSEQ - LATE - 1)
        eng.wait_ge(s_slots, 1)
        experts(0)
        EX[0]["yo"].wait(eng, NJ - 1)
        for r in late_rounds():
            late_body(r)
        for r in late_rounds():
            late_down(r)
        FF[0]["add"].wait(eng, NSEQ - 1)

        def queries(r):
            N[1]["xT"].wait(eng, r.n)
            for m in range(KD):
                for k in range(KD):
                    ins = mm(bank[0][:, m * SEQ:(m + 1) * SEQ], w_qkv[:, k, m * P:(m + 1) * P], xT[r.u][:, k, :], k == 0, k == KD - 1)
            A["q"].mark(ins)

        def values(r):
            A["qc"].wait(eng, r.n)
            for c in range(CH):
                for k in range(KD):
                    ins = mm(bank[0][:, c * D:(c + 1) * D], xT[r.u][:, k, c * P:(c + 1) * P], w_qkv[:, k, 2 * D:3 * D], k == 0, k == KD - 1)
            A["v"].mark(ins)

        def keys(r):
            A["vc"].wait(eng, r.n)
            for m in range(KD):
                for k in range(KD):
                    ins = mm(bank[0][:, m * SEQ:(m + 1) * SEQ], w_qkv[:, k, D + m * P:D + (m + 1) * P], xT[r.u][:, k, :], k == 0, k == KD - 1)
            A["k"].mark(ins)

        def scores(r, g, new):
            if r:
                n = r.n * PAIRS + g
                if g == 0:
                    A["kc"].wait(eng, r.n)
                A["exp"].wait(eng, n, 2)
            if new:
                logits_stage(1, new)
            if not r:
                return
            for h in range(2):
                hd = 2 * g + h
                j, row, m = hd * DH // P, hd // BAND * BAND * DH % P, hd % BAND
                b = bank[1 + 2 * (g % 2) + h]
                for q in range(CH):
                    o = b[:, q * P:q * P + (q + 1) * P]
                    mm(o, QT[r.u][row:row + BAND * DH, j, q * P:(q + 1) * P],
                       KM[r.u][m][row:row + BAND * DH, j, 0:(q + 1) * P], True, False)
                    ins = mm(b[:, 2 * q * P:(2 * q + 1) * P], ident_b[:, :], future_b[:, :], False, True)
            A["s"].mark(ins)

        def turn_probs(r, g):
            n = r.n * PAIRS + g
            A["exp"].wait(eng, n)
            A["ptc0"].wait(eng, n, 1)
            A["ptc1"].wait(eng, n, 1)
            for h in range(2):
                for b in range(3):
                    ins = eng.transpose(bank[5 + h][:, b * P:(b + 1) * P], PR[g % 2][:, h, b, :], ident[:, :])
            A["pt"].mark(ins)

        def weigh(r, g):
            n = r.n * PAIRS + g
            A["ptc0"].wait(eng, n)
            A["ptc1"].wait(eng, n)
            if g == 0:
                A["on"].wait(eng, r.n, 1)
            for h in range(2):
                hd = 2 * g + h
                for b, (q, t) in enumerate(((0, 0), (1, 0), (1, 1))):
                    o = bank[7][:, q * D + hd * DH:q * D + (hd + 1) * DH]
                    ins = mm(o, PT[g % 2][:, h, b, :], V[r.u][:, t, hd * DH:(hd + 1) * DH], b != 2, b != 1)
            A["pv"].mark(ins)

        def turn_out(r):
            A["on"].wait(eng, r.n)
            A["add"].wait(eng, r.n, 1)
            if isinstance(r.n, int) and r.n == NSEQ - 2:
                eng.wait_ge(s_placed, 2)
            for c in range(CH):
                for k in range(KD):
                    ins = eng.transpose(bank[0][:, k * SEQ + c * P:k * SEQ + (c + 1) * P],
                                        ON[:, c, k * AH // 2:(k + 1) * AH // 2, :].rearrange("p h d -> p (h d)"), ident[:, :])
            A["ot"].mark(ins)

        def project_out(r):
            A["otc"].wait(eng, r.n)
            for c in range(CH):
                for k in range(KD):
                    ins = mm(bank[0][:, c * D:(c + 1) * D], OT[:, k, c * P:(c + 1) * P], w_o[:, k, :], k == 0, k == KD - 1)
            A["wo"].mark(ins)
        def rank_late():
            A["add"].wait(eng, NSEQ - 3)
            rank(1)
        eng.wait_ge(s_l1a, 48)
        attention(eng, first=scores, turns=turn_probs, last=weigh, done_pieces={0: turn_out, 1: project_out},
                  new_pieces={2: lambda r: norm_stage(1, r), 3: queries, 4: values, 5: keys},
                  tail={3: rank_late})
        A["add"].wait(eng, NSEQ - 1)
        eng.wait_ge(s_placed, 2)
        pipelined(eng, NSEQ, 2, lambda new, old: old and list_sum(1, old))
        eng.wait_ge(s_l1b, 16 * (3 + 2 * E + 1))
        eng.wait_ge(s_slots, 2)
        experts(1)
        EX[1]["yo"].wait(eng, NJ - 1)
        ffn(1)


_NAMES = ["u", "w_in", "w_dt", "conv_w", "conv_b", "w_out", "A_log", "D_param", "dt_bias", "gate0", "gu0", "dn0",
          "sh_gu0", "sh_dn0", "qkv", "w_o", "gate1", "wg1", "wu1", "wd1", "sg1", "su1", "sd1"]


def kernel(L0_attn_u, L0_attn_W_in, L0_attn_conv_w, L0_attn_conv_b, L0_attn_W_out, L0_attn_A_log, L0_attn_D_param,
           L0_attn_dt_bias, L0_ffn_gate_w, L0_ffn_w_gate_up, L0_ffn_w_down, L0_ffn_shared_gate_up, L0_ffn_shared_down,
           L1_attn_w_qkv, L1_attn_w_o, L1_ffn_gate_w, L1_ffn_wg, L1_ffn_wu, L1_ffn_wd, L1_ffn_sg, L1_ffn_su, L1_ffn_sd):
    import numpy as np
    import concourse.bacc as bacc
    from concourse.bass_utils import run_bass_kernel_spmd

    ndt = 2 * D + 2 * MS
    given = dict(
        u=np.asarray(L0_attn_u).reshape(NTOK, D), w_in=np.asarray(L0_attn_W_in)[:ndt].T,
        w_dt=np.asarray(L0_attn_W_in)[ndt:].T, 
        conv_w=np.asarray(L0_attn_conv_w).reshape(3, P, TAPS).transpose(1, 0, 2), conv_b=np.asarray(L0_attn_conv_b).reshape(3, P).T,
        w_out=np.asarray(L0_attn_W_out).T, A_log=L0_attn_A_log, D_param=np.asarray(L0_attn_D_param).reshape(KD, 2).T, dt_bias=L0_attn_dt_bias,
        gate0=L0_ffn_gate_w, gu0=L0_ffn_w_gate_up, dn0=L0_ffn_w_down, sh_gu0=L0_ffn_shared_gate_up,
        sh_dn0=L0_ffn_shared_down, qkv=L1_attn_w_qkv, w_o=L1_attn_w_o, gate1=np.asarray(L1_ffn_gate_w).T,
        wg1=L1_ffn_wg, wu1=L1_ffn_wu, wd1=L1_ffn_wd, sg1=L1_ffn_sg, su1=L1_ffn_su, sd1=L1_ffn_sd)
    nc = bacc.Bacc("TRN2", target_bir_lowering=False, num_devices=1)
    arrays, aps = {}, {}
    for name in _NAMES:
        v = np.ascontiguousarray(given[name])
        arrays[f"in_{name}"] = v
        aps[name] = nc.dram_tensor(f"in_{name}", v.shape, mybir.dt.from_np(v.dtype), kind="ExternalInput").ap()
    out = nc.dram_tensor("out", (NTOK, D), F32, kind="ExternalOutput").ap()
    build(nc, aps, out)
    r = run_bass_kernel_spmd(nc, [arrays], core_ids=[0])
    return r.results[0]["out"].reshape(NSEQ, SEQ, D)
```
